# Optimizing a Trainium2 kernel written in Bass

```python
import numpy as np
import jax
import jax.numpy as jnp

def _softmax(x, axis=-1):
    return jax.nn.softmax(x, axis=axis)

def _gelu(x):
    return jax.nn.gelu(x, approximate=True)

def _silu(x):
    return jax.nn.silu(x)

def _sigmoid(x):
    return jax.nn.sigmoid(x)

def _layernorm(x, axis=-1, eps=1e-05):
    m = jnp.mean(x, axis=axis, keepdims=True)
    v = jnp.var(x, axis=axis, keepdims=True)
    return (x - m) / jnp.sqrt(v + eps)

def _scatter_add(tgt, idx, src, axis=0):
    return tgt.at[idx].add(src)

def _segment_sum(src, seg, n):
    return jax.ops.segment_sum(src, seg, n)
kernel_name = 'mk_perceiver_d1_seqx_r4_58ed81'

def setup_inputs(seed: int=0):
    np.random.seed(seed)
    _w = jnp.asarray

    def _rec_inputs():
        import jax
        import jax.numpy as jnp
        _rk = jax.random.key(seed)
        x = -0.000125 + 0.9999 * jax.random.normal(jax.random.fold_in(_rk, 1), (16, 64, 256), jnp.float32)
        _lenS = 64 - jax.random.randint(jax.random.fold_in(_rk, 7), (16,), 0, max(1, 64 // 4) + 1, jnp.int32)
        _lenS2 = 1601 - jax.random.randint(jax.random.fold_in(_rk, 8), (16,), 0, max(1, 1601 // 4) + 1, jnp.int32)
        _ctx_1024P = jax.random.normal(jax.random.fold_in(_rk, 11), (16, 16, 256), jnp.float32)
        _ctx_1024c = jax.random.dirichlet(jax.random.fold_in(_rk, 511), 0.3 * jnp.ones((16,), jnp.float32), (16, 1601))
        _ctx_1024t = jnp.einsum('bsk,bkd->bsd', _ctx_1024c, _ctx_1024P)
        _ctx_1024t = _ctx_1024t * jax.lax.rsqrt(jnp.mean(jnp.square(_ctx_1024t)) + 1e-12) * 0.953939
        ctx_1024 = -4.4511e-05 + 0.999885 * (_ctx_1024t + 0.3 * jax.random.normal(jax.random.fold_in(_rk, 611), (16, 1601, 256), jnp.float32))
        return (x, ctx_1024)
    x, ctx_1024 = _rec_inputs()

    def _L0_xattn_setup():
        import jax, jax.numpy as jnp
        import numpy as np
        H = 16
        D = 64
        SCALE = D ** (-0.5)
        TEXT = 77
        IMG = 16
        AUD = 32
        MAXREL = 16
        B, NQ, QD = (32, 256, 256)
        INNER = H * D

        def _heads(t):
            return t.reshape(t.shape[0], t.shape[1], H, D)
        key = jax.random.key(seed)
        ks = jax.random.split(key, 14)
        w = lambda k, s: jax.random.normal(k, s, jnp.float32) * 0.02
        return {'x': jax.random.normal(ks[0], (B, NQ, QD), jnp.float32), 'context': jax.random.normal(ks[1], (B, TEXT + IMG + AUD, QD), jnp.float32), 'Wq': w(ks[2], (QD, INNER)), 'Wk': w(ks[3], (QD, INNER)), 'Wv': w(ks[4], (QD, INNER)), 'Wk_ip': w(ks[5], (QD, INNER)), 'Wv_ip': w(ks[6], (QD, INNER)), 'Wk_ap': w(ks[7], (QD, INNER)), 'Wv_ap': w(ks[8], (QD, INNER)), 'Wo': w(ks[9], (INNER, QD)), 'bo': jnp.zeros((QD,), jnp.float32), 'rel_k': w(ks[10], (2 * MAXREL + 1, D)), 'rel_v': w(ks[11], (2 * MAXREL + 1, D)), 'alpha': jnp.zeros((), jnp.float32), 'beta': jnp.zeros((), jnp.float32)}
    _L0_xattn_all = _L0_xattn_setup()
    _L0_xattn_in = {k: v for k, v in _L0_xattn_all.items() if k in ('Wq', 'Wk', 'Wv', 'Wk_ip', 'Wv_ip', 'Wk_ap', 'Wv_ap', 'Wo', 'bo', 'rel_k', 'rel_v', 'alpha', 'beta')}
    del _L0_xattn_all

    def _L0_attn_setup():
        import jax, jax.numpy as jnp
        import numpy as np
        B, S, D, NH = (4, 512, 256, 16)
        HD = D // NH
        key = jax.random.key(seed)
        ks = jax.random.split(key, 5)
        scale = 0.02
        return {'x': jax.random.normal(ks[0], (B, S, D), dtype=jnp.float32), 'w_attn': jax.random.normal(ks[1], (D, 3 * D), dtype=jnp.float32) * scale, 'b_attn': jax.random.normal(ks[2], (3 * D,), dtype=jnp.float32) * scale, 'w_proj': jax.random.normal(ks[3], (D, D), dtype=jnp.float32) * scale, 'b_proj': jax.random.normal(ks[4], (D,), dtype=jnp.float32) * scale}
    _L0_attn_all = _L0_attn_setup()
    _L0_attn_in = {k: v for k, v in _L0_attn_all.items() if k in ('w_attn', 'b_attn', 'w_proj', 'b_proj')}
    del _L0_attn_all

    def _L0_ffn_setup():
        import jax, jax.numpy as jnp
        import numpy as np
        D = 256
        H = 256
        E = 8
        K = 2
        I = 2 * 256
        ROUTE_SCALE = 1.0
        key = jax.random.key(seed)
        ks = jax.random.split(key, 12)
        s = lambda *sh: 1.0 / np.sqrt(sh[-1])
        return {'x': jax.random.normal(ks[0], (1, 512, D), jnp.float32), 'gate_w': jax.random.normal(ks[1], (E, D), jnp.float32) * s(E, D), 'w1': jax.random.normal(ks[2], (E, H, D), jnp.float32) * s(H, D), 'b1': jax.random.normal(ks[3], (E, H), jnp.float32) * 0.01, 'w2': jax.random.normal(ks[4], (E, D, H), jnp.float32) * s(D, H), 'b2': jax.random.normal(ks[5], (E, D), jnp.float32) * 0.01, 'w3': jax.random.normal(ks[6], (E, H, D), jnp.float32) * s(H, D), 'b3': jax.random.normal(ks[7], (E, H), jnp.float32) * 0.01, 'sw1': jax.random.normal(ks[8], (I, D), jnp.float32) * s(I, D), 'sw2': jax.random.normal(ks[9], (I, D), jnp.float32) * s(I, D), 'sw3': jax.random.normal(ks[10], (D, I), jnp.float32) * s(D, I)}
    _L0_ffn_all = _L0_ffn_setup()
    _L0_ffn_in = {k: v for k, v in _L0_ffn_all.items() if k in ('gate_w', 'w1', 'b1', 'w2', 'b2', 'w3', 'b3', 'sw1', 'sw2', 'sw3')}
    del _L0_ffn_all
    return {'x': x, 'ctx_1024': ctx_1024, 'L0_xattn_Wq': _L0_xattn_in['Wq'], 'L0_xattn_Wk': _L0_xattn_in['Wk'], 'L0_xattn_Wv': _L0_xattn_in['Wv'], 'L0_xattn_Wk_ip': _L0_xattn_in['Wk_ip'], 'L0_xattn_Wv_ip': _L0_xattn_in['Wv_ip'], 'L0_xattn_Wk_ap': _L0_xattn_in['Wk_ap'], 'L0_xattn_Wv_ap': _L0_xattn_in['Wv_ap'], 'L0_xattn_Wo': _L0_xattn_in['Wo'], 'L0_xattn_bo': _L0_xattn_in['bo'], 'L0_xattn_rel_k': _L0_xattn_in['rel_k'], 'L0_xattn_rel_v': _L0_xattn_in['rel_v'], 'L0_xattn_alpha': _L0_xattn_in['alpha'], 'L0_xattn_beta': _L0_xattn_in['beta'], 'L0_attn_w_attn': _L0_attn_in['w_attn'], 'L0_attn_b_attn': _L0_attn_in['b_attn'], 'L0_attn_w_proj': _L0_attn_in['w_proj'], 'L0_attn_b_proj': _L0_attn_in['b_proj'], 'L0_ffn_gate_w': _L0_ffn_in['gate_w'], 'L0_ffn_w1': _L0_ffn_in['w1'], 'L0_ffn_b1': _L0_ffn_in['b1'], 'L0_ffn_w2': _L0_ffn_in['w2'], 'L0_ffn_b2': _L0_ffn_in['b2'], 'L0_ffn_w3': _L0_ffn_in['w3'], 'L0_ffn_b3': _L0_ffn_in['b3'], 'L0_ffn_sw1': _L0_ffn_in['sw1'], 'L0_ffn_sw2': _L0_ffn_in['sw2'], 'L0_ffn_sw3': _L0_ffn_in['sw3']}

def reference(x, ctx_1024, L0_xattn_Wq, L0_xattn_Wk, L0_xattn_Wv, L0_xattn_Wk_ip, L0_xattn_Wv_ip, L0_xattn_Wk_ap, L0_xattn_Wv_ap, L0_xattn_Wo, L0_xattn_bo, L0_xattn_rel_k, L0_xattn_rel_v, L0_xattn_alpha, L0_xattn_beta, L0_attn_w_attn, L0_attn_b_attn, L0_attn_w_proj, L0_attn_b_proj, L0_ffn_gate_w, L0_ffn_w1, L0_ffn_b1, L0_ffn_w2, L0_ffn_b2, L0_ffn_w3, L0_ffn_b3, L0_ffn_sw1, L0_ffn_sw2, L0_ffn_sw3):
    import jax
    import jax.numpy as jnp

    def _L0_xattn_ref(x, context, Wq, Wk, Wv, Wk_ip, Wv_ip, Wk_ap, Wv_ap, Wo, bo, rel_k, rel_v, alpha, beta):
        import jax, jax.numpy as jnp
        import numpy as np
        H = 16
        D = 64
        SCALE = D ** (-0.5)
        TEXT = 77
        IMG = 16
        AUD = 32
        MAXREL = 16
        B, NQ, QD = (32, 256, 256)
        INNER = H * D

        def _heads(t):
            return t.reshape(t.shape[0], t.shape[1], H, D)
        b, nq, _ = x.shape
        q = _heads(x @ Wq)
        ctx_t = context[:, :TEXT]
        ctx_i = context[:, TEXT:TEXT + IMG]
        ctx_a = context[:, TEXT + IMG:]
        k = _heads(ctx_t @ Wk)
        v = _heads(ctx_t @ Wv)
        sim = jnp.einsum('bihd,bjhd->bhij', q, k) * SCALE
        dist = jnp.clip(jnp.arange(TEXT)[None, :] - jnp.arange(nq)[:, None], -MAXREL, MAXREL) + MAXREL
        k2 = rel_k[dist]
        sim = sim + jnp.einsum('bihd,ijd->bhij', q, k2) * SCALE
        attn = jax.nn.softmax(sim, axis=-1)
        out = jnp.einsum('bhij,bjhd->bihd', attn, v)
        out = out + jnp.einsum('bhij,ijd->bihd', attn, rel_v[dist])

        def stream(W_k, W_v, ctx):
            kh = _heads(ctx @ W_k)
            vh = _heads(ctx @ W_v)
            a = jax.nn.softmax(jnp.einsum('bihd,bjhd->bhij', q, kh) * SCALE, axis=-1)
            return jnp.einsum('bhij,bjhd->bihd', a, vh)
        out = out + stream(Wk_ip, Wv_ip, ctx_i) * (jnp.tanh(alpha) + 1.0)
        out = out + stream(Wk_ap, Wv_ap, ctx_a) * (jnp.tanh(beta) + 1.0)
        out = out.reshape(b, nq, INNER)
        return out @ Wo + bo

    def _L0_attn_ref(x, w_attn, b_attn, w_proj, b_proj):
        import jax, jax.numpy as jnp
        import numpy as np
        B, S, D, NH = (4, 512, 256, 16)
        HD = D // NH
        batch, seq_len, d_model = x.shape
        hd = d_model // NH
        qkv = x @ w_attn + b_attn
        q, k, v = jnp.split(qkv, 3, axis=2)
        q = q.reshape(batch, seq_len, NH, hd).transpose(0, 2, 1, 3)
        k = k.reshape(batch, seq_len, NH, hd).transpose(0, 2, 1, 3)
        v = v.reshape(batch, seq_len, NH, hd).transpose(0, 2, 1, 3)
        att = jnp.einsum('bhqd,bhkd->bhqk', q, k) * (1.0 / np.sqrt(hd).astype(np.float32))
        att = jax.nn.softmax(att, axis=-1)
        y = jnp.einsum('bhqk,bhkd->bhqd', att, v)
        y = y.transpose(0, 2, 1, 3).reshape(batch, seq_len, d_model)
        return y @ w_proj + b_proj

    def _L0_ffn_ref(x, gate_w, w1, b1, w2, b2, w3, b3, sw1, sw2, sw3):
        import jax, jax.numpy as jnp
        import numpy as np
        D = 256
        H = 256
        E = 8
        K = 2
        I = 2 * 256
        ROUTE_SCALE = 1.0
        B, S, _ = x.shape
        xt = x.reshape(-1, D)
        logits = xt @ gate_w.T
        scores = jax.nn.softmax(logits.astype(jnp.float32), axis=-1)
        top_vals, idx = jax.lax.top_k(scores, K)
        weights = jnp.take_along_axis(scores, idx, axis=1).astype(x.dtype) * ROUTE_SCALE
        xs = xt[:, None, :] * weights[:, :, None]
        y = jnp.zeros_like(xt)
        for e in range(E):
            mask = (idx == e).astype(x.dtype)
            h = jax.nn.silu(jnp.einsum('tkd,hd->tkh', xs, w1[e]) + b1[e])
            x2 = jnp.einsum('tkh,dh->tkd', h, w2[e]) + b2[e]
            x3 = jnp.einsum('tkd,hd->tkh', xs, w3[e]) + b3[e]
            y = y + jnp.sum(x2 * x3 * mask[:, :, None], axis=1)
        z = jax.nn.silu(xt @ sw1.T) * (xt @ sw2.T) @ sw3.T
        return (y + z).reshape(B, S, D)
    x = x + _L0_xattn_ref(_layernorm(x, axis=-1), ctx_1024, L0_xattn_Wq, L0_xattn_Wk, L0_xattn_Wv, L0_xattn_Wk_ip, L0_xattn_Wv_ip, L0_xattn_Wk_ap, L0_xattn_Wv_ap, L0_xattn_Wo, L0_xattn_bo, L0_xattn_rel_k, L0_xattn_rel_v, L0_xattn_alpha, L0_xattn_beta)
    x = x + _L0_attn_ref(_layernorm(x, axis=-1), L0_attn_w_attn, L0_attn_b_attn, L0_attn_w_proj, L0_attn_b_proj)
    x = x + _L0_ffn_ref(_layernorm(x, axis=-1), L0_ffn_gate_w, L0_ffn_w1, L0_ffn_b1, L0_ffn_w2, L0_ffn_b2, L0_ffn_w3, L0_ffn_b3, L0_ffn_sw1, L0_ffn_sw2, L0_ffn_sw3)
    return x

_drawn_inputs = setup_inputs


def setup_inputs(seed=0):
    import zlib

    import numpy as np

    out = dict(_drawn_inputs(seed))
    spreads = {'L0_xattn_bo': (0.0, 0.1)}
    factors = {'L0_xattn_Wq': 6.545,
     'L0_xattn_Wk': 8.0,
     'L0_xattn_Wk_ip': 8.0,
     'L0_xattn_Wk_ap': 8.0,
     'L0_xattn_rel_k': 24.985,
     'L0_xattn_rel_v': 6.565,
     'L0_attn_b_attn': 6.847,
     'L0_ffn_b1': 29.093,
     'L0_ffn_b2': 8.0,
     'L0_ffn_b3': 26.069,
     'L0_attn_b_proj': 2.721}
    for name, (base, spread) in spreads.items():
        noise = np.random.default_rng([zlib.crc32(name.encode()), seed]).standard_normal(out[name].shape)
        drawn = base * np.exp(spread * noise) if base else spread * noise
        out[name] = jnp.asarray(drawn.astype(out[name].dtype))
    for name, factor in factors.items():
        out[name] = (out[name] * factor).astype(out[name].dtype)
    return out
```

```python
from contextlib import ExitStack

import numpy as np
import concourse.bass as bass
from concourse import mybir
from concourse.alu_op_type import AluOpType as ALU

F32 = mybir.dt.float32
F16 = mybir.dt.float16
ACT = mybir.ActivationFunctionType
X = mybir.AxisListType.X

P = 128
B, NQ, D = 16, 64, 256
T = B * NQ
TT = T // P
KD = D // P
H, HD = 16, 64
INNER = H * HD
PAIRS = H // 2
TXT, IMG, CTX = 77, 16, 1601
TI = TXT + IMG
AUD = CTX - TI
NCH = -(-AUD // P)
TAIL = AUD - (NCH - 1) * P
SB = 3
MAXREL = 16
NREL = 2 * MAXREL + 1
EXT = NQ + TXT - 1
REL0 = NQ - 1 - MAXREL
SCALE = HD ** -0.5
SA, SW, SP = 16.0, 256.0, 4096.0
EPS = 1e-5


def mm3(pe, out, lhs, rhs, first=True, last=True):
    (lh, ll), (rh, rl) = lhs, rhs
    pe.matmul(out, lh, rh, start=first, stop=False)
    pe.matmul(out, lh, rl, start=False, stop=False)
    return pe.matmul(out, ll, rh, start=False, stop=last)


def split_hi(act, hi, src, scale):
    return act.activation(hi, src, ACT.Copy, scale=scale)


def split_lo(dve, lo, src, hi, scale):
    return dve.scalar_tensor_tensor(out=lo, in0=src, scalar=scale, in1=hi, op0=ALU.mult, op1=ALU.subtract)


class Mem:

    def __init__(self, nc, ctx):
        self.nc, self.ctx, self.sems = nc, ctx, []

    def sb(self, name, shape, dt=F32):
        return self.ctx.enter_context(self.nc.sbuf_tensor(name, shape, dt))

    def ps(self, name, shape, dt=F32):
        return self.ctx.enter_context(self.nc.psum_tensor(name, shape, dt))

    def sem(self, name):
        handle = self.ctx.enter_context(self.nc.semaphore(name))
        self.sems.append(handle)
        return handle


def make_identity(pool, ident, made):
    pool.memset(ident, 0.0).then_inc(made, 1)
    pool.wait_ge(made, 1)
    pool.affine_select(out=ident, in_=ident, compare_op=ALU.not_equal, fill=1.0, base=0,
                       pattern=[[-1, ident.shape[1]]], channel_multiplier=1).then_inc(made, 1)


class Norm:

    def __init__(self, m, name):
        self.stats = m.sb(name + "_stats", [P, TT, 6])
        self.mean_var = m.sb(name + "_mean_var", [P, TT, 2])
        self.rstd = m.sb(name + "_rstd", [P, TT])
        self.power = m.sb(name + "_power", [P, TT])
        self.stats_ready = m.sem(name + "_stats_ready")
        self.moments_ready = m.sem(name + "_moments_ready")
        self.rstd_ready = m.sem(name + "_rstd_ready")
        self.xn_ready = m.sem(name + "_xn_ready")

    def pool(self, pool):
        pool.memset(self.power[:, :], -0.5).then_inc(self.rstd_ready, 1)
        pool.wait_ge(self.moments_ready, TT)
        pool.tensor_scalar(self.rstd[:, :], self.mean_var[:, :, 1], EPS, None, ALU.add).then_inc(self.rstd_ready, 1)
        pool.wait_ge(self.rstd_ready, 2)
        pool.tensor_tensor(self.rstd[:, :], self.rstd[:, :], self.power[:, :], ALU.pow).then_inc(self.rstd_ready, 1)

    def vector(self, dve, xn, x, wait_tile=None):
        for t in range(TT):
            if wait_tile:
                wait_tile(t)
            dve.bn_stats(self.stats[:, t, :], x[:, t, :]).then_inc(self.stats_ready, 1)
        for t in range(TT):
            dve.wait_ge(self.stats_ready, t + 1)
            dve.bn_aggr(self.mean_var[:, t, :], self.stats[:, t, :]).then_inc(self.moments_ready, 1)
        dve.wait_ge(self.rstd_ready, 3)
        for t in range(TT):
            dve.tensor_scalar(xn[:, t, :], x[:, t, :], self.mean_var[:, t, 0:1], self.rstd[:, t:t + 1],
                              ALU.subtract, ALU.mult).then_inc(self.xn_ready, 1)


def weight_rows(w):
    return w.rearrange("(k p) n -> p k n", p=P)


def project(nc, m, a, scr, qT, ident):
    x = m.sb("x_a", [P, TT, D])
    xn = m.sb("xn_a", [P, TT, D])
    xnT = [m.sb(f"xnT_a{s}", [P, KD, T], F16) for s in "hl"]
    ctx_ti = m.sb("ctx_ti", [TI, B, D])
    txtT = [m.sb(f"txtT_{s}", [P, KD, B, TXT], F16) for s in "hl"]
    imgT = [m.sb(f"imgT_{s}", [P, KD, B, IMG], F16) for s in "hl"]
    staged = [m.sb(f"staged{i}", [P, KD, INNER]) for i in range(2)]
    names = ["Wq", "Wk", "Wk_ip", "Wv", "Wv_ip"]
    W = {n: [m.sb(f"{n}_{s}", [P, KD, INNER], F16) for s in "hl"] for n in names}
    KT = m.sb("KT", [P, B, 2, PAIRS, TI], F16)
    v_out = [m.sb(f"v_out{i}", [P, 2, INNER], F16) for i in range(2)]
    bank = m.ps("bank_a", [P, 8, 512])

    norm = Norm(m, "norm_a")
    ident_made = m.sem("ident_a_made")
    x_loaded = m.sem("x_a_loaded")
    ctx_loaded = m.sem("ctx_ti_loaded")
    w_loaded = {n: m.sem(f"{n}_loaded") for n in names}
    w_hi = m.sem("w_hi")
    w_lo = m.sem("w_lo")
    job_ready = m.sem("job_a_ready")
    job_hi = m.sem("job_a_hi")
    job_lo = m.sem("job_a_lo")
    v_stored = [m.sem(f"v_stored{i}") for i in range(2)]
    kt_stored = m.sem("kt_stored")

    XN, CT, Q, K = 0, TT // 2, TT // 2 + B // 2, TT // 2 + B // 2 + 2 * PAIRS
    G = 4
    NK = B // G + 1
    V = K + NK * PAIRS
    v_chunks = [("Wv", txtT, c * P, min(P, B * TXT - c * P)) for c in range(-(-B * TXT // P))]
    v_chunks += [("Wv_ip", imgT, c * P, P) for c in range(B * IMG // P)]

    block = m.ctx.enter_context(nc.Block())

    @block.sync
    def _(sp):
        sp.dma_start(x[:, :, :], a["x"].rearrange("(t b) q d -> (b q) t d", b=2)).then_inc(x_loaded, 16)
        sp.dma_start(ctx_ti[:, :, :], a["ctx"][:, 0:TI, :].rearrange("b j d -> j b d")).then_inc(ctx_loaded, 16)
        for n, name in enumerate(names):
            if n >= 2:
                sp.wait_ge(w_lo, n - 1)
            sp.dma_start(staged[n % 2][:, :, :], weight_rows(a[name])).then_inc(w_loaded[name], 16)
        sp.wait_ge(job_hi, V)
        sp.wait_ge(job_lo, V)
        sp.dma_start(scr["kt"].rearrange("b p f -> p b f"), KT[:, :, :, :, :].rearrange("p b s m j -> p b (s m j)")).then_inc(kt_stored, 16)
        row = 0
        for c, (_, _, _, n) in enumerate(v_chunks):
            sp.wait_ge(job_lo, V + 2 * c + 2)
            sp.dma_start(scr["v"][row:row + n, :], v_out[c % 2][0:n, :, :].rearrange("p s n -> p (s n)")).then_inc(v_stored[c % 2], 16)
            row += n
        for i in range(2):
            sp.wait_ge(v_stored[i], 16 * (len(v_chunks) // 2))
        sp.wait_ge(kt_stored, 16)

    @block.gpsimd
    def _(pool):
        make_identity(pool, ident[:, :], ident_made)
        norm.pool(pool)

    def xn_dst(s, g):
        return xnT[s][:, :, g * 2 * P:(g + 1) * 2 * P]

    def ctx_job(g):
        src = bank[:, (CT + g) % 8, 0:4 * TI].rearrange("p (k b j) -> p k b j", k=KD, b=2)
        return src[:, :, :, 0:TXT], src[:, :, :, TXT:TI]

    @block.tensor
    def _(pe):
        pe.wait_ge(ident_made, 2)
        for g in range(TT // 2):
            pe.wait_ge(norm.xn_ready, 2 * g + 2)
            for k in range(KD):
                for t in range(2):
                    at = (2 * k + t) * P
                    mm = pe.transpose(bank[:, XN + g, at:at + P], xn[:, 2 * g + t, k * P:(k + 1) * P], ident[:, :])
            mm.then_inc(job_ready, 1)
        pe.wait_ge(ctx_loaded, 16)
        for g in range(B // 2):
            if CT + g >= 8:
                pe.wait_ge(job_lo, CT + g - 7)
            for k in range(KD):
                for b in range(2):
                    at = (2 * k + b) * TI
                    mm = pe.transpose(bank[:, (CT + g) % 8, at:at + TI], ctx_ti[:, 2 * g + b, k * P:(k + 1) * P],
                                      ident[0:TI, 0:TI])
            mm.then_inc(job_ready, 1)
        pe.wait_ge(w_lo, 1)
        pe.wait_ge(w_hi, 1)
        with pe.Fori(0, PAIRS // 4) as i:
            for u in range(4):
                for n in range(2):
                    job = Q + 2 * u + n
                    pe.wait_ge(job_lo, i * 8 + (job - 7))
                    for k in range(KD):
                        lhs = [w[:, k, bass.ds(i * (4 * P) + u * P, P)] for w in W["Wq"]]
                        rhs = [x_[:, k, n * 512:(n + 1) * 512] for x_ in xnT]
                        mm = mm3(pe, bank[:, job % 8, :], lhs, rhs, k == 0, k == KD - 1)
                    mm.then_inc(job_ready, 1)
        pe.wait_ge(w_lo, 3)
        pe.wait_ge(w_hi, 3)
        with pe.Fori(0, PAIRS) as i:
            for n in range(NK):
                pe.wait_ge(job_lo, i * NK + (K + n - NK + 1))
                name, src = ("Wk", txtT) if n < NK - 1 else ("Wk_ip", imgT)
                for k in range(KD):
                    lhs = [w[:, k, bass.ds(i * P, P)] for w in W[name]]
                    rhs = [(s[:, k, n * G:(n + 1) * G, :] if n < NK - 1 else s[:, k, :, :]).rearrange("p b j -> p (b j)") for s in src]
                    mm = mm3(pe, bank[:, (n + 4) % 8, 0:rhs[0].shape[1]], lhs, rhs, k == 0, k == KD - 1)
                mm.then_inc(job_ready, 1)
        pe.wait_ge(w_lo, 5)
        pe.wait_ge(w_hi, 5)
        for c, (name, src, at, rows) in enumerate(v_chunks):
            for n in range(2):
                job = V + 2 * c + n
                pe.wait_ge(job_lo, job - 4)
                for k in range(KD):
                    lhs = [s[:, k, :, :].rearrange("p b j -> p (b j)")[:, at:at + rows] for s in src]
                    rhs = [w[:, k, n * 512:(n + 1) * 512] for w in W[name]]
                    mm = mm3(pe, bank[0:rows, (4 + (job - V) % 5) % 8, :], lhs, rhs, k == 0, k == KD - 1)
                mm.then_inc(job_ready, 1)

    @block.scalar
    def _(act):
        def hi(job, dst, src, scale):
            act.wait_ge(job_ready, job)
            split_hi(act, dst, src, scale).then_inc(job_hi, 1)

        def weight(n):
            act.wait_ge(w_loaded[names[n]], 16)
            split_hi(act, W[names[n]][0][:, :, :], staged[n % 2][:, :, :], SW).then_inc(w_hi, 1)

        weight(0)
        weight(1)
        for g in range(TT // 2):
            hi(XN + g + 1, xn_dst(0, g), bank[:, XN + g, :].rearrange("p (k t) -> p k t", k=KD), SA)
        for g in range(B // 2):
            act.wait_ge(job_ready, CT + g + 1)
            txt, img = ctx_job(g)
            split_hi(act, txtT[0][:, :, 2 * g:2 * g + 2, :], txt, SA)
            split_hi(act, imgT[0][:, :, 2 * g:2 * g + 2, :], img, SA).then_inc(job_hi, 1)
        weight(2)
        weight(3)
        with act.Fori(0, PAIRS // 4) as i:
            for u in range(4):
                for n in range(2):
                    job = Q + 2 * u + n
                    hi(i * 8 + (job + 1), qT[0][:, bass.ds(i * 4 + u, 1), n * 512:(n + 1) * 512], bank[:, job % 8, :].unsqueeze(1),
                       SCALE * SA / (SA * SW))
        weight(4)
        with act.Fori(0, PAIRS) as i:
            for n in range(NK):
                src, dst = (bank[:, (n + 4) % 8, 0:G * TXT], KT[:, n * G:(n + 1) * G, 0, :, 0:TXT]) if n < NK - 1 else \
                    (bank[:, (n + 4) % 8, 0:B * IMG], KT[:, :, 0, :, TXT:TI])
                hi(i * NK + (K + n + 1), dst[:, :, bass.ds(i, 1), :].squeeze(2), src.rearrange("p (b j) -> p b j", j=dst.shape[3]),
                   SA / (SA * SW))
        for c, (_, _, _, rows) in enumerate(v_chunks):
            if c >= 2:
                act.wait_ge(v_stored[c % 2], 16 * (c // 2))
            for n in range(2):
                job = V + 2 * c + n
                hi(job + 1, v_out[c % 2][0:rows, 0, n * 512:(n + 1) * 512], bank[0:rows, (4 + (job - V) % 5) % 8, :], SA / (SA * SW))

    @block.vector
    def _(dve):
        def lo(job, dst, src, hi_, scale):
            dve.wait_ge(job_hi, job)
            split_lo(dve, dst, src, hi_, scale).then_inc(job_lo, 1)

        def weight(n):
            dve.wait_ge(w_hi, n + 1)
            split_lo(dve, W[names[n]][1][:, :, :], staged[n % 2][:, :, :], W[names[n]][0][:, :, :], SW).then_inc(w_lo, 1)

        norm.vector(dve, xn, x, lambda t: dve.wait_ge(x_loaded, 16))
        weight(0)
        weight(1)
        for g in range(TT // 2):
            lo(XN + g + 1, xn_dst(1, g), bank[:, XN + g, :].rearrange("p (k t) -> p k t", k=KD), xn_dst(0, g), SA)
        for g in range(B // 2):
            dve.wait_ge(job_hi, CT + g + 1)
            for k in range(KD):
                for part, (src, dst) in enumerate(zip(ctx_job(g), (txtT, imgT))):
                    io = [s[:, k, 2 * g:2 * g + 2, :] for s in dst]
                    ins = split_lo(dve, io[1], src[:, k, :, :], io[0], SA)
            ins.then_inc(job_lo, 1)
        weight(2)
        weight(3)
        with dve.Fori(0, PAIRS // 4) as i:
            for u in range(4):
                for n in range(2):
                    job = Q + 2 * u + n
                    dst = [q[:, bass.ds(i * 4 + u, 1), n * 512:(n + 1) * 512] for q in qT]
                    lo(i * 8 + (job + 1), dst[1], bank[:, job % 8, :].unsqueeze(1), dst[0], SCALE * SA / (SA * SW))
        weight(4)
        with dve.Fori(0, PAIRS) as i:
            for n in range(NK):
                if n < NK - 1:
                    src, dst = bank[:, (n + 4) % 8, 0:G * TXT], [KT[:, n * G:(n + 1) * G, s, :, 0:TXT] for s in range(2)]
                else:
                    src, dst = bank[:, (n + 4) % 8, 0:B * IMG], [KT[:, :, s, :, TXT:TI] for s in range(2)]
                dst = [d[:, :, bass.ds(i, 1), :].squeeze(2) for d in dst]
                lo(i * NK + (K + n + 1), dst[1], src.rearrange("p (b j) -> p b j", j=dst[0].shape[2]), dst[0], SA / (SA * SW))
        for c, (_, _, _, rows) in enumerate(v_chunks):
            if c >= 2:
                dve.wait_ge(v_stored[c % 2], 16 * (c // 2))
            for n in range(2):
                job = V + 2 * c + n
                io = [v_out[c % 2][0:rows, s, n * 512:(n + 1) * 512] for s in range(2)]
                lo(job + 1, io[1], bank[0:rows, (4 + (job - V) % 5) % 8, :], io[0], SA / (SA * SW))


def extended_rows(w):
    return [(0, REL0, w[0:1, :]), (REL0, NREL, w[:, :]), (REL0 + NREL, EXT - REL0 - NREL, w[NREL - 1:NREL, :])]


def relative_scores(nc, m, a, scr, qT, ident):
    ext = [m.sb("relk_rows0", [P, 2, HD]), m.sb("relk_rows1", [EXT - P, 2, HD])]
    table = [m.sb(f"relk_table_{s}", [P, 2, EXT], F16) for s in "hl"]
    R = m.sb("R", [TXT, B * PAIRS, 2, NQ])
    tbank = m.ps("relk_bank", [P, 512])
    bank = m.ps("R_bank", [P, 4, 512])
    relv_rows = [m.sb("relv_rows0", [P, HD]), m.sb("relv_rows1", [EXT - P, HD])]

    rows_loaded = m.sem("relk_rows_loaded")
    relv_loaded = m.sem("relv_rows_loaded")
    relv_stored = m.sem("relv_ext_stored")
    zeroed = m.sem("relk_zeroed")
    turned = m.sem("relk_turned")
    table_hi = m.sem("relk_table_hi")
    table_lo = m.sem("relk_table_lo")
    even_ready, odd_ready = m.sem("R_even_ready"), m.sem("R_odd_ready")
    even_out, odd_out = m.sem("R_even_out"), m.sem("R_odd_out")
    r_stored = m.sem("R_stored")
    U = 4
    loads = [0]

    block = m.ctx.enter_context(nc.Block())

    @block.sync
    def _(sp):
        for first, n, src in extended_rows(a["rel_k"]):
            for tile, lo_, hi_ in ((ext[0], 0, P), (ext[1], P, EXT)):
                s, e = max(first, lo_), min(first + n, hi_)
                if s < e:
                    rows = src.broadcast_to([n, HD])[0:e - s, :] if src.shape[0] == 1 else src[s - first:e - first, :]
                    for d in range(2):
                        sp.dma_start(tile[s - lo_:e - lo_, d, :], rows).then_inc(rows_loaded, 16)
                        loads[0] += 16
        n_v = 0
        for first, n, src in extended_rows(a["rel_v"]):
            for tile, lo_, hi_ in ((relv_rows[0], 0, P), (relv_rows[1], P, EXT)):
                s, e = max(first, lo_), min(first + n, hi_)
                if s < e:
                    rows = src.broadcast_to([n, HD])[0:e - s, :] if src.shape[0] == 1 else src[s - first:e - first, :]
                    sp.dma_start(tile[s - lo_:e - lo_, :], rows).then_inc(relv_loaded, 16)
                    n_v += 16
        sp.wait_ge(relv_loaded, n_v)
        sp.dma_start(scr["relv"][0:P, :], relv_rows[0][:, :]).then_inc(relv_stored, 16)
        sp.dma_start(scr["relv"][P:EXT, :], relv_rows[1][:, :]).then_inc(relv_stored, 16)
        sp.wait_ge(even_out, NQ // U)
        sp.wait_ge(odd_out, NQ // U)
        sp.dma_start(scr["R"].rearrange("b j f -> j b f"), R[:, :, :, :].rearrange("j (b p) e i -> j b (p e i)", b=B)).then_inc(r_stored, 16)
        sp.wait_ge(relv_stored, 32)
        sp.wait_ge(r_stored, 16)

    @block.gpsimd
    def _(pool):
        pool.memset(table[0][:, :, :], 0.0).then_inc(zeroed, 1)
        pool.memset(table[1][:, :, :], 0.0).then_inc(zeroed, 1)

    @block.tensor
    def _(pe):
        pe.wait_ge(rows_loaded, loads[0])
        pe.transpose(tbank[:, 0:P], ext[0][:, :, :].rearrange("r e d -> r (e d)"), ident[:, :])
        pe.transpose(tbank[:, P:EXT], ext[1][:, :, :].rearrange("r e d -> r (e d)"), ident[0:EXT - P, 0:EXT - P]).then_inc(turned, 1)
        pe.wait_ge(table_lo, 2)

        def group(g, u):
            for e, ready in ((0, even_ready), (1, odd_ready)):
                for v in range(U):
                    lhs = [t[:, e, bass.ds(g * (-2 * U) + (NQ - 1 - U * u - v), TXT)] for t in table]
                    rhs = [q[:, :, :].rearrange("d p (b i) -> d b p i", i=NQ)[:, :, :, bass.ds(g * (2 * U) + (U * u + v), 1)].squeeze(3) for q in qT]
                    mm = mm3(pe, bank[0:TXT, 2 * u + e, v * P:(v + 1) * P], lhs, rhs)
                mm.then_inc(ready, 1)

        group(0, 0)
        group(0, 1)
        with pe.Fori(1, NQ // (2 * U)) as g:
            for u in range(2):
                pe.wait_ge(even_out, g * 2 + (u - 1))
                pe.wait_ge(odd_out, g * 2 + (u - 1))
                group(g, u)

    def R_at(g, u, e):
        return R[:, :, e, bass.ds(g * (2 * U) + U * u, U)].rearrange("j q i -> j i q")

    def bank_of(u, e):
        return bank[0:TXT, 2 * u + e, :].rearrange("j (i q) -> j i q", i=U)

    @block.scalar
    def _(act):
        act.wait_ge(zeroed, 2)
        act.wait_ge(turned, 1)
        for e in range(2):
            h = slice(e * HD, (e + 1) * HD)
            split_hi(act, table[0][h, e, :], tbank[h, 0:EXT], SA).then_inc(table_hi, 1)
        with act.Fori(0, NQ // (2 * U)) as g:
            for u in range(2):
                act.wait_ge(even_ready, g * 2 + (u + 1))
                act.activation(R_at(g, u, 0), bank_of(u, 0), ACT.Copy, scale=1 / (SA * SA)).then_inc(even_out, 1)

    @block.vector
    def _(dve):
        for e in range(2):
            h = slice(e * HD, (e + 1) * HD)
            dve.wait_ge(table_hi, 2)
            split_lo(dve, table[1][h, e, :], tbank[h, 0:EXT], table[0][h, e, :], SA).then_inc(table_lo, 1)
        with dve.Fori(0, NQ // (2 * U)) as g:
            for u in range(2):
                dve.wait_ge(odd_ready, g * 2 + (u + 1))
                dve.tensor_scalar(R_at(g, u, 1), bank_of(u, 1), 1 / (SA * SA), None, ALU.mult).then_inc(odd_out, 1)


def audio_weights(nc, m, a, wkT, wv, gains, ident):
    wk_f = m.sb("wk_ap_f", [P, KD, INNER])
    wv_f = m.sb("wv_ap_f", [P, KD, INNER])
    bank = m.ps("wkT_bank", [P, 4, 512])
    wk_loaded, wv_loaded, ab_loaded = m.sem("wk_ap_loaded"), m.sem("wv_ap_loaded"), m.sem("alpha_beta_loaded")
    turned, hi_out, lo_out = m.sem("wkT_turned"), m.sem("wkT_hi"), m.sem("wkT_lo")
    wv_hi, wv_lo = m.sem("wv_ap_hi"), m.sem("wv_ap_lo")
    tanh_ready, gain_ready = m.sem("tanh_ready"), m.sem("gain_ready")
    block = m.ctx.enter_context(nc.Block())

    @block.sync
    def _(sp):
        sp.dma_start(wk_f[:, :, :], weight_rows(a["Wk_ap"])).then_inc(wk_loaded, 16)
        sp.dma_start(wv_f[:, :, :], weight_rows(a["Wv_ap"])).then_inc(wv_loaded, 16)
        for n, name in enumerate(("alpha", "beta")):
            sp.dma_start(gains[:, n:n + 1], a[name].rearrange("(a b) -> a b", a=1).broadcast_to([P, 1])).then_inc(ab_loaded, 16)

    def job(g):
        return bank[:, g, :].rearrange("p (m d) -> p m d", m=2), [w[:, 2 * g:2 * g + 2, :] for w in wkT]

    @block.tensor
    def _(pe):
        pe.wait_ge(wk_loaded, 16)
        for g in range(PAIRS // 2):
            for u in range(2):
                for k in range(KD):
                    mm = pe.transpose(bank[:, g, (2 * u + k) * P:(2 * u + k + 1) * P],
                                      wk_f[:, k, (2 * g + u) * P:(2 * g + u + 1) * P], ident[:, :])
            mm.then_inc(turned, 1)

    @block.scalar
    def _(act):
        for g in range(PAIRS // 2):
            act.wait_ge(turned, g + 1)
            src, dst = job(g)
            split_hi(act, dst[0], src, SW).then_inc(hi_out, 1)
        act.wait_ge(wv_loaded, 16)
        split_hi(act, wv[0][:, :, :], wv_f[:, :, :], SW).then_inc(wv_hi, 1)
        act.wait_ge(ab_loaded, 32)
        act.activation(gains[:, :], gains[:, :], ACT.Tanh).then_inc(tanh_ready, 1)

    @block.vector
    def _(dve):
        for g in range(PAIRS // 2):
            dve.wait_ge(hi_out, g + 1)
            src, dst = job(g)
            split_lo(dve, dst[1], src, dst[0], SW).then_inc(lo_out, 1)
        dve.wait_ge(wv_hi, 1)
        split_lo(dve, wv[1][:, :, :], wv_f[:, :, :], wv[0][:, :, :], SW).then_inc(wv_lo, 1)
        dve.wait_ge(tanh_ready, 1)
        dve.tensor_scalar(gains[:, 0:1], gains[:, 0:1], 1.0, None, ALU.add)
        dve.tensor_scalar(gains[:, 1:2], gains[:, 1:2], 1.0, 1 / (SP * SA), ALU.add, ALU.mult).then_inc(gain_ready, 1)


def cross_attention(nc, m, a, scr, qT, OT, wkT, wv, gains, ident):
    NPREP = NCH // 2
    nat = m.sb("ctx_nat", [P, NCH, D])
    ctx_s = [[m.sb(f"ctx_{s}{i}", [P, NCH, D], F16) for s in "hl"] for i in range(2)]
    ctxT = [[m.sb(f"ctxT_{s}{i}", [P, KD, NCH * P], F16) for s in "hl"] for i in range(2)]
    qf = [m.sb(f"q_fold_{s}", [P, KD, PAIRS, P], F16) for s in "hl"]
    prob = m.sb("prob", [P, AUD])
    PT = [m.sb(f"probT_{s}", [P, NCH, P], F16) for s in "hl"]
    BD = [[m.sb(f"q_diag_{s}{i}", [P, PAIRS, P], F16) for s in "hl"] for i in range(2)]
    u_sb = m.sb("u_sb", [P, D])
    UT = [m.sb(f"uT_{s}", [P, KD, P], F16) for s in "hl"]
    maxes = m.sb("maxes", [P, SB])
    top = m.sb("top", [P, 1])
    negmax = m.sb("negmax", [P, 1])
    den = m.sb("den", [P, 2])
    rden = m.sb("rden", [P, 1])
    KTb = m.sb("KT_b", [P, 2, PAIRS, TI], F16)
    Vb = m.sb("V_b", [TI, 2, INNER], F16)
    Rb = m.sb("R_b", [TI, 2 * 512])
    ST = m.sb("ST", [TI, 512])
    tprob = m.sb("tprob", [P, 4, TI])
    tmax = m.sb("tmax", [P, 2, 4])
    tsum = m.sb("tsum", [P, 2, 4])
    PTt = [m.sb(f"tprobT_{s}", [TI, 2, 512], F16) for s in "hl"]
    S = m.ps("S", [P, SB, 512])
    PTb = m.ps("PT_bank", [P, 2, 512])
    Ub = m.ps("U_bank", [P, 512])
    M0 = m.ps("M0", [P, 512])
    M1 = m.ps("M1", [P, 512])

    nat_loaded = m.sem("nat_loaded")
    kt_loaded, v_loaded, r_loaded = m.sem("kt_loaded"), m.sem("v_loaded"), m.sem("r_loaded")
    pt_stored = m.sem("tprob_stored")
    zeroed = m.sem("zeroed")
    bd_ready = m.sem("q_diag_ready")
    scores_ready = m.sem("scores_ready")
    maxes_ready = m.sem("maxes_ready")
    top_ready = m.sem("top_ready")
    negmax_ready = m.sem("negmax_ready")
    prob_ready = m.sem("prob_ready")
    pt_ready, pt_hi, pt_lo = m.sem("pt_ready"), m.sem("pt_hi"), m.sem("pt_lo")
    u_ready, rden_ready, u_normed = m.sem("u_ready"), m.sem("rden_ready"), m.sem("u_normed")
    ut_ready, ut_hi, ut_lo = m.sem("ut_ready"), m.sem("ut_hi"), m.sem("ut_lo")
    proj_ready = m.sem("proj_ready")
    ot_added = m.sem("ot_added")
    fold_ready, fold_hi, fold_lo = m.sem("fold_ready"), m.sem("fold_hi"), m.sem("fold_lo")
    ctxt_ready, ctxt_hi, ctxt_lo = m.sem("ctxt_ready"), m.sem("ctxt_hi"), m.sem("ctxt_lo")
    csplit_hi, csplit_lo = m.sem("csplit_hi"), m.sem("csplit_lo")
    text_ready = m.sem("text_ready")
    text_added = m.sem("text_added")
    st_ready = m.sem("st_ready")
    tmax_ready, ts_ready, te_ready = m.sem("tmax_ready"), m.sem("ts_ready"), m.sem("te_ready")
    tsum_ready, trec_ready, tgain_ready, tp_ready = m.sem("tsum_ready"), m.sem("trec_ready"), m.sem("tgain_ready"), m.sem("tp_ready")
    ptt_hi, ptt_lo = m.sem("ptt_hi"), m.sem("ptt_lo")

    block = m.ctx.enter_context(nc.Block())
    ctx = a["ctx"]
    MAIN = (NCH - 1) * P

    def rows_of(c):
        return TAIL if c == NCH - 1 else P

    def width(n):
        return min(512, AUD - 512 * n)

    def batches(eng, body):
        with eng.Fori(0, B // 2 - 1) as j:
            body(j * 2, 0, B)
            body(j * 2 + 1, 1, B)
        body(B - 2, 0, 1)
        body(B - 1, 1, 0)

    @block.sync
    def _(sp):
        def flat(t, offset, n):
            whole = t.rearrange(" ".join("abcd"[:len(t.shape)]) + " -> (" + " ".join("abcd"[:len(t.shape)]) + ")")
            return whole[bass.ds(offset, n)]

        def load_nat(at, tail_at):
            sp.dma_start(nat[:, 0:NCH - 1, :], flat(ctx, at, MAIN * D).rearrange("(p c d) -> p c d", p=P, d=D)).then_inc(nat_loaded, 16)
            sp.dma_start(nat[0:TAIL, NCH - 1, :], flat(ctx, tail_at, TAIL * D).rearrange("(p d) -> p d", p=TAIL)).then_inc(nat_loaded, 16)

        def load_kt(at):
            sp.dma_start(KTb[:, :, :, :].rearrange("p s m j -> p (s m j)"),
                         flat(scr["kt"], at, P * KT_ROW).rearrange("(p f) -> p f", p=P)).then_inc(kt_loaded, 16)

        def load_r(at):
            sp.dma_start(Rb[0:TXT, :], flat(scr["R"], at, TXT * 1024).rearrange("(j f) -> j f", j=TXT)).then_inc(r_loaded, 16)

        def load_v(text_at, image_at):
            v = Vb[:, :, :].rearrange("j s n -> j (s n)")
            sp.dma_start(v[0:TXT, :], flat(scr["v"], text_at, TXT * V_ROW).rearrange("(j f) -> j f", j=TXT)).then_inc(v_loaded, 16)
            sp.dma_start(v[TXT:TI, :], flat(scr["v"], image_at, IMG * V_ROW).rearrange("(j f) -> j f", j=IMG)).then_inc(v_loaded, 16)

        V_ROW, KT_ROW = 2 * INNER, 2 * PAIRS * TI
        V_IMG = B * TXT * V_ROW
        NAT0 = TI * D
        load_nat(NAT0, NAT0 + MAIN * D)
        load_kt(0)
        sp.wait_ge(zeroed, 1)
        load_r(0)
        load_v(0, V_IMG)
        sp.wait_ge(ctxt_ready, NPREP)
        sp.wait_ge(csplit_lo, NPREP)
        load_nat(NAT0 + CTX * D, NAT0 + (CTX + MAIN) * D)

        def body(b, parity, left):
            fixed = (lambda v: v) if isinstance(b, int) else sp.snap
            nat_at = fixed(b * (CTX * D) + (NAT0 + 2 * CTX * D))
            nat_tail_at = fixed(b * (CTX * D) + (NAT0 + 2 * CTX * D + MAIN * D))
            kt_at = fixed(b * (P * KT_ROW) + P * KT_ROW)
            r_at = fixed(b * (TXT * 1024) + TXT * 1024)
            vt_at = fixed(b * (TXT * V_ROW) + TXT * V_ROW)
            vi_at = fixed(b * (IMG * V_ROW) + (V_IMG + IMG * V_ROW))
            pt_at = fixed(b * (TXT * 2048))
            kt_read, v_read = fixed(b * 8 + 5), fixed(b * 8 + 8)
            r_read, prepared, stored = fixed(b * 2 + 2), fixed((b + 2) * NPREP), fixed((b + 1) * 32)
            if left:
                sp.wait_ge(text_ready, kt_read)
                load_kt(kt_at)
                sp.wait_ge(st_ready, r_read)
                load_r(r_at)
            if left > 1:
                sp.wait_ge(ctxt_ready, prepared)
                sp.wait_ge(csplit_lo, prepared)
                load_nat(nat_at, nat_tail_at)
            sp.wait_ge(text_ready, v_read)
            for s in range(2):
                sp.dma_start(flat(scr["pt"], pt_at, TXT * 2048).rearrange("(j s f) -> j s f", j=TXT, s=2)[:, s, :],
                             PTt[s][0:TXT, :, :].rearrange("j h f -> j (h f)")).then_inc(pt_stored, 16)
            if left:
                sp.wait_ge(pt_stored, stored)
                load_v(vt_at, vi_at)

        batches(sp, body)
        sp.wait_ge(pt_stored, B * 32)

    @block.gpsimd
    def _(pool):
        pool.memset(Rb[64:TI, :], 0.0).then_inc(zeroed, 1)
        pool.wait_ge(zeroed, 1)
        for i in range(2):
            for s in range(2):
                pool.memset(BD[i][s][:, :, :], 0.0).then_inc(zeroed, 1)
        pool.wait_ge(zeroed, 5)

        def diagonal(b, parity):
            for s in range(2):
                for e in range(2):
                    h = slice(e * HD, (e + 1) * HD)
                    pool.tensor_copy(BD[parity][s][h, :, h], qT[s][h, :, bass.ds(b * NQ, NQ)]).then_inc(bd_ready, 1)
                    pool.wait_ge(bd_ready, b * 4 + (2 * s + e + 1))

        diagonal(0, 0)
        diagonal(1, 1)

        def body(b, parity, left):
            if left > 1:
                pool.wait_ge(text_ready, b * 8 + 5)
                diagonal(b + 2, parity)

        batches(pool, body)

    @block.tensor
    def _(pe):
        def scores(r, p, parity, n):
            for k in range(KD):
                lhs = [q[:, k, p, :] for q in qf]
                rhs = [c[:, k, n * 512:n * 512 + width(n)] for c in ctxT[parity]]
                mm = mm3(pe, S[:, n, 0:width(n)], lhs, rhs, k == 0, k == KD - 1)
            mm.then_inc(scores_ready, 1)

        def turn_prob(r, j):
            for c in range(4 * j, 4 * j + 4):
                mm = pe.transpose(PTb[0:rows_of(c), j % 2, (c % 4) * P:(c % 4 + 1) * P],
                                  prob[:, c * P:c * P + rows_of(c)], ident[:, :])
            mm.then_inc(pt_ready, 1)

        def prob_ctx(r, parity, j):
            pe.wait_ge(pt_lo, r * 3 + (j + 1))
            for c in range(4 * j, 4 * j + 4):
                n = rows_of(c)
                mm = mm3(pe, Ub[:, 0:D], [t[0:n, c, :] for t in PT], [x[0:n, c, :] for x in ctx_s[parity]],
                         c == 0, c == NCH - 1)
            if j == 2:
                mm.then_inc(u_ready, 1)

        def turn_u(r):
            pe.wait_ge(u_normed, r + 1)
            for k in range(KD):
                mm = pe.transpose(M0[:, k * P:(k + 1) * P], u_sb[:, k * P:(k + 1) * P], ident[:, :])
            mm.then_inc(ut_ready, 1)

        def project_u(r, p):
            pe.wait_ge(ut_lo, r + 1)
            for k in range(KD):
                mm = mm3(pe, M0[:, 0:P], [w[:, k, p * P:(p + 1) * P] for w in wv], [u[:, k, :] for u in UT],
                         k == 0, k == KD - 1)
            mm.then_inc(proj_ready, 1)

        def fold(p, parity):
            for k in range(KD):
                mm = mm3(pe, M0[:, k * P:(k + 1) * P], [w[:, p, k * P:(k + 1) * P] for w in wkT],
                         [q[:, p, :] for q in BD[parity]])
            mm.then_inc(fold_ready, 1)

        def turn_ctx(j):
            for u in range(2):
                n = rows_of(2 * j + u)
                for k in range(KD):
                    at = (2 * k + u) * P
                    mm = pe.transpose(M1[:, at:at + n], nat[0:n, 2 * j + u, k * P:(k + 1) * P], ident[0:n, 0:n])
            mm.then_inc(ctxt_ready, 1)

        def text(b, p, parity):
            half, stage = divmod(p, 4)
            if stage == 0:
                if half == 0:
                    pe.wait_ge(kt_loaded, (b + 1) * 16)
                for q in range(4):
                    mm = mm3(pe, M1[0:TI, q * P:(q + 1) * P], [KTb[:, s, 4 * half + q, :] for s in range(2)],
                             [BD[parity][s][:, 4 * half + q, :] for s in range(2)])
            elif stage == 1:
                pe.wait_ge(st_ready, b * 2 + (half + 1))
                for q in range(4):
                    mm = pe.transpose(M1[:, q * TI:(q + 1) * TI], ST[:, q * P:(q + 1) * P], ident[0:TI, 0:TI])
            elif stage == 2:
                pe.wait_ge(tp_ready, b * 2 + (half + 1))
                for q in range(4):
                    mm = pe.transpose(M1[0:TI, q * P:(q + 1) * P], tprob[:, q, :], ident[:, :])
            else:
                pe.wait_ge(ptt_lo, b * 2 + (half + 1))
                if half == 0:
                    pe.wait_ge(v_loaded, (b + 1) * 32)
                for q in range(4):
                    at = (4 * half + q) * P
                    mm = mm3(pe, M1[:, q * P:(q + 1) * P], [Vb[:, s, at:at + P] for s in range(2)],
                             [t[:, half, q * P:(q + 1) * P] for t in PTt])
            mm.then_inc(text_ready, 1)

        def text_bank_free(b, p):
            half, stage = divmod(p - 1, 4)
            if p == 0:
                pe.wait_ge(text_added, b * 2 + 1)
            elif stage == 3:
                pe.wait_ge(text_added, b * 2 + (half + 2))
            else:
                pe.wait_ge((st_ready, ts_ready, ptt_lo)[stage], b * 2 + (half + 1))

        for j in range(NPREP):
            if j == 0:
                pe.wait_ge(nat_loaded, 32)
            else:
                pe.wait_ge(ctxt_lo, j)
            turn_ctx(j)
        pe.wait_ge(bd_ready, 4)
        for p in range(PAIRS):
            if p:
                pe.wait_ge(fold_lo, p)
            fold(p, 0)
        pe.wait_ge(ctxt_lo, NPREP)
        pe.wait_ge(fold_lo, 1)
        for n in range(SB):
            scores(0, 0, 0, n)
        pe.wait_ge(fold_lo, PAIRS)

        def body(b, parity, left):
            for p in range(PAIRS):
                r = b * 8 + p
                follows = p < PAIRS - 1 or left
                nb, np_, npar = (b, p + 1, parity) if p < PAIRS - 1 else (b + 1, 0, 1 - parity)

                def next_scores(n):
                    if follows:
                        if p == PAIRS - 1:
                            pe.wait_ge(ctxt_lo, nb * NPREP + (2 * n + 2))
                        scores(r + 1, np_, npar, n)

                pe.wait_ge(prob_ready, r + 1)
                turn_prob(r, 0)
                turn_prob(r, 1)
                if p:
                    if left:
                        pe.wait_ge(fold_lo, (b + 1) * 8 + p)
                    else:
                        pe.wait_ge(ot_added, r)
                    turn_u(r - 1)
                next_scores(0)
                pe.wait_ge(pt_lo, r * 3 + 1)
                turn_prob(r, 2)
                next_scores(1)
                if p:
                    project_u(r - 1, p - 1)
                next_scores(2)
                text_bank_free(b, p)
                if left and 1 <= p <= NPREP:
                    if p == 1:
                        pe.wait_ge(nat_loaded, (b + 2) * 32)
                    turn_ctx(p - 1)
                if p == 0:
                    pe.wait_ge(csplit_lo, (b + 1) * NPREP)
                prob_ctx(r, parity, 0)
                if left:
                    if p == 0:
                        pe.wait_ge(bd_ready, (b + 2) * 4)
                    pe.wait_ge(ot_added, r + 1)
                    fold(p, 1 - parity)
                prob_ctx(r, parity, 1)
                if left and 1 <= p <= NPREP:
                    pe.wait_ge(ctxt_lo, (b + 1) * NPREP + p)
                if p < PAIRS - 1:
                    text(b, p, parity)
                prob_ctx(r, parity, 2)
                if p == PAIRS - 1:
                    text(b, p, parity)
            r = b * 8 + (PAIRS - 1)
            if left:
                pe.wait_ge(fold_lo, (b + 1) * 8 + PAIRS)
            else:
                pe.wait_ge(ot_added, r + 1)
            turn_u(r)
            project_u(r, PAIRS - 1)

        batches(pe, body)

    def pt_io(j):
        full = 4 if j < 2 else 3
        bank = PTb[:, j % 2, :].rearrange("p (c q) -> p c q", c=4)
        io = [(bank[:, 0:full, :], [t[:, 4 * j:4 * j + full, :] for t in PT])]
        if full < 4:
            io.append((bank[0:TAIL, 3, :], [t[0:TAIL, 4 * j + 3, :] for t in PT]))
        return io

    def ctxt_io(j, parity):
        n = P + rows_of(2 * j + 1)
        return [(M1[:, 2 * k * P:2 * k * P + n], [t[:, k, 2 * j * P:2 * j * P + n] for t in ctxT[parity]]) for k in range(KD)]

    def each(io, f):
        for src, dst in io:
            ins = f(src, dst)
        return ins

    M0_k = M0[:, 0:KD * P].rearrange("p (k q) -> p k q", k=KD)

    @block.scalar
    def _(act):
        def prob_exp(r, p):
            act.wait_ge(negmax_ready, r + 1)
            act.activation(prob[:, :], S[:, :, :].rearrange("p n f -> p (n f)")[:, 0:AUD], ACT.Exp, bias=negmax[:, 0:1],
                           scale=1 / (SA * SA), accum_out=den[:, p % 2:p % 2 + 1]).then_inc(prob_ready, 1)

        def prob_hi(r, j):
            act.wait_ge(pt_ready, r * 3 + (j + 1))
            each(pt_io(j), lambda s, d: split_hi(act, d[0], s, SP)).then_inc(pt_hi, 1)

        def u_hi(r):
            act.wait_ge(ut_ready, r + 1)
            split_hi(act, UT[0][:, :, :], M0_k, SA).then_inc(ut_hi, 1)

        def fold_hi_(count, p):
            act.wait_ge(fold_ready, count)
            split_hi(act, qf[0][:, :, p, :], M0_k, SA / (SA * SW)).then_inc(fold_hi, 1)

        def ctxt_hi_(count, j, parity):
            act.wait_ge(ctxt_ready, count)
            each(ctxt_io(j, parity), lambda s, d: split_hi(act, d[0], s, SA)).then_inc(ctxt_hi, 1)

        for j in range(NPREP):
            ctxt_hi_(j + 1, j, 0)
        for p in range(PAIRS):
            fold_hi_(p + 1, p)
        prob_exp(0, 0)

        def body(b, parity, left):
            for p in range(PAIRS):
                r = b * 8 + p
                half, stage = divmod(p, 4)
                prob_hi(r, 0)
                prob_hi(r, 1)
                if p:
                    u_hi(r - 1)
                prob_hi(r, 2)
                if p < PAIRS - 1 or left:
                    prob_exp(r + 1, p + 1)
                if left and 1 <= p <= NPREP:
                    ctxt_hi_((b + 1) * NPREP + p, p - 1, 1 - parity)
                if left:
                    fold_hi_((b + 1) * 8 + (p + 1), p)
                if stage == 1:
                    act.wait_ge(ts_ready, b * 2 + (half + 1))
                    act.activation(tprob[:, :, :], tprob[:, :, :], ACT.Exp).then_inc(te_ready, 1)
                if stage == 2:
                    if half == 0:
                        act.wait_ge(v_loaded, (b + 1) * 32)
                    act.wait_ge(text_ready, r + 1)
                    split_hi(act, PTt[0][:, half, :], M1[0:TI, :], SP).then_inc(ptt_hi, 1)
            u_hi(b * 8 + (PAIRS - 1))

        batches(act, body)

    @block.vector
    def _(dve):
        def row_max(r, n):
            dve.wait_ge(scores_ready, r * 3 + (n + 1))
            dve.tensor_reduce(maxes[:, n:n + 1], S[:, n, 0:width(n)], X, ALU.max).then_inc(maxes_ready, 1)
            if n == SB - 1:
                dve.wait_ge(maxes_ready, r * 3 + SB)
                dve.tensor_reduce(top[:, :], maxes[:, :], X, ALU.max).then_inc(top_ready, 1)
                dve.wait_ge(top_ready, r + 1)
                dve.tensor_scalar(negmax[:, :], top[:, :], -1 / (SA * SA), None, ALU.mult).then_inc(negmax_ready, 1)

        def prob_lo(r, j):
            dve.wait_ge(pt_hi, r * 3 + (j + 1))
            each(pt_io(j), lambda s, d: split_lo(dve, d[1], s, d[0], SP)).then_inc(pt_lo, 1)

        def u_lo(r):
            dve.wait_ge(ut_hi, r + 1)
            split_lo(dve, UT[1][:, :, :], M0_k, UT[0][:, :, :], SA).then_inc(ut_lo, 1)

        def u_norm(r, p):
            dve.wait_ge(prob_ready, r + 1)
            dve.reciprocal(rden[:, :], den[:, p % 2:p % 2 + 1]).then_inc(rden_ready, 1)
            dve.wait_ge(rden_ready, r + 1)
            dve.wait_ge(u_ready, r + 1)
            dve.tensor_scalar(u_sb[:, :], Ub[:, 0:D], rden[:, 0:1], gains[:, 1:2], ALU.mult, ALU.mult).then_inc(u_normed, 1)

        def add_heads(b, pairs, src, scale):
            for e in range(2):
                h = slice(e * HD, (e + 1) * HD)
                dst = OT[h, pairs, bass.ds(b * NQ, NQ)]
                ins = dve.scalar_tensor_tensor(out=dst, in0=src[h, :, h], scalar=scale, in1=dst, op0=ALU.mult, op1=ALU.add)
            return ins

        def add_audio(b, r, p):
            dve.wait_ge(proj_ready, r + 1)
            dve.wait_ge(text_added, b * 2 + (1 if p < 3 else 2 if p < PAIRS - 1 else 3))
            add_heads(b, slice(p, p + 1), M0[:, 0:P].unsqueeze(1), 1 / (SA * SW)).then_inc(ot_added, 1)

        def fold_lo_(count, p):
            dve.wait_ge(fold_hi, count)
            split_lo(dve, qf[1][:, :, p, :], M0_k, qf[0][:, :, p, :], SA / (SA * SW)).then_inc(fold_lo, 1)

        def ctxt_lo_(count, j, parity):
            dve.wait_ge(ctxt_hi, count)
            each(ctxt_io(j, parity), lambda s, d: split_lo(dve, d[1], s, d[0], SA)).then_inc(ctxt_lo, 1)

        def ctx_split(count, j, parity):
            parts = [(slice(0, P), slice(2 * j, 2 * j + 2))] if 2 * j + 2 < NCH else \
                [(slice(0, P), slice(2 * j, 2 * j + 1)), (slice(0, TAIL), slice(2 * j + 1, 2 * j + 2))]
            hi, lo = ctx_s[parity]
            for ps, cs in parts:
                ins = dve.tensor_scalar(hi[ps, cs, :], nat[ps, cs, :], SA, None, ALU.mult)
            ins.then_inc(csplit_hi, 1)
            dve.wait_ge(csplit_hi, count)
            for ps, cs in parts:
                ins = split_lo(dve, lo[ps, cs, :], nat[ps, cs, :], hi[ps, cs, :], SA)
            ins.then_inc(csplit_lo, 1)

        def text_probs(b, half):
            dve.wait_ge(te_ready, b * 2 + (half + 1))
            dve.tensor_reduce(tsum[:, 0, :], tprob[:, :, 0:TXT], X, ALU.add)
            dve.tensor_reduce(tsum[:, 1, :], tprob[:, :, TXT:TI], X, ALU.add).then_inc(tsum_ready, 1)
            dve.wait_ge(tsum_ready, b * 2 + (half + 1))
            dve.reciprocal(tsum[:, :, :], tsum[:, :, :]).then_inc(trec_ready, 1)
            dve.wait_ge(trec_ready, b * 2 + (half + 1))
            dve.tensor_scalar(tsum[:, 1, :], tsum[:, 1, :], gains[:, 0:1], None, ALU.mult).then_inc(tgain_ready, 1)
            dve.tensor_tensor(tprob[:, :, 0:TXT], tprob[:, :, 0:TXT], tsum[:, 0, :].unsqueeze(2).broadcast_to([P, 4, TXT]), ALU.mult)
            dve.wait_ge(tgain_ready, b * 2 + (half + 1))
            dve.tensor_tensor(tprob[:, :, TXT:TI], tprob[:, :, TXT:TI], tsum[:, 1, :].unsqueeze(2).broadcast_to([P, 4, IMG]),
                              ALU.mult).then_inc(tp_ready, 1)

        def text(b, r, p):
            half, stage = divmod(p, 4)
            n = b * 2 + (half + 1)
            if stage == 0:
                if half == 0:
                    dve.wait_ge(r_loaded, (b + 1) * 16)
                dve.wait_ge(text_ready, r + 1)
                dve.scalar_tensor_tensor(out=ST[:, :], in0=M1[0:TI, :], scalar=1 / (SA * SA), in1=Rb[:, half * 512:(half + 1) * 512],
                                         op0=ALU.mult, op1=ALU.add).then_inc(st_ready, 1)
            elif stage == 1:
                dve.wait_ge(text_ready, r + 1)
                s = M1[:, 0:4 * TI].rearrange("p (q j) -> p q j", q=4)
                dve.tensor_reduce(tmax[:, 0, :], s[:, :, 0:TXT], X, ALU.max)
                dve.tensor_reduce(tmax[:, 1, :], s[:, :, TXT:TI], X, ALU.max).then_inc(tmax_ready, 1)
                dve.wait_ge(tmax_ready, n)
                dve.tensor_tensor(tprob[:, :, 0:TXT], s[:, :, 0:TXT], tmax[:, 0, :].unsqueeze(2).broadcast_to([P, 4, TXT]), ALU.subtract)
                dve.tensor_tensor(tprob[:, :, TXT:TI], s[:, :, TXT:TI], tmax[:, 1, :].unsqueeze(2).broadcast_to([P, 4, IMG]),
                                  ALU.subtract).then_inc(ts_ready, 1)
            elif stage == 2:
                dve.wait_ge(ptt_hi, n)
                split_lo(dve, PTt[1][:, half, :], M1[0:TI, :], PTt[0][:, half, :], SP).then_inc(ptt_lo, 1)
            else:
                dve.wait_ge(text_ready, r + 1)
                dve.wait_ge(ot_added, r + 1)
                add_heads(b, slice(4 * half, 4 * half + 4), M1[:, :].rearrange("p (q c) -> p q c", q=4),
                          1 / (SP * SA)).then_inc(text_added, 1)

        dve.memset(OT[:, 0:PAIRS // 2, :], 0.0).then_inc(ot_added, 1)
        dve.memset(OT[:, PAIRS // 2:, :], 0.0).then_inc(text_added, 1)
        dve.wait_ge(nat_loaded, 32)
        for j in range(NPREP):
            ctx_split(j + 1, j, 0)
            ctxt_lo_(j + 1, j, 0)
        for p in range(PAIRS):
            fold_lo_(p + 1, p)
        for n in range(SB):
            row_max(0, n)

        def body(b, parity, left):
            for p in range(PAIRS):
                r = b * 8 + p
                follows = p < PAIRS - 1 or left
                prob_lo(r, 0)
                prob_lo(r, 1)
                if p:
                    u_lo(r - 1)
                if follows:
                    row_max(r + 1, 0)
                prob_lo(r, 2)
                if follows:
                    row_max(r + 1, 1)
                if p:
                    add_audio(b, r - 1, p - 1)
                if follows:
                    row_max(r + 1, 2)
                if p % 4 == 2:
                    text_probs(b, p // 4)
                if left and 1 <= p <= NPREP:
                    if p == 1:
                        dve.wait_ge(nat_loaded, (b + 2) * 32)
                    ctxt_lo_((b + 1) * NPREP + p, p - 1, 1 - parity)
                if left:
                    fold_lo_((b + 1) * 8 + (p + 1), p)
                if left and 1 <= p <= NPREP:
                    ctx_split((b + 1) * NPREP + p, p - 1, 1 - parity)
                text(b, r, p)
                u_norm(r, p)
            r = b * 8 + (PAIRS - 1)
            u_lo(r)
            add_audio(b, r, PAIRS - 1)

        batches(dve, body)


def relative_values(nc, m, scr, OT, ident):
    probs = m.sb("tprob_all", [TXT, B, 2, PAIRS * 2 * NQ], F16)
    window_f = m.sb("relv_window_f", [TXT, NQ, HD])
    window = [m.sb(f"relv_window_{s}", [TXT, NQ, 2, HD], F16) for s in "hl"]
    U = 4
    bank = m.ps("relv_bank", [P, U, 512])
    probs_loaded, window_loaded = m.sem("tprobs_loaded"), m.sem("relv_window_loaded")
    window_hi, window_lo = m.sem("relv_window_hi"), m.sem("relv_window_lo")
    rel_ready, rel_added = m.sem("relv_ready"), m.sem("relv_added")
    block = m.ctx.enter_context(nc.Block())

    @block.sync
    def _(sp):
        rows = scr["relv"]
        overlapping = bass.AP(tensor=rows.tensor, offset=rows.offset, ap=[[HD, TXT], [1, NQ * HD]])
        sp.dma_start(window_f[:, :, :].rearrange("j i d -> j (i d)"), overlapping).then_inc(window_loaded, 16)
        sp.dma_start(probs[:, :, :, :].rearrange("j b s f -> j b (s f)"), scr["pt"].rearrange("b j s f -> j b (s f)")).then_inc(probs_loaded, 16)

    @block.tensor
    def _(pe):
        pe.wait_ge(window_lo, 1)
        pe.wait_ge(probs_loaded, 16)

        def group(g, u):
            for v in range(2):
                at = 2 * u + v
                lhs = [w[:, bass.ds(g * (-2 * U) + (NQ - 1 - at), 1), :, :].rearrange("j o e d -> j (o e d)") for w in window]
                rhs = [probs[:, :, s, :].rearrange("j b (h i) -> j h b i", i=NQ)[:, :, :, bass.ds(g * (2 * U) + at, 1)].squeeze(3)
                       for s in range(2)]
                mm = mm3(pe, bank[:, u, v * 256:(v + 1) * 256], lhs, rhs)
            mm.then_inc(rel_ready, 1)

        for u in range(U):
            group(0, u)
        with pe.Fori(1, NQ // (2 * U)) as g:
            for u in range(U):
                pe.wait_ge(rel_added, g * U + (u + 1 - U))
                group(g, u)

    @block.scalar
    def _(act):
        act.wait_ge(window_loaded, 16)
        for e in range(2):
            split_hi(act, window[0][:, :, e, :], window_f[:, :, :], SW).then_inc(window_hi, 1)

    @block.vector
    def _(dve):
        for e in range(2):
            dve.wait_ge(window_hi, e + 1)
            ins = split_lo(dve, window[1][:, :, e, :], window_f[:, :, :], window[0][:, :, e, :], SW)
        ins.then_inc(window_lo, 1)

        with dve.Fori(0, NQ // (2 * U)) as g:
            for u in range(U):
                dve.wait_ge(rel_ready, g * U + (u + 1))
                for e in range(2):
                    h = slice(e * HD, (e + 1) * HD)
                    for v in range(2):
                        dst = OT[h, :, :].rearrange("d p (b i) -> d p b i", i=NQ)[:, :, :, bass.ds(g * (2 * U) + (2 * u + v), 1)].squeeze(3)
                        src = bank[h, u, v * 256:(v + 1) * 256].rearrange("d (p e b) -> d p e b", p=PAIRS, e=2)[:, :, e, :]
                        ins = dve.scalar_tensor_tensor(out=dst, in0=src, scalar=1 / (SP * SW), in1=dst, op0=ALU.mult, op1=ALU.add)
                ins.then_inc(rel_added, 1)


def cross_output(nc, m, a, OT, x):
    O = [m.sb(f"O_{s}", [P, PAIRS, T], F16) for s in "hl"]
    wo_f = m.sb("wo_f", [P, PAIRS, D])
    wo = [m.sb(f"wo_{s}", [P, PAIRS, D], F16) for s in "hl"]
    bo = m.sb("bo", [P, D])
    bank = m.ps("out_bank", [P, TT, 512])
    x_loaded, wo_loaded, bo_loaded = m.sem("x_loaded"), m.sem("wo_loaded"), m.sem("bo_loaded")
    wo_hi, wo_lo, o_hi, o_lo = m.sem("wo_hi"), m.sem("wo_lo"), m.sem("o_hi"), m.sem("o_lo")
    xb_ready, y_ready, x_ready = m.sem("xb_ready"), m.sem("y_ready"), m.sem("x1_ready")
    block = m.ctx.enter_context(nc.Block())

    @block.sync
    def _(sp):
        sp.dma_start(wo_f[:, :, :], a["Wo"].rearrange("(m p) n -> p m n", p=P)).then_inc(wo_loaded, 16)
        sp.dma_start(x[:, :, :], a["x"].rearrange("(t b) q d -> (b q) t d", b=2)).then_inc(x_loaded, 16)
        sp.dma_start(bo[:, :], a["bo"].rearrange("(o n) -> o n", o=1).broadcast_to([P, D])).then_inc(bo_loaded, 16)

    @block.gpsimd
    def _(pool):
        pool.wait_ge(x_loaded, 16)
        pool.wait_ge(bo_loaded, 16)
        pool.tensor_tensor(x[:, :, :], x[:, :, :], bo[:, :].unsqueeze(1).broadcast_to([P, TT, D]), ALU.add).then_inc(xb_ready, 1)

    HALF = T // 2

    @block.scalar
    def _(act):
        act.wait_ge(wo_loaded, 16)
        split_hi(act, wo[0][:, :, :], wo_f[:, :, :], SW).then_inc(wo_hi, 1)
        for h in range(4):
            c = slice(h * 256, (h + 1) * 256)
            split_hi(act, O[0][:, :, c], OT[:, :, c], SA).then_inc(o_hi, 1)

    @block.vector
    def _(dve):
        dve.wait_ge(wo_hi, 1)
        split_lo(dve, wo[1][:, :, :], wo_f[:, :, :], wo[0][:, :, :], SW).then_inc(wo_lo, 1)
        for h in range(4):
            c = slice(h * 256, (h + 1) * 256)
            dve.wait_ge(o_hi, h + 1)
            split_lo(dve, O[1][:, :, c], OT[:, :, c], O[0][:, :, c], SA).then_inc(o_lo, 1)
        dve.wait_ge(xb_ready, 1)
        for t in range(TT):
            dve.wait_ge(y_ready, t + 1)
            dve.scalar_tensor_tensor(out=x[:, t, :], in0=bank[:, t, 0:D], scalar=1 / (SA * SW), in1=x[:, t, :],
                                     op0=ALU.mult, op1=ALU.add).then_inc(x_ready, 1)

    @block.tensor
    def _(pe):
        pe.wait_ge(wo_lo, 1)
        for t in range(TT):
            pe.wait_ge(o_lo, t // 2 + 1)
            for k in range(PAIRS):
                mm = mm3(pe, bank[:, t, 0:D], [o[:, k, t * P:(t + 1) * P] for o in O], [w[:, k, :] for w in wo],
                         k == 0, k == PAIRS - 1)
            mm.then_inc(y_ready, 1)


class TurnedTokens:

    def __init__(self, m, name, bank):
        self.T = [m.sb(f"{name}_T{s}", [P, KD, T], F16) for s in "hl"]
        self.bank = bank
        self.ready, self.hi, self.lo = m.sem(name + "_turned"), m.sem(name + "_T_hi"), m.sem(name + "_T_lo")

    def tensor(self, pe, xn, xn_ready, ident):
        for g in range(TT // 2):
            pe.wait_ge(xn_ready, 2 * g + 2)
            for k in range(KD):
                for t in range(2):
                    at = (2 * k + t) * P
                    mm = pe.transpose(self.bank[:, g, at:at + P], xn[:, 2 * g + t, k * P:(k + 1) * P], ident[:, :])
            mm.then_inc(self.ready, 1)

    def io(self, g, s):
        return self.T[s][:, :, g * 2 * P:(g + 1) * 2 * P], self.bank[:, g, :].rearrange("p (k t) -> p k t", k=KD)

    def scalar(self, act):
        for g in range(TT // 2):
            act.wait_ge(self.ready, g + 1)
            split_hi(act, *self.io(g, 0), SA).then_inc(self.hi, 1)

    def vector(self, dve):
        for g in range(TT // 2):
            dve.wait_ge(self.hi, g + 1)
            dst, src = self.io(g, 1)
            split_lo(dve, dst, src, self.io(g, 0)[0], SA).then_inc(self.lo, 1)


def self_attention(nc, m, a, x, ident, used):
    SH, SHD, G = 16, D // 16, 8
    NG = SH // G
    AW = D * 3
    w_f = m.sb("w_attn_f", [P, KD, AW])
    w = [m.sb(f"w_attn_{s}", [P, KD, AW], F16) for s in "hl"]
    wp_f = m.sb("w_proj_f", [P, KD, D])
    wp = [m.sb(f"w_proj_{s}", [P, KD, D], F16) for s in "hl"]
    b_rows = m.sb("b_attn_rows", [4, P])
    b_cols = m.sb("b_attn_cols", [P, 4])
    b_v = m.sb("b_v", [P, D])
    b_p = m.sb("b_proj", [P, D])
    xn = m.sb("xn_b", [P, TT, D])
    qk = m.sb("qk_T", [P, 2 * NG, T])
    spread = m.sb("head_mask", [P, G])
    kd = [m.sb(f"k_diag{i}", [P, G, NQ]) for i in range(4)]
    vd = m.sb("v_diag", [P, B, SH // 2, 2, SHD])
    pr = [m.sb(f"self_prob{i}", [P, G, NQ]) for i in range(2)]
    prT = [m.sb(f"self_probT{i}", [P, 4, P]) for i in range(2)]
    top, total = m.sb("self_max", [P, 2, G]), m.sb("self_sum", [P, 2, G])
    o_sb = m.sb("self_o", [P, TT, D])
    oT = [m.sb(f"self_oT_{s}", [P, KD, T], F16) for s in "hl"]
    bank = m.ps("self_bank", [P, 8, 512])

    norm = Norm(m, "norm_b")
    turned = TurnedTokens(m, "xn_b", bank)
    w_loaded, wp_loaded, b_loaded = m.sem("w_attn_loaded"), m.sem("w_proj_loaded"), m.sem("b_attn_loaded")
    bv_loaded, bp_loaded = m.sem("b_v_loaded"), m.sem("b_proj_loaded")
    w_hi, w_lo = m.sem("w_attn_hi"), m.sem("w_attn_lo")
    mask_ready = m.sem("head_mask_ready")
    vd_cleared = m.sem("v_diag_cleared")
    bias_turned, bias_ready = m.sem("b_attn_turned"), m.sem("b_attn_ready")
    qk_ready, qk_out = m.sem("qk_ready"), m.sem("qk_out")
    v_ready, v_out = m.sem("self_v_ready"), m.sem("self_v_out")
    kd_ready = m.sem("k_diag_ready")
    s_ready, top_ready, sub_ready, exp_ready = m.sem("self_s_ready"), m.sem("self_top_ready"), m.sem("self_sub_ready"), m.sem("self_exp_ready")
    sum_ready, rec_ready, p_ready = m.sem("self_sum_ready"), m.sem("self_rec_ready"), m.sem("self_p_ready")
    pT_ready, pT_out = m.sem("self_pT_ready"), m.sem("self_pT_out")
    o_ready, o_out = m.sem("self_o_ready"), m.sem("self_o_out")
    oT_ready, oT_hi, oT_lo = m.sem("self_oT_ready"), m.sem("self_oT_hi"), m.sem("self_oT_lo")
    xb_ready, y_ready, y_added = m.sem("xb2_ready"), m.sem("self_y_ready"), m.sem("x2_ready")
    block = m.ctx.enter_context(nc.Block())
    NQK = 2 * NG * 2
    S_BANK, T_BANK, O_BANK = (0, 1), (2, 3), (4, 5)

    @block.sync
    def _(sp):
        sp.dma_start(w_f[:, :, :], weight_rows(a["w_attn"])).then_inc(w_loaded, 16)
        sp.dma_start(b_rows[:, :], a["b_attn"][0:2 * D].rearrange("(m p) -> m p", p=P)).then_inc(b_loaded, 16)
        sp.dma_start(b_v[:, :], a["b_attn"][2 * D:3 * D].rearrange("(o n) -> o n", o=1).broadcast_to([P, D])).then_inc(bv_loaded, 16)
        sp.dma_start(b_p[:, :], a["b_proj"].rearrange("(o n) -> o n", o=1).broadcast_to([P, D])).then_inc(bp_loaded, 16)
        sp.dma_start(wp_f[:, :, :], weight_rows(a["w_proj"])).then_inc(wp_loaded, 16)
        sp.sem_clear(range(min(s.num for s in used), max(s.num for s in used) + 1))

    @block.gpsimd
    def _(pool):
        norm.pool(pool)
        pool.memset(spread[:, :], 1.0).then_inc(mask_ready, 1)
        pool.wait_ge(mask_ready, 1)
        pool.affine_select(out=spread[:, :], in_=spread[:, :], compare_op=ALU.is_ge, fill=0.0, base=0,
                           pattern=[[-SHD, G]], channel_multiplier=1).then_inc(mask_ready, 1)
        pool.wait_ge(mask_ready, 2)
        pool.affine_select(out=spread[:, :], in_=spread[:, :], compare_op=ALU.is_ge, fill=0.0, base=SHD - 1,
                           pattern=[[SHD, G]], channel_multiplier=-1).then_inc(mask_ready, 1)
        pool.memset(vd[:, :, :, :, :], 0.0).then_inc(vd_cleared, 1)
        pool.wait_ge(mask_ready, 3)
        pool.wait_ge(qk_out, NQK)
        for u in range(TT * NG):
            t, g = divmod(u, NG)
            if u >= 2:
                pool.wait_ge(s_ready, u - 1)
            for e in range(2):
                k = qk[:, NG + g, (2 * t + e) * NQ:(2 * t + e + 1) * NQ]
                pool.tensor_tensor(kd[(2 * u + e) % 4][:, :, :], k.unsqueeze(1).broadcast_to([P, G, NQ]),
                                   spread[:, :].unsqueeze(2).broadcast_to([P, G, NQ]), ALU.mult).then_inc(kd_ready, 1)
            if u == 0:
                pool.wait_ge(norm.xn_ready, TT)
                pool.wait_ge(bp_loaded, 16)
                pool.tensor_tensor(x[:, :, :], x[:, :, :], b_p[:, :].unsqueeze(1).broadcast_to([P, TT, D]), ALU.add).then_inc(xb_ready, 1)

    @block.tensor
    def _(pe):
        turned.tensor(pe, xn, norm.xn_ready, ident)
        pe.wait_ge(b_loaded, 16)
        pe.transpose(bank[:, 4, 0:4], b_rows[:, :], ident[0:4, 0:4]).then_inc(bias_turned, 1)
        pe.wait_ge(turned.lo, TT // 2)
        pe.wait_ge(w_lo, 1)
        for job in range(NQK):
            c, n = divmod(job, 2)
            if job >= 3:
                pe.wait_ge(qk_out, job - 2)
            if job == 0:
                pe.wait_ge(bias_ready, 1)
            for k in range(KD):
                mm = mm3(pe, bank[:, 4 + job % 3, :], [x_[:, k, c * P:(c + 1) * P] for x_ in w],
                         [x_[:, k, n * 512:(n + 1) * 512] for x_ in turned.T], k == 0, k == KD - 1)
            mm.then_inc(qk_ready, 1)
        for b in range(B):
            if b >= 2:
                pe.wait_ge(v_out, b - 1)
            for e in range(2):
                for k in range(KD):
                    mm = mm3(pe, bank[e * NQ:(e + 1) * NQ, b % 2, 0:D], [x_[:, k, b * NQ:(b + 1) * NQ] for x_ in turned.T],
                             [x_[:, k, 2 * D:3 * D] for x_ in w], k == 0, k == KD - 1)
            mm.then_inc(v_ready, 1)

        def scores(u):
            t, g = divmod(u, NG)
            pe.wait_ge(kd_ready, 2 * u + 2)
            if u >= 2:
                pe.wait_ge(sub_ready, u - 1)
            for e in range(2):
                h = slice(e * NQ, (e + 1) * NQ)
                mm = pe.matmul(bank[h, S_BANK[u % 2], :], qk[:, g, (2 * t + e) * NQ:(2 * t + e + 1) * NQ],
                               kd[(2 * u + e) % 4][:, :, :].rearrange("p h k -> p (h k)"), start=True, stop=True)
            mm.then_inc(s_ready, 1)

        def values(u):
            t, g = divmod(u, NG)
            pe.wait_ge(p_ready, u + 1)
            if u >= 2:
                pe.wait_ge(pT_out, u - 1)
            for c in range(4):
                mm = pe.transpose(bank[:, T_BANK[u % 2], c * P:(c + 1) * P],
                                  pr[u % 2][:, 2 * c:2 * c + 2, :].rearrange("p h k -> p (h k)"), ident[:, :])
            mm.then_inc(pT_ready, 1)

        def outputs(u):
            t, g = divmod(u, NG)
            pe.wait_ge(pT_out, u + 1)
            if t >= 2:
                pe.wait_ge(o_out, t - 1)
            for e in range(2):
                h = slice(e * NQ, (e + 1) * NQ)
                for c in range(4):
                    pair = 4 * g + c
                    mm = pe.matmul(bank[h, O_BANK[t % 2], pair * 32:(pair + 1) * 32], prT[u % 2][:, c, h],
                                   vd[:, 2 * t + e, pair, :, :].rearrange("p e d -> p (e d)"), start=True, stop=True)
            mm.then_inc(o_ready, 1)

        pe.wait_ge(v_out, B)
        scores(0)
        for u in range(TT * NG):
            if u + 1 < TT * NG:
                scores(u + 1)
            values(u)
            if u:
                outputs(u - 1)
        outputs(TT * NG - 1)
        for t in range(TT):
            pe.wait_ge(o_out, t + 1)
            if t >= 2:
                pe.wait_ge(oT_lo, t - 1)
            for k in range(KD):
                mm = pe.transpose(bank[:, S_BANK[t % 2], k * P:(k + 1) * P], o_sb[:, t, k * P:(k + 1) * P], ident[:, :])
            mm.then_inc(oT_ready, 1)
        for t in range(TT):
            pe.wait_ge(oT_lo, t + 1)
            pe.wait_ge(w_lo, 2)
            if t >= 2:
                pe.wait_ge(y_added, t - 1)
            for k in range(KD):
                mm = mm3(pe, bank[:, 6 + t % 2, 0:D], [o[:, k, t * P:(t + 1) * P] for o in oT],
                         [x_[:, k, :] for x_ in wp], k == 0, k == KD - 1)
            mm.then_inc(y_ready, 1)

    @block.scalar
    def _(act):
        act.wait_ge(w_loaded, 16)
        split_hi(act, w[0][:, :, :], w_f[:, :, :], SW).then_inc(w_hi, 1)
        turned.scalar(act)
        act.wait_ge(bias_turned, 1)
        act.activation(b_cols[:, :], bank[:, 4, 0:4], ACT.Copy).then_inc(bias_ready, 1)
        act.wait_ge(bias_ready, 1)
        act.mul(b_cols[:, 0:NG], b_cols[:, 0:NG], SHD ** -0.5).then_inc(bias_ready, 1)
        act.wait_ge(bias_ready, 2)
        for job in range(NQK):
            c, n = divmod(job, 2)
            act.wait_ge(qk_ready, job + 1)
            scale = (SHD ** -0.5 if c < NG else 1.0) / (SA * SW)
            act.activation(qk[:, c, n * 512:(n + 1) * 512], bank[:, 4 + job % 3, :], ACT.Identity, bias=b_cols[:, c:c + 1],
                           scale=scale).then_inc(qk_out, 1)
        act.wait_ge(wp_loaded, 16)
        split_hi(act, wp[0][:, :, :], wp_f[:, :, :], SW).then_inc(w_hi, 1)
        for u in range(TT * NG):
            t, g = divmod(u, NG)
            act.wait_ge(sub_ready, u + 1)
            act.activation(pr[u % 2][:, :, :], pr[u % 2][:, :, :], ACT.Exp).then_inc(exp_ready, 1)
            act.wait_ge(pT_ready, u + 1)
            if u >= 2:
                act.wait_ge(o_ready, u - 1)
            act.activation(prT[u % 2][:, :, :].rearrange("p c q -> p (c q)"), bank[:, T_BANK[u % 2], :], ACT.Copy).then_inc(pT_out, 1)
            if u >= 2 and g == 0:
                act.wait_ge(o_ready, u)
                act.activation(o_sb[:, t - 1, :], bank[:, O_BANK[(t - 1) % 2], 0:D], ACT.Copy).then_inc(o_out, 1)
        act.wait_ge(o_ready, TT * NG)
        act.activation(o_sb[:, TT - 1, :], bank[:, O_BANK[(TT - 1) % 2], 0:D], ACT.Copy).then_inc(o_out, 1)
        for t in range(TT):
            act.wait_ge(oT_ready, t + 1)
            split_hi(act, oT[0][:, :, t * P:(t + 1) * P], bank[:, S_BANK[t % 2], 0:D].rearrange("p (k q) -> p k q", k=KD), SA).then_inc(oT_hi, 1)

    @block.vector
    def _(dve):
        norm.vector(dve, xn, x)
        dve.wait_ge(w_hi, 1)
        split_lo(dve, w[1][:, :, :], w_f[:, :, :], w[0][:, :, :], SW).then_inc(w_lo, 1)
        turned.vector(dve)
        dve.wait_ge(vd_cleared, 1)
        dve.wait_ge(bv_loaded, 16)
        for b in range(B):
            dve.wait_ge(v_ready, b + 1)
            for e in range(2):
                h = slice(e * NQ, (e + 1) * NQ)
                src = bank[h, b % 2, 0:D].rearrange("p (c e d) -> p c e d", e=2, d=SHD)[:, :, e, :]
                bias = b_v[h, :].rearrange("p (c e d) -> p c e d", e=2, d=SHD)[:, :, e, :]
                ins = dve.scalar_tensor_tensor(out=vd[h, b, :, e, :], in0=src, scalar=1 / (SA * SW), in1=bias,
                                               op0=ALU.mult, op1=ALU.add)
            ins.then_inc(v_out, 1)
        dve.wait_ge(w_hi, 2)
        split_lo(dve, wp[1][:, :, :], wp_f[:, :, :], wp[0][:, :, :], SW).then_inc(w_lo, 1)

        def shift(u):
            s = bank[:, S_BANK[u % 2], :].rearrange("p (h k) -> p h k", h=G)
            dve.wait_ge(s_ready, u + 1)
            dve.tensor_reduce(top[:, u % 2, :], s, X, ALU.max).then_inc(top_ready, 1)
            dve.wait_ge(top_ready, u + 1)
            if u >= 2:
                dve.wait_ge(pT_ready, u - 1)
            dve.tensor_tensor(pr[u % 2][:, :, :], s, top[:, u % 2, :].unsqueeze(2).broadcast_to([P, G, NQ]), ALU.subtract).then_inc(sub_ready, 1)

        def scale(u):
            dve.wait_ge(exp_ready, u + 1)
            dve.tensor_reduce(total[:, u % 2, :], pr[u % 2][:, :, :], X, ALU.add).then_inc(sum_ready, 1)
            dve.wait_ge(sum_ready, u + 1)
            dve.reciprocal(total[:, u % 2, :], total[:, u % 2, :]).then_inc(rec_ready, 1)
            dve.wait_ge(rec_ready, u + 1)
            dve.tensor_tensor(pr[u % 2][:, :, :], pr[u % 2][:, :, :], total[:, u % 2, :].unsqueeze(2).broadcast_to([P, G, NQ]),
                              ALU.mult).then_inc(p_ready, 1)

        shift(0)
        for u in range(TT * NG):
            if u + 1 < TT * NG:
                shift(u + 1)
            scale(u)
        for t in range(TT):
            dve.wait_ge(oT_hi, t + 1)
            io = [o[:, :, t * P:(t + 1) * P] for o in oT]
            split_lo(dve, io[1], bank[:, S_BANK[t % 2], 0:D].rearrange("p (k q) -> p k q", k=KD), io[0], SA).then_inc(oT_lo, 1)
        dve.wait_ge(xb_ready, 1)
        for t in range(TT):
            dve.wait_ge(y_ready, t + 1)
            dve.scalar_tensor_tensor(out=x[:, t, :], in0=bank[:, 6 + t % 2, 0:D], scalar=1 / (SA * SW), in1=x[:, t, :],
                                     op0=ALU.mult, op1=ALU.add).then_inc(y_added, 1)


def experts(nc, m, a, x, out, ident):
    E, HID, SHID = 8, 256, 512
    KH, KS = HID // P, SHID // P
    HALF = T // 2
    NU = 2 * E
    xn = m.sb("xn_c", [P, TT, D])
    gate_rows = m.sb("gate_rows", [E, D])
    gate = [m.sb(f"gate_{s}", [P, KD, E], F16) for s in "hl"]
    bias_rows = m.sb("bias_rows", [3 * E * KH, P])
    bias = m.sb("bias", [P, 3, E, KH])
    b1_now = [m.sb(f"b1_now{i}", [P, KH]) for i in range(2)]
    select = m.sb("select", [E, E, P], F16)
    before = m.sb("before", [P, E, E])
    gs = m.sb("gate_scores", [P, TT, E])
    gmax, gsum = m.sb("gate_max", [P, TT]), m.sb("gate_sum", [P, TT])
    above = m.sb("above", [P, TT, E, E])
    equal = m.sb("equal", [P, TT, E, E])
    rank = m.sb("rank", [P, TT, E])
    mask = m.sb("mask", [P, TT, E])
    wT = [m.sb(f"gate_T{s}", [E, T], F16) for s in "hl"]
    mT = m.sb("mask_T", [E, T], F16)
    WB = m.sb("weight_all", [P, E, T])
    MB = m.sb("mask_all", [P, E, T], F16)
    wf = [m.sb(f"expert_f{i}", [P, 3, KD, HID]) for i in range(2)]
    we = [[m.sb(f"expert_{s}{i}", [P, 3, KD, HID], F16) for s in "hl"] for i in range(2)]
    sf = m.sb("shared_f", [P, 3, 1024])
    ws = [m.sb(f"shared_w_{s}", [P, 3, 1024], F16) for s in "hl"]
    ta = [m.sb(f"ta{i}", [P, KH, HALF]) for i in range(2)]
    tb = [m.sb(f"tb{i}", [P, KH, HALF]) for i in range(2)]
    hT = [[m.sb(f"hT_{s}{i}", [P, KH, HALF], F16) for s in "hl"] for i in range(2)]
    acc = m.sb("acc", [P, KD, T])
    sg = m.sb("shared_prod", [P, KS, HALF])
    sh = [m.sb(f"shared_prod_{s}", [P, KS, HALF], F16) for s in "hl"]
    bank = m.ps("ffn_bank", [P, 8, 512])

    norm = Norm(m, "norm_c")
    turned = TurnedTokens(m, "xn_c", bank)
    gate_loaded, bias_loaded, shared_loaded = m.sem("gate_loaded"), m.sem("bias_loaded"), m.sem("shared_loaded")
    wf_loaded = [m.sem(f"expert_loaded{i}") for i in range(2)]
    consts = m.sem("select_before")
    rows_turned, bias_out, gate_hi, gate_lo = m.sem("rows_turned"), m.sem("bias_out"), m.sem("gate_hi"), m.sem("gate_lo")
    logits_ready, shifted, gexp_ready = m.sem("logits_ready"), m.sem("logits_shifted"), m.sem("gate_exp_ready")
    gstep = m.sem("gate_step")
    gates_ready, gT_ready, gT_hi, gT_lo, mT_out = m.sem("gates_ready"), m.sem("gate_T_ready"), m.sem("gate_T_hi"), m.sem("gate_T_lo"), m.sem("mask_T_out")
    wb_ready, mb_ready, wb_out, mb_out = m.sem("wb_ready"), m.sem("mb_ready"), m.sem("wb_out"), m.sem("mb_out")
    ws_turned, ws_hi, ws_lo = m.sem("shared_turned"), m.sem("shared_w_hi"), m.sem("shared_w_lo")
    sg_ready, sg_out, su_ready, su_out = m.sem("sg_ready"), m.sem("sg_out"), m.sem("su_ready"), m.sem("su_out")
    sh_hi, sh_lo, sz_ready, sz_out = m.sem("shared_h_hi"), m.sem("shared_h_lo"), m.sem("sz_ready"), m.sem("sz_out")
    b1_ready = m.sem("b1_now_ready")
    we_turned, we_hi, we_lo = m.sem("expert_turned"), m.sem("expert_w_hi"), m.sem("expert_w_lo")
    a_ready, ta_ready, h_ready, h_hi, h_lo = m.sem("a_ready"), m.sem("ta_ready"), m.sem("h_ready"), m.sem("h_hi"), m.sem("h_lo")
    b_ready, tb_ready, x3_ready = m.sem("b_ready"), m.sem("tb_ready"), m.sem("x3_ready")
    y_ready, yt_ready, acc_ready = m.sem("ffn_y_ready"), m.sem("yt_ready"), m.sem("acc_ready")
    fin_ready, fin_added, stored = m.sem("fin_ready"), m.sem("fin_added"), m.sem("out_stored")
    block = m.ctx.enter_context(nc.Block())
    names = ("w1", "w3", "w2")
    NT2 = 2 * E

    def units(eng, body):
        def pair(i, e, last):
            for v in range(4):
                body(i * 4 + v, e + v // 2, v % 2, v // 2, last and v == 3, last)
        with eng.Fori(0, E // 2 - 1) as i:
            pair(i, i * 2, False)
        pair(E // 2 - 1, E - 2, True)

    def next_of(e, half, parity):
        return (e, 1, parity) if half == 0 else (e + 1, 0, 1 - parity)

    @block.sync
    def _(sp):
        sp.dma_start(gate_rows[:, :], a["gate_w"]).then_inc(gate_loaded, 16)
        for n, b in enumerate(("b1", "b2", "b3")):
            sp.dma_start(bias_rows[n * E * KH:(n + 1) * E * KH, :], a[b].rearrange("e (k p) -> (e k) p", p=P)).then_inc(bias_loaded, 16)
        sp.dma_start(sf[:, 0, :].rearrange("p (j d) -> p j d", j=KS), a["sw1"].rearrange("(j p) d -> p j d", p=P)).then_inc(shared_loaded, 16)
        sp.dma_start(sf[:, 1, :].rearrange("p (j d) -> p j d", j=KS), a["sw2"].rearrange("(j p) d -> p j d", p=P)).then_inc(shared_loaded, 16)
        sp.dma_start(sf[:, 2, :].rearrange("p (k i) -> p k i", k=KD), a["sw3"].rearrange("(k p) i -> p k i", p=P)).then_inc(shared_loaded, 16)

        def load_expert(at, parity):
            for n, w in enumerate(names):
                flat = a[w].rearrange("e h d -> (e h d)")[bass.ds(at, HID * D)]
                sp.dma_start(wf[parity][:, n, :, :], flat.rearrange("(k p d) -> p k d", k=KH, p=P)).then_inc(wf_loaded[parity], 16)

        load_expert(0, 0)
        load_expert(HID * D, 1)

        def pair(i, last):
            for parity in range(2):
                if not last:
                    at = i * (2 * HID * D) + (parity + 2) * HID * D
                    at = at if isinstance(i, int) else sp.snap(at)
                    sp.wait_ge(we_lo, i * 6 + (3 * parity + 3))
                    load_expert(at, parity)

        with sp.Fori(0, E // 2 - 1) as i:
            pair(i, False)
        for t in range(TT):
            sp.wait_ge(fin_added, t + 1)
            sp.dma_start(out.rearrange("(t b) q d -> (b q) t d", b=2)[:, t, :], xn[:, t, :]).then_inc(stored, 16)
        sp.wait_ge(stored, 16 * TT)

    @block.gpsimd
    def _(pool):
        norm.pool(pool)
        pool.memset(select[:, :, :], 0.0).then_inc(consts, 1)
        pool.wait_ge(consts, 1)
        pool.affine_select(out=select[:, :, :], in_=select[:, :, :], compare_op=ALU.not_equal, fill=1.0, base=0,
                           pattern=[[-1, E], [0, P]], channel_multiplier=1).then_inc(consts, 1)
        pool.wait_ge(consts, 2)
        pool.memset(before[:, :, :], 1.0).then_inc(consts, 1)
        pool.wait_ge(consts, 3)
        pool.affine_select(out=before[:, :, :], in_=before[:, :, :], compare_op=ALU.is_gt, fill=0.0, base=0,
                           pattern=[[1, E], [-1, E]], channel_multiplier=0).then_inc(consts, 1)
        pool.wait_ge(sz_out, 2 * KD)

        def body(u, e, half, parity, very_last, last):
            at = acc[:, :, half * HALF:(half + 1) * HALF]
            pool.wait_ge(yt_ready, u + 1)
            pool.tensor_tensor(at, at, tb[half][:, :, :], ALU.add).then_inc(acc_ready, 1)

        units(pool, body)

    def shared_turn(job):
        n, half = divmod(job, 2)
        if n < 2:
            src = [sf[:, n, j * D + half * P:j * D + (half + 1) * P] for j in range(KS)]
        else:
            src = [sf[:, 2, k * SHID + j * P:k * SHID + (j + 1) * P] for j in (2 * half, 2 * half + 1) for k in range(KD)]
        return src, [w[:, n, half * 512:(half + 1) * 512] for w in ws]

    @block.tensor
    def _(pe):
        pe.wait_ge(bias_loaded, 48)
        pe.wait_ge(gate_loaded, 16)
        pe.transpose(bank[:, 4, 0:3 * E * KH], bias_rows[:, :], ident[0:3 * E * KH, 0:3 * E * KH])
        for k in range(KD):
            mm = pe.transpose(bank[:, 4, 64 + k * E:64 + (k + 1) * E], gate_rows[:, k * P:(k + 1) * P], ident[0:E, 0:E])
        mm.then_inc(rows_turned, 1)
        pe.wait_ge(shared_loaded, 48)
        for job in range(6):
            if job >= 3:
                pe.wait_ge(ws_lo, job - 2)
            for q, src in enumerate(shared_turn(job)[0]):
                mm = pe.transpose(bank[:, 5 + job % 3, q * P:(q + 1) * P], src, ident[:, :])
            mm.then_inc(ws_turned, 1)
        turned.tensor(pe, xn, norm.xn_ready, ident)
        pe.wait_ge(turned.lo, TT // 2)
        pe.wait_ge(gate_lo, 1)
        pe.wait_ge(bias_out, 2)
        for t in range(TT):
            for k in range(KD):
                mm = mm3(pe, bank[:, 4, t * E:(t + 1) * E], [x_[:, k, t * P:(t + 1) * P] for x_ in turned.T],
                         [g[:, k, :] for g in gate], k == 0, k == KD - 1)
        mm.then_inc(logits_ready, 1)
        pe.wait_ge(ws_lo, 6)
        for n in range(2):
            rhs = [[x_[:, k, n * HALF:(n + 1) * HALF] for x_ in turned.T] for k in range(KD)]
            for j in range(KS):
                at = n * KS + j
                if at >= 2:
                    pe.wait_ge(sg_out, at - 1)
                for k in range(KD):
                    mm = mm3(pe, bank[:, at % 2, :], [w[:, 0, k * SHID + j * P:k * SHID + (j + 1) * P] for w in ws], rhs[k],
                             k == 0, k == KD - 1)
                mm.then_inc(sg_ready, 1)
                if at >= 2:
                    pe.wait_ge(su_out, at - 1)
                for k in range(KD):
                    mm = mm3(pe, bank[:, 2 + at % 2, :], [w[:, 1, k * SHID + j * P:k * SHID + (j + 1) * P] for w in ws], rhs[k],
                             k == 0, k == KD - 1)
                mm.then_inc(su_ready, 1)
            for k in range(KD):
                if k == 0:
                    pe.wait_ge(sh_lo, KS * (n + 1))
                if n:
                    pe.wait_ge(sz_out, k + 1)
                for j in range(KS):
                    mm = mm3(pe, bank[:, 5 + k, :], [w[:, 2, j * D + k * P:j * D + (k + 1) * P] for w in ws],
                             [h[:, j, :] for h in sh], j == 0, j == KS - 1)
                mm.then_inc(sz_ready, 1)
        pe.wait_ge(gates_ready, 1)
        pe.wait_ge(sz_out, 2 * KD)
        for n, (src, at) in enumerate(((gs, 6), (mask, 4))):
            for t in range(TT):
                mm = pe.transpose(bank[0:E, at + t // 4, (t % 4) * P:(t % 4 + 1) * P], src[:, t, :], ident[:, :])
            mm.then_inc(gT_ready, 1)
        pe.wait_ge(gT_lo, 1)
        pe.wait_ge(mT_out, 1)
        pe.wait_ge(su_out, 2 * KS)
        for job in range(NT2):
            e, n = divmod(job, 2)
            if job >= 2:
                pe.wait_ge(wb_out, job - 1)
                pe.wait_ge(mb_out, job - 1)
            at = slice(n * HALF, (n + 1) * HALF)
            pe.matmul(bank[:, job % 2, :], select[:, e, :], wT[0][:, at], start=True, stop=False)
            pe.matmul(bank[:, job % 2, :], select[:, e, :], wT[1][:, at], start=False, stop=True).then_inc(wb_ready, 1)
            pe.matmul(bank[:, 2 + job % 2, :], select[:, e, :], mT[:, at], start=True, stop=True).then_inc(mb_ready, 1)

        def first_two(u, e, half, parity):
            for n, (at, free, ready) in enumerate(((0, ta_ready, a_ready), (2, tb_ready, b_ready))):
                if not isinstance(u, int) or u > 0:
                    pe.wait_ge(free, u)
                for c in range(KH):
                    for k in range(KD):
                        mm = mm3(pe, bank[:, at + c, :], [w[:, n, k, c * P:(c + 1) * P] for w in we[parity]],
                                 [x_[:, k, half * HALF:(half + 1) * HALF] for x_ in turned.T], k == 0, k == KD - 1)
                mm.then_inc(ready, 1)

        def last_one(u, half, parity):
            pe.wait_ge(h_lo, u + 1)
            if not isinstance(u, int) or u > 0:
                pe.wait_ge(yt_ready, u)
            for c in range(KD):
                for k in range(KH):
                    mm = mm3(pe, bank[:, 6 + c, :], [w[:, 2, k, c * P:(c + 1) * P] for w in we[parity]],
                             [h[:, k, :] for h in hT[half]], k == 0, k == KH - 1)
            mm.then_inc(y_ready, 1)

        def turn_weights(e, parity, loads):
            pe.wait_ge(wf_loaded[parity], loads)
            for n in range(3):
                if not (isinstance(e, int) and e == 0 and n < 2):
                    pe.wait_ge(we_lo, e * 3 + (n - 1))
                for r in range(KD):
                    for c in range(2):
                        mm = pe.transpose(bank[:, 4 + (3 * parity + n) % 2, (2 * r + c) * P:(2 * r + c + 1) * P],
                                          wf[parity][:, n, c, r * P:(r + 1) * P], ident[:, :])
                mm.then_inc(we_turned, 1)

        turn_weights(0, 0, 48)
        pe.wait_ge(wb_out, NT2)
        pe.wait_ge(mb_out, NT2)
        pe.wait_ge(we_lo, 3)
        first_two(0, 0, 0, 0)

        def body(u, e, half, parity, very_last, last):
            if half == 0 and not (last and parity == 1):
                turn_weights(e + 1, 1 - parity, e * 24 + (72 if parity else 48))
            if not very_last:
                ne, nhalf, nparity = next_of(e, half, parity)
                if nhalf == 0:
                    pe.wait_ge(we_lo, (e + 2) * 3)
                first_two(u + 1, ne, nhalf, nparity)
            last_one(u, half, parity)

        units(pe, body)
        pe.wait_ge(acc_ready, NU)
        for t in range(TT):
            for k in range(KD):
                mm = pe.transpose(bank[:, t, k * P:(k + 1) * P], acc[:, k, t * P:(t + 1) * P], ident[:, :])
            mm.then_inc(fin_ready, 1)

    @block.scalar
    def _(act):
        act.wait_ge(rows_turned, 1)
        act.activation(bias[:, :, :, :].rearrange("p n e k -> p (n e k)"), bank[:, 4, 0:3 * E * KH], ACT.Copy).then_inc(bias_out, 1)
        act.wait_ge(bias_out, 1)
        act.mul(bias[:, 1, :, :], bias[:, 1, :, :], SA * SW).then_inc(bias_out, 1)
        split_hi(act, gate[0][:, :, :], bank[:, 4, 64:64 + KD * E].rearrange("p (k e) -> p k e", k=KD), SW).then_inc(gate_hi, 1)
        for job in range(6):
            act.wait_ge(ws_turned, job + 1)
            split_hi(act, shared_turn(job)[1][0], bank[:, 5 + job % 3, :], SW).then_inc(ws_hi, 1)
        turned.scalar(act)
        act.wait_ge(shifted, 1)
        act.activation(gs[:, :, :], gs[:, :, :], ACT.Exp, scale=1 / (SA * SW)).then_inc(gexp_ready, 1)
        for n in range(2):
            for j in range(KS):
                at = n * KS + j
                act.wait_ge(sg_ready, at + 1)
                if n and j == 0:
                    act.wait_ge(sh_lo, KS)
                act.activation(sg[:, j, :], bank[:, at % 2, :], ACT.Silu, scale=1 / (SA * SW)).then_inc(sg_out, 1)
                act.wait_ge(su_out, at + 1)
                if n and j == 0:
                    act.wait_ge(sz_ready, KD)
                split_hi(act, sh[0][:, j, :], sg[:, j, :], SA).then_inc(sh_hi, 1)
            for k in range(KD):
                act.wait_ge(sz_ready, n * KD + k + 1)
                act.activation(acc[:, k, n * HALF:(n + 1) * HALF], bank[:, 5 + k, :], ACT.Copy, scale=1 / (SA * SW)).then_inc(sz_out, 1)
        act.wait_ge(gT_ready, 1)
        split_hi(act, wT[0][:, :], bank[0:E, 6:8, :].rearrange("p a b -> p (a b)"), SP).then_inc(gT_hi, 1)
        act.wait_ge(gT_ready, 2)
        act.activation(mT[:, :], bank[0:E, 4:6, :].rearrange("p a b -> p (a b)"), ACT.Copy).then_inc(mT_out, 1)
        for job in range(NT2):
            e, n = divmod(job, 2)
            act.wait_ge(wb_ready, job + 1)
            act.activation(WB[:, e, n * HALF:(n + 1) * HALF], bank[:, job % 2, :], ACT.Copy, scale=1 / (SP * SA * SW)).then_inc(wb_out, 1)

        def weights_hi(e, parity):
            src = bias[:, 0, e, :] if isinstance(e, int) else bias[:, 0, bass.ds(e, 1), :].squeeze(1)
            act.activation(b1_now[parity][:, :], src, ACT.Copy).then_inc(b1_ready, 1)
            for n in range(3):
                act.wait_ge(we_turned, e * 3 + (n + 1))
                split_hi(act, we[parity][0][:, n, :, :], bank[:, 4 + (3 * parity + n) % 2, :].rearrange("p (k c) -> p k c", k=KD), SW).then_inc(we_hi, 1)

        def hidden(u, e, half, parity):
            if half == 0:
                act.wait_ge(b1_ready, e + 1)
            act.wait_ge(ta_ready, u + 1)
            for k in range(KH):
                ins = act.activation(ta[half][:, k, :], ta[half][:, k, :], ACT.Silu, bias=b1_now[parity][:, k:k + 1])
            ins.then_inc(h_ready, 1)
            act.wait_ge(h_ready, u + 1)
            split_hi(act, hT[half][0][:, :, :], ta[half][:, :, :], SA).then_inc(h_hi, 1)

        weights_hi(0, 0)
        hidden(0, 0, 0, 0)

        def body(u, e, half, parity, very_last, last):
            if half == 0 and not (last and parity == 1):
                weights_hi(e + 1, 1 - parity)
            if not very_last:
                hidden(u + 1, *next_of(e, half, parity))

        units(act, body)

    @block.vector
    def _(dve):
        norm.vector(dve, xn, x)
        dve.wait_ge(gate_hi, 1)
        split_lo(dve, gate[1][:, :, :], bank[:, 4, 64:64 + KD * E].rearrange("p (k e) -> p k e", k=KD), gate[0][:, :, :], SW).then_inc(gate_lo, 1)
        for job in range(6):
            dve.wait_ge(ws_hi, job + 1)
            dst = shared_turn(job)[1]
            split_lo(dve, dst[1], bank[:, 5 + job % 3, :], dst[0], SW).then_inc(ws_lo, 1)
        turned.vector(dve)
        logits = bank[:, 4, 0:TT * E].rearrange("p (t e) -> p t e", t=TT)
        by_token = lambda v: v.unsqueeze(2).broadcast_to([P, TT, E])
        dve.wait_ge(logits_ready, 1)
        dve.tensor_reduce(gmax[:, :], logits, X, ALU.max).then_inc(gstep, 1)
        dve.wait_ge(gstep, 1)
        dve.tensor_tensor(gs[:, :, :], logits, by_token(gmax[:, :]), ALU.subtract).then_inc(shifted, 1)
        dve.wait_ge(gexp_ready, 1)
        dve.tensor_reduce(gsum[:, :], gs[:, :, :], X, ALU.add).then_inc(gstep, 1)
        dve.wait_ge(gstep, 2)
        dve.reciprocal(gsum[:, :], gsum[:, :]).then_inc(gstep, 1)
        dve.wait_ge(gstep, 3)
        dve.tensor_tensor(gs[:, :, :], gs[:, :, :], by_token(gsum[:, :]), ALU.mult).then_inc(gstep, 1)
        dve.wait_ge(gstep, 4)
        dve.wait_ge(consts, 4)
        for t in range(TT):
            own = gs[:, t, :].unsqueeze(2).broadcast_to([P, E, E])
            other = gs[:, t, :].unsqueeze(1).broadcast_to([P, E, E])
            dve.tensor_tensor(above[:, t, :, :], other, own, ALU.is_gt)
            dve.tensor_tensor(equal[:, t, :, :], other, own, ALU.is_equal).then_inc(gstep, 1)
        dve.wait_ge(gstep, 4 + TT)
        dve.tensor_tensor(equal[:, :, :, :].rearrange("p t e j -> p t (e j)"), equal[:, :, :, :].rearrange("p t e j -> p t (e j)"),
                          before[:, :, :].rearrange("p e j -> p (e j)").unsqueeze(1).broadcast_to([P, TT, E * E]), ALU.mult).then_inc(gstep, 1)
        dve.wait_ge(gstep, 5 + TT)
        dve.tensor_tensor(above[:, :, :, :].rearrange("p t e j -> p (t e j)"), above[:, :, :, :].rearrange("p t e j -> p (t e j)"),
                          equal[:, :, :, :].rearrange("p t e j -> p (t e j)"), ALU.add).then_inc(gstep, 1)
        dve.wait_ge(gstep, 6 + TT)
        dve.tensor_reduce(rank[:, :, :], above[:, :, :, :], X, ALU.add).then_inc(gstep, 1)
        dve.wait_ge(gstep, 7 + TT)
        dve.tensor_scalar(mask[:, :, :], rank[:, :, :], 1.5, None, ALU.is_lt).then_inc(gstep, 1)
        dve.wait_ge(gstep, 8 + TT)
        dve.tensor_tensor(gs[:, :, :], gs[:, :, :], mask[:, :, :], ALU.mult).then_inc(gates_ready, 1)
        for n in range(2):
            for j in range(KS):
                at = n * KS + j
                dve.wait_ge(su_ready, at + 1)
                dve.wait_ge(sg_out, at + 1)
                dve.scalar_tensor_tensor(out=sg[:, j, :], in0=bank[:, 2 + at % 2, :], scalar=1 / (SA * SW), in1=sg[:, j, :],
                                         op0=ALU.mult, op1=ALU.mult).then_inc(su_out, 1)
                dve.wait_ge(sh_hi, at + 1)
                split_lo(dve, sh[1][:, j, :], sg[:, j, :], sh[0][:, j, :], SA).then_inc(sh_lo, 1)
        dve.wait_ge(gT_hi, 1)
        split_lo(dve, wT[1][:, :], bank[0:E, 6:8, :].rearrange("p a b -> p (a b)"), wT[0][:, :], SP).then_inc(gT_lo, 1)
        for job in range(NT2):
            e, n = divmod(job, 2)
            dve.wait_ge(mb_ready, job + 1)
            dve.tensor_scalar(MB[:, e, n * HALF:(n + 1) * HALF], bank[:, 2 + job % 2, :], 1 / (SA * SW), None, ALU.mult).then_inc(mb_out, 1)

        def weights_lo(e, parity):
            for n in range(3):
                dve.wait_ge(we_hi, e * 3 + (n + 1))
                split_lo(dve, we[parity][1][:, n, :, :], bank[:, 4 + (3 * parity + n) % 2, :].rearrange("p (k c) -> p k c", k=KD),
                         we[parity][0][:, n, :, :], SW).then_inc(we_lo, 1)

        def at_tokens(tile, e, half):
            t = tile[:, e, half * HALF:(half + 1) * HALF].unsqueeze(1) if isinstance(e, int) else \
                tile[:, bass.ds(e, 1), half * HALF:(half + 1) * HALF]
            return t.broadcast_to([P, KH, HALF])

        def column(n, e, k):
            return bias[:, n, e, k:k + 1] if isinstance(e, int) else bias[:, n, bass.ds(e, 1), k]

        def weigh(u, e, half, first):
            dve.wait_ge(a_ready, u + 1)
            dve.tensor_tensor(ta[half][:, :, :], bank[:, 0:2, :], at_tokens(WB, e, half), ALU.mult).then_inc(ta_ready, 1)
            dve.wait_ge(b_ready, u + 1)
            if not first:
                dve.wait_ge(acc_ready, u - 1)
            dve.tensor_tensor(tb[half][:, :, :], bank[:, 2:4, :], at_tokens(WB, e, half), ALU.mult).then_inc(tb_ready, 1)
            dve.wait_ge(tb_ready, u + 1)
            for k in range(KH):
                m_at = MB[:, e, half * HALF:(half + 1) * HALF] if isinstance(e, int) else \
                    MB[:, bass.ds(e, 1), half * HALF:(half + 1) * HALF].squeeze(1)
                ins = dve.scalar_tensor_tensor(out=tb[half][:, k, :], in0=tb[half][:, k, :], scalar=column(2, e, k), in1=m_at,
                                               op0=ALU.add, op1=ALU.mult)
            ins.then_inc(x3_ready, 1)
            dve.wait_ge(h_hi, u + 1)
            split_lo(dve, hT[half][1][:, :, :], ta[half][:, :, :], hT[half][0][:, :, :], SA).then_inc(h_lo, 1)

        weights_lo(0, 0)
        weigh(0, 0, 0, True)

        def body(u, e, half, parity, very_last, last):
            if half == 0 and not (last and parity == 1):
                weights_lo(e + 1, 1 - parity)
            if not very_last:
                ne, nhalf, _ = next_of(e, half, parity)
                weigh(u + 1, ne, nhalf, False)
            dve.wait_ge(y_ready, u + 1)
            dve.wait_ge(x3_ready, u + 1)
            for k in range(KD):
                ins = dve.scalar_tensor_tensor(out=tb[half][:, k, :], in0=bank[:, 6 + k, :], scalar=column(1, e, k),
                                               in1=tb[half][:, k, :], op0=ALU.add, op1=ALU.mult)
            ins.then_inc(yt_ready, 1)

        units(dve, body)
        for t in range(TT):
            dve.wait_ge(fin_ready, t + 1)
            dve.tensor_tensor(xn[:, t, :], bank[:, t, 0:D], x[:, t, :], ALU.add).then_inc(fin_added, 1)


INPUTS = {"x": "x", "ctx": "ctx_1024", "Wq": "L0_xattn_Wq", "Wk": "L0_xattn_Wk", "Wv": "L0_xattn_Wv",
          "Wk_ip": "L0_xattn_Wk_ip", "Wv_ip": "L0_xattn_Wv_ip", "Wk_ap": "L0_xattn_Wk_ap", "Wv_ap": "L0_xattn_Wv_ap",
          "Wo": "L0_xattn_Wo", "bo": "L0_xattn_bo", "rel_k": "L0_xattn_rel_k", "rel_v": "L0_xattn_rel_v",
          "alpha": "L0_xattn_alpha", "beta": "L0_xattn_beta", "w_attn": "L0_attn_w_attn", "b_attn": "L0_attn_b_attn",
          "w_proj": "L0_attn_w_proj", "b_proj": "L0_attn_b_proj", "gate_w": "L0_ffn_gate_w", "w1": "L0_ffn_w1",
          "b1": "L0_ffn_b1", "w2": "L0_ffn_w2", "b2": "L0_ffn_b2", "w3": "L0_ffn_w3", "b3": "L0_ffn_b3",
          "sw1": "L0_ffn_sw1", "sw2": "L0_ffn_sw2", "sw3": "L0_ffn_sw3"}


def perceiver_layer(nc, a, out):
    scr = {
        "kt": nc.dram_tensor("kt_scratch", [B, P, 2 * PAIRS * TI], F16).ap(),
        "v": nc.dram_tensor("v_scratch", [B * TI, 2 * INNER], F16).ap(),
        "R": nc.dram_tensor("rel_scratch", [B, TXT, PAIRS * 2 * NQ], F32).ap(),
        "relv": nc.dram_tensor("relv_scratch", [EXT, HD], F32).ap(),
        "pt": nc.dram_tensor("prob_scratch", [B, TXT, 2, PAIRS * 2 * NQ], F16).ap(),
    }
    with ExitStack() as whole:
        m = Mem(nc, whole)
        ident = m.sb("ident", [P, P])
        x = m.sb("x_res", [P, TT, D])

        used = []

        def phase(f, *args):
            with ExitStack() as ctx:
                m = Mem(nc, ctx)
                f(nc, m, *args)
                used.extend(m.sems)

        with ExitStack() as attending:
            keep = Mem(nc, attending)
            qT = [keep.sb(f"qT_{s}", [P, PAIRS, T], F16) for s in "hl"]
            phase(project, a, scr, qT, ident)
            phase(relative_scores, a, scr, qT, ident)
            OT = keep.sb("OT", [P, PAIRS, T])
            with ExitStack() as streaming:
                s = Mem(nc, streaming)
                wkT = [s.sb(f"wkT_{n}", [P, PAIRS, D], F16) for n in "hl"]
                wv = [s.sb(f"wv_{n}", [P, KD, INNER], F16) for n in "hl"]
                gains = s.sb("gains", [P, 2])
                phase(audio_weights, a, wkT, wv, gains, ident)
                phase(cross_attention, a, scr, qT, OT, wkT, wv, gains, ident)
            phase(relative_values, scr, OT, ident)
            phase(cross_output, a, OT, x)
        phase(self_attention, a, x, ident, used)
        phase(experts, a, x, out, ident)


def kernel(**inputs):
    import concourse.bacc as bacc
    from concourse.bass_utils import run_bass_kernel_spmd

    nc = bacc.Bacc("TRN2", target_bir_lowering=False, num_devices=1)
    arrays, a = {}, {}
    for name, key in INPUTS.items():
        v = np.ascontiguousarray(inputs[key])
        v = v.reshape(1) if v.ndim == 0 else v
        arrays["in_" + name] = v
        a[name] = nc.dram_tensor("in_" + name, v.shape, mybir.dt.from_np(v.dtype), kind="ExternalInput").ap()
    out = nc.dram_tensor("out_x", [B, NQ, D], F32, kind="ExternalOutput").ap()
    perceiver_layer(nc, a, out)
    r = run_bass_kernel_spmd(nc, [arrays], core_ids=[0])
    return r.results[0]["out_x"]
```

```python
from contextlib import ExitStack

import numpy as np
import concourse.bass as bass
from concourse import mybir
from concourse.alu_op_type import AluOpType as ALU

F32 = mybir.dt.float32
F16 = mybir.dt.float16
ACT = mybir.ActivationFunctionType
X = mybir.AxisListType.X

P = 128
B, NQ, D = 16, 64, 256
T = B * NQ
TT = T // P
KD = D // P
H, HD = 16, 64
INNER = H * HD
PAIRS = H // 2
TXT, IMG, CTX = 77, 16, 1601
TI = TXT + IMG
AUD = CTX - TI
NCH = -(-AUD // P)
TAIL = AUD - (NCH - 1) * P
SB = 3
MAXREL = 16
NREL = 2 * MAXREL + 1
EXT = NQ + TXT - 1
REL0 = NQ - 1 - MAXREL
SCALE = HD ** -0.5
SA, SW, SP = 16.0, 256.0, 4096.0
EPS = 1e-5


def mm3(pe, out, lhs, rhs, first=True, last=True):
    (lh, ll), (rh, rl) = lhs, rhs
    pe.matmul(out, lh, rh, start=first, stop=False)
    pe.matmul(out, lh, rl, start=False, stop=False)
    return pe.matmul(out, ll, rh, start=False, stop=last)


def split_hi(act, hi, src, scale):
    return act.activation(hi, src, ACT.Copy, scale=scale)


def split_lo(dve, lo, src, hi, scale):
    return dve.scalar_tensor_tensor(out=lo, in0=src, scalar=scale, in1=hi, op0=ALU.mult, op1=ALU.subtract)


class Mem:

    def __init__(self, nc, ctx):
        self.nc, self.ctx, self.sems = nc, ctx, []

    def sb(self, name, shape, dt=F32):
        return self.ctx.enter_context(self.nc.sbuf_tensor(name, shape, dt))

    def ps(self, name, shape, dt=F32):
        return self.ctx.enter_context(self.nc.psum_tensor(name, shape, dt))

    def sem(self, name):
        handle = self.ctx.enter_context(self.nc.semaphore(name))
        self.sems.append(handle)
        return handle


def make_identity(pool, ident, made):
    pool.memset(ident, 0.0).then_inc(made, 1)
    pool.wait_ge(made, 1)
    pool.affine_select(out=ident, in_=ident, compare_op=ALU.not_equal, fill=1.0, base=0,
                       pattern=[[-1, ident.shape[1]]], channel_multiplier=1).then_inc(made, 1)


class Norm:

    def __init__(self, m, name):
        self.stats = m.sb(name + "_stats", [P, TT, 6])
        self.mean_var = m.sb(name + "_mean_var", [P, TT, 2])
        self.rstd = m.sb(name + "_rstd", [P, TT])
        self.power = m.sb(name + "_power", [P, TT])
        self.stats_ready = m.sem(name + "_stats_ready")
        self.moments_ready = m.sem(name + "_moments_ready")
        self.rstd_ready = m.sem(name + "_rstd_ready")
        self.xn_ready = m.sem(name + "_xn_ready")

    def pool(self, pool):
        pool.memset(self.power[:, :], -0.5).then_inc(self.rstd_ready, 1)
        pool.wait_ge(self.moments_ready, TT)
        pool.tensor_scalar(self.rstd[:, :], self.mean_var[:, :, 1], EPS, None, ALU.add).then_inc(self.rstd_ready, 1)
        pool.wait_ge(self.rstd_ready, 2)
        pool.tensor_tensor(self.rstd[:, :], self.rstd[:, :], self.power[:, :], ALU.pow).then_inc(self.rstd_ready, 1)

    def vector(self, dve, xn, x, wait_tile=None):
        for t in range(TT):
            if wait_tile:
                wait_tile(t)
            dve.bn_stats(self.stats[:, t, :], x[:, t, :]).then_inc(self.stats_ready, 1)
        for t in range(TT):
            dve.wait_ge(self.stats_ready, t + 1)
            dve.bn_aggr(self.mean_var[:, t, :], self.stats[:, t, :]).then_inc(self.moments_ready, 1)
        dve.wait_ge(self.rstd_ready, 3)
        for t in range(TT):
            dve.tensor_scalar(xn[:, t, :], x[:, t, :], self.mean_var[:, t, 0:1], self.rstd[:, t:t + 1],
                              ALU.subtract, ALU.mult).then_inc(self.xn_ready, 1)


def weight_rows(w):
    return w.rearrange("(k p) n -> p k n", p=P)


def project(nc, m, a, scr, x, qT, rel_k, rel_v, ident):
    xn = m.sb("xn_a", [P, TT, D])
    xnT = [m.sb(f"xnT_a{s}", [P, KD, T], F16) for s in "hl"]
    ctx_ti = m.sb("ctx_ti", [TI, B, D])
    txtT = [m.sb(f"txtT_{s}", [P, KD, B, TXT], F16) for s in "hl"]
    imgT = [m.sb(f"imgT_{s}", [P, KD, B, IMG], F16) for s in "hl"]
    staged = [m.sb(f"staged{i}", [P, KD, INNER]) for i in range(2)]
    names = ["Wq", "Wk", "Wk_ip", "Wv", "Wv_ip"]
    W = {n: [m.sb(f"{n}_{s}", [P, KD, INNER], F16) for s in "hl"] for n in names}
    KT = m.sb("KT", [P, B, 2, PAIRS, TI], F16)
    v_out = [m.sb(f"v_out{i}", [P, 2, INNER], F16) for i in range(2)]
    bank = m.ps("bank_a", [P, 8, 512])

    norm = Norm(m, "norm_a")
    ident_made = m.sem("ident_a_made")
    x_loaded = m.sem("x_a_loaded")
    ctx_loaded = m.sem("ctx_ti_loaded")
    w_loaded = {n: m.sem(f"{n}_loaded") for n in names}
    w_hi = m.sem("w_hi")
    w_lo = m.sem("w_lo")
    job_ready = m.sem("job_a_ready")
    job_hi = m.sem("job_a_hi")
    job_lo = m.sem("job_a_lo")
    v_stored = [m.sem(f"v_stored{i}") for i in range(2)]
    kt_stored = m.sem("kt_stored")

    XN, CT, Q, K = 0, TT // 2, TT // 2 + B // 2, TT // 2 + B // 2 + 2 * PAIRS
    G = 4
    NK = B // G + 1
    V = K + NK * PAIRS
    v_chunks = [("Wv", txtT, c * P, min(P, B * TXT - c * P)) for c in range(-(-B * TXT // P))]
    v_chunks += [("Wv_ip", imgT, c * P, P) for c in range(B * IMG // P)]

    block = m.ctx.enter_context(nc.Block())

    @block.sync
    def _(sp):
        sp.dma_start(x[:, :, :], a["x"].rearrange("(t b) q d -> (b q) t d", b=2)).then_inc(x_loaded, 16)
        sp.dma_start(ctx_ti[:, :, :], a["ctx"][:, 0:TI, :].rearrange("b j d -> j b d")).then_inc(ctx_loaded, 16)
        for n, name in enumerate(names):
            if n >= 2:
                sp.wait_ge(w_lo, n - 1)
            sp.dma_start(staged[n % 2][:, :, :], weight_rows(a[name])).then_inc(w_loaded[name], 16)
            if n == 1:
                rel_k.load(sp)
                rel_v.load(sp)
        sp.wait_ge(job_hi, V)
        sp.wait_ge(job_lo, V)
        sp.dma_start(scr["kt"].rearrange("b p f -> p b f"), KT[:, :, :, :, :].rearrange("p b s m j -> p b (s m j)")).then_inc(kt_stored, 16)
        row = 0
        for c, (_, _, _, n) in enumerate(v_chunks):
            sp.wait_ge(job_lo, V + 2 * c + 2)
            sp.dma_start(scr["v"][row:row + n, :], v_out[c % 2][0:n, :, :].rearrange("p s n -> p (s n)")).then_inc(v_stored[c % 2], 16)
            row += n
        for i in range(2):
            sp.wait_ge(v_stored[i], 16 * (len(v_chunks) // 2))
        sp.wait_ge(kt_stored, 16)

    @block.gpsimd
    def _(pool):
        make_identity(pool, ident[:, :], ident_made)
        norm.pool(pool)

    def xn_dst(s, g):
        return xnT[s][:, :, g * 2 * P:(g + 1) * 2 * P]

    def ctx_job(g):
        src = bank[:, (CT + g) % 8, 0:4 * TI].rearrange("p (k b j) -> p k b j", k=KD, b=2)
        return src[:, :, :, 0:TXT], src[:, :, :, TXT:TI]

    @block.tensor
    def _(pe):
        pe.wait_ge(ident_made, 2)
        for g in range(TT // 2):
            pe.wait_ge(norm.xn_ready, 2 * g + 2)
            for k in range(KD):
                for t in range(2):
                    at = (2 * k + t) * P
                    mm = pe.transpose(bank[:, XN + g, at:at + P], xn[:, 2 * g + t, k * P:(k + 1) * P], ident[:, :])
            mm.then_inc(job_ready, 1)
        pe.wait_ge(ctx_loaded, 16)
        for g in range(B // 2):
            if CT + g >= 8:
                pe.wait_ge(job_lo, CT + g - 7)
            for k in range(KD):
                for b in range(2):
                    at = (2 * k + b) * TI
                    mm = pe.transpose(bank[:, (CT + g) % 8, at:at + TI], ctx_ti[:, 2 * g + b, k * P:(k + 1) * P],
                                      ident[0:TI, 0:TI])
            mm.then_inc(job_ready, 1)
        pe.wait_ge(w_lo, 1)
        pe.wait_ge(w_hi, 1)
        with pe.Fori(0, PAIRS // 4) as i:
            for u in range(4):
                for n in range(2):
                    job = Q + 2 * u + n
                    pe.wait_ge(job_lo, i * 8 + (job - 7))
                    for k in range(KD):
                        lhs = [w[:, k, bass.ds(i * (4 * P) + u * P, P)] for w in W["Wq"]]
                        rhs = [x_[:, k, n * 512:(n + 1) * 512] for x_ in xnT]
                        mm = mm3(pe, bank[:, job % 8, :], lhs, rhs, k == 0, k == KD - 1)
                    mm.then_inc(job_ready, 1)
        pe.wait_ge(w_lo, 3)
        pe.wait_ge(w_hi, 3)
        with pe.Fori(0, PAIRS) as i:
            for n in range(NK):
                pe.wait_ge(job_lo, i * NK + (K + n - NK + 1))
                name, src = ("Wk", txtT) if n < NK - 1 else ("Wk_ip", imgT)
                for k in range(KD):
                    lhs = [w[:, k, bass.ds(i * P, P)] for w in W[name]]
                    rhs = [(s[:, k, n * G:(n + 1) * G, :] if n < NK - 1 else s[:, k, :, :]).rearrange("p b j -> p (b j)") for s in src]
                    mm = mm3(pe, bank[:, (n + 4) % 8, 0:rhs[0].shape[1]], lhs, rhs, k == 0, k == KD - 1)
                mm.then_inc(job_ready, 1)
        pe.wait_ge(w_lo, 5)
        pe.wait_ge(w_hi, 5)
        for c, (name, src, at, rows) in enumerate(v_chunks):
            for n in range(2):
                job = V + 2 * c + n
                pe.wait_ge(job_lo, job - 4)
                for k in range(KD):
                    lhs = [s[:, k, :, :].rearrange("p b j -> p (b j)")[:, at:at + rows] for s in src]
                    rhs = [w[:, k, n * 512:(n + 1) * 512] for w in W[name]]
                    mm = mm3(pe, bank[0:rows, (4 + (job - V) % 5) % 8, :], lhs, rhs, k == 0, k == KD - 1)
                mm.then_inc(job_ready, 1)

    @block.scalar
    def _(act):
        def hi(job, dst, src, scale):
            act.wait_ge(job_ready, job)
            split_hi(act, dst, src, scale).then_inc(job_hi, 1)

        def weight(n):
            act.wait_ge(w_loaded[names[n]], 16)
            split_hi(act, W[names[n]][0][:, :, :], staged[n % 2][:, :, :], SW).then_inc(w_hi, 1)

        weight(0)
        weight(1)
        for g in range(TT // 2):
            hi(XN + g + 1, xn_dst(0, g), bank[:, XN + g, :].rearrange("p (k t) -> p k t", k=KD), SA)
        for g in range(B // 2):
            act.wait_ge(job_ready, CT + g + 1)
            txt, img = ctx_job(g)
            split_hi(act, txtT[0][:, :, 2 * g:2 * g + 2, :], txt, SA)
            split_hi(act, imgT[0][:, :, 2 * g:2 * g + 2, :], img, SA).then_inc(job_hi, 1)
        weight(2)
        weight(3)
        with act.Fori(0, PAIRS // 4) as i:
            for u in range(4):
                for n in range(2):
                    job = Q + 2 * u + n
                    hi(i * 8 + (job + 1), qT[0][:, bass.ds(i * 4 + u, 1), n * 512:(n + 1) * 512], bank[:, job % 8, :].unsqueeze(1),
                       SCALE * SA / (SA * SW))
        weight(4)
        with act.Fori(0, PAIRS) as i:
            for n in range(NK):
                src, dst = (bank[:, (n + 4) % 8, 0:G * TXT], KT[:, n * G:(n + 1) * G, 0, :, 0:TXT]) if n < NK - 1 else \
                    (bank[:, (n + 4) % 8, 0:B * IMG], KT[:, :, 0, :, TXT:TI])
                hi(i * NK + (K + n + 1), dst[:, :, bass.ds(i, 1), :].squeeze(2), src.rearrange("p (b j) -> p b j", j=dst.shape[3]),
                   SA / (SA * SW))
        for c, (_, _, _, rows) in enumerate(v_chunks):
            if c >= 2:
                act.wait_ge(v_stored[c % 2], 16 * (c // 2))
            for n in range(2):
                job = V + 2 * c + n
                hi(job + 1, v_out[c % 2][0:rows, 0, n * 512:(n + 1) * 512], bank[0:rows, (4 + (job - V) % 5) % 8, :], SA / (SA * SW))

    @block.vector
    def _(dve):
        def lo(job, dst, src, hi_, scale):
            dve.wait_ge(job_hi, job)
            split_lo(dve, dst, src, hi_, scale).then_inc(job_lo, 1)

        def weight(n):
            dve.wait_ge(w_hi, n + 1)
            split_lo(dve, W[names[n]][1][:, :, :], staged[n % 2][:, :, :], W[names[n]][0][:, :, :], SW).then_inc(w_lo, 1)

        norm.vector(dve, xn, x, lambda t: dve.wait_ge(x_loaded, 16))
        weight(0)
        weight(1)
        for g in range(TT // 2):
            lo(XN + g + 1, xn_dst(1, g), bank[:, XN + g, :].rearrange("p (k t) -> p k t", k=KD), xn_dst(0, g), SA)
        for g in range(B // 2):
            dve.wait_ge(job_hi, CT + g + 1)
            for k in range(KD):
                for part, (src, dst) in enumerate(zip(ctx_job(g), (txtT, imgT))):
                    io = [s[:, k, 2 * g:2 * g + 2, :] for s in dst]
                    ins = split_lo(dve, io[1], src[:, k, :, :], io[0], SA)
            ins.then_inc(job_lo, 1)
        weight(2)
        weight(3)
        with dve.Fori(0, PAIRS // 4) as i:
            for u in range(4):
                for n in range(2):
                    job = Q + 2 * u + n
                    dst = [q[:, bass.ds(i * 4 + u, 1), n * 512:(n + 1) * 512] for q in qT]
                    lo(i * 8 + (job + 1), dst[1], bank[:, job % 8, :].unsqueeze(1), dst[0], SCALE * SA / (SA * SW))
        weight(4)
        with dve.Fori(0, PAIRS) as i:
            for n in range(NK):
                if n < NK - 1:
                    src, dst = bank[:, (n + 4) % 8, 0:G * TXT], [KT[:, n * G:(n + 1) * G, s, :, 0:TXT] for s in range(2)]
                else:
                    src, dst = bank[:, (n + 4) % 8, 0:B * IMG], [KT[:, :, s, :, TXT:TI] for s in range(2)]
                dst = [d[:, :, bass.ds(i, 1), :].squeeze(2) for d in dst]
                lo(i * NK + (K + n + 1), dst[1], src.rearrange("p (b j) -> p b j", j=dst[0].shape[2]), dst[0], SA / (SA * SW))
        for c, (_, _, _, rows) in enumerate(v_chunks):
            if c >= 2:
                dve.wait_ge(v_stored[c % 2], 16 * (c // 2))
            for n in range(2):
                job = V + 2 * c + n
                io = [v_out[c % 2][0:rows, s, n * 512:(n + 1) * 512] for s in range(2)]
                lo(job + 1, io[1], bank[0:rows, (4 + (job - V) % 5) % 8, :], io[0], SA / (SA * SW))


class ExtendedRows:

    def __init__(self, m, name, source, copies):
        self.tiles = [m.sb(name + "_rows0", [P, copies, HD]), m.sb(name + "_rows1", [EXT - P, copies, HD])]
        self.loaded = m.sem(name + "_rows_loaded")
        parts = [(0, REL0, source[0:1, :]), (REL0, NREL, source[:, :]), (REL0 + NREL, EXT - REL0 - NREL, source[NREL - 1:NREL, :])]
        self.transfers = []
        for first, n, rows in parts:
            for tile, low, high in ((self.tiles[0], 0, P), (self.tiles[1], P, EXT)):
                start, end = max(first, low), min(first + n, high)
                if start < end:
                    src = rows.broadcast_to([end - start, HD]) if rows.shape[0] == 1 else rows[start - first:end - first, :]
                    self.transfers += [(tile[start - low:end - low, c, :], src) for c in range(copies)]
        self.loads = 16 * len(self.transfers)

    def load(self, sp):
        for dst, src in self.transfers:
            sp.dma_start(dst, src).then_inc(self.loaded, 16)


class AudioWeights:

    def __init__(self, m):
        self.wkT = [m.sb(f"wkT_{n}", [P, PAIRS, D], F16) for n in "hl"]
        self.wv = [m.sb(f"wv_{n}", [P, KD, INNER], F16) for n in "hl"]
        self.gains = m.sb("gains", [P, 2])


class AudioWeightsWork:

    def __init__(self, m, audio, bank):
        self.to, self.bank = audio, bank
        self.wk_f = m.sb("wk_ap_f", [P, KD, INNER])
        self.wv_f = m.sb("wv_ap_f", [P, KD, INNER])
        self.wk_loaded, self.wv_loaded, self.ab_loaded = m.sem("wk_ap_loaded"), m.sem("wv_ap_loaded"), m.sem("alpha_beta_loaded")
        self.turned, self.wk_hi, self.wk_lo = m.sem("wkT_turned"), m.sem("wkT_hi"), m.sem("wkT_lo")
        self.wv_hi, self.wv_lo = m.sem("wv_ap_hi"), m.sem("wv_ap_lo")
        self.tanh_ready, self.gain_ready = m.sem("tanh_ready"), m.sem("gain_ready")

    def sync(self, sp, a):
        sp.dma_start(self.wv_f[:, :, :], weight_rows(a["Wv_ap"])).then_inc(self.wv_loaded, 16)
        sp.dma_start(self.wk_f[:, :, :], weight_rows(a["Wk_ap"])).then_inc(self.wk_loaded, 16)
        for n, name in enumerate(("alpha", "beta")):
            sp.dma_start(self.to.gains[:, n:n + 1], a[name].rearrange("(a b) -> a b", a=1).broadcast_to([P, 1])).then_inc(self.ab_loaded, 16)

    def job(self, g):
        return self.bank[:, g, :].rearrange("p (m d) -> p m d", m=2), [w[:, 2 * g:2 * g + 2, :] for w in self.to.wkT]

    def tensor(self, pe, ident):
        pe.wait_ge(self.wk_loaded, 16)
        for g in range(PAIRS // 2):
            for u in range(2):
                for k in range(KD):
                    mm = pe.transpose(self.bank[:, g, (2 * u + k) * P:(2 * u + k + 1) * P],
                                      self.wk_f[:, k, (2 * g + u) * P:(2 * g + u + 1) * P], ident[:, :])
            mm.then_inc(self.turned, 1)

    def scalar(self, act):
        act.wait_ge(self.wv_loaded, 16)
        split_hi(act, self.to.wv[0][:, :, :], self.wv_f[:, :, :], SW).then_inc(self.wv_hi, 1)
        for g in range(PAIRS // 2):
            act.wait_ge(self.turned, g + 1)
            src, dst = self.job(g)
            split_hi(act, dst[0], src, SW).then_inc(self.wk_hi, 1)
        act.wait_ge(self.ab_loaded, 32)
        act.activation(self.to.gains[:, :], self.to.gains[:, :], ACT.Tanh).then_inc(self.tanh_ready, 1)

    def vector(self, dve):
        dve.wait_ge(self.wv_hi, 1)
        split_lo(dve, self.to.wv[1][:, :, :], self.wv_f[:, :, :], self.to.wv[0][:, :, :], SW).then_inc(self.wv_lo, 1)
        for g in range(PAIRS // 2):
            dve.wait_ge(self.wk_hi, g + 1)
            src, dst = self.job(g)
            split_lo(dve, dst[1], src, dst[0], SW).then_inc(self.wk_lo, 1)
        dve.wait_ge(self.tanh_ready, 1)
        gains = self.to.gains
        dve.tensor_scalar(gains[:, 0:1], gains[:, 0:1], 1.0, None, ALU.add)
        dve.tensor_scalar(gains[:, 1:2], gains[:, 1:2], 1.0, 1 / (SP * SA), ALU.add, ALU.mult).then_inc(self.gain_ready, 1)


class AudioContext:

    def __init__(self, m, ctx):
        self.nat = m.sb("ctx_nat", [P, NCH, D])
        self.loaded = m.sem("nat_loaded")
        self.ctx = ctx.rearrange("b j d -> (b j d)")

    def load(self, sp, at, tail_at):
        sp.dma_start(self.nat[:, 0:NCH - 1, :], self.ctx[bass.ds(at, (NCH - 1) * P * D)].rearrange("(p c d) -> p c d", p=P, d=D)).then_inc(self.loaded, 16)
        sp.dma_start(self.nat[0:TAIL, NCH - 1, :], self.ctx[bass.ds(tail_at, TAIL * D)].rearrange("(p d) -> p d", p=TAIL)).then_inc(self.loaded, 16)

    def load_first(self, sp):
        self.load(sp, TI * D, TI * D + (NCH - 1) * P * D)


def relative_scores(nc, m, a, scr, qT, rel_k, rel_v, audio, first_load, ident):
    ext = rel_k.tiles
    table = [m.sb(f"relk_table_{s}", [P, 2, EXT], F16) for s in "hl"]
    R = m.sb("R", [TXT, B * PAIRS, 2, NQ])
    tbank = m.ps("relk_bank", [P, 512])
    bank = m.ps("R_bank", [P, 4, 512])
    relv_stored = m.sem("relv_ext_stored")
    zeroed = m.sem("relk_zeroed")
    turned = m.sem("relk_turned")
    table_hi = m.sem("relk_table_hi")
    table_lo = m.sem("relk_table_lo")
    even_ready, odd_ready = m.sem("R_even_ready"), m.sem("R_odd_ready")
    even_out, odd_out = m.sem("R_even_out"), m.sem("R_odd_out")
    r_stored = m.sem("R_stored")
    U = 4
    work = AudioWeightsWork(m, audio, bank)

    block = m.ctx.enter_context(nc.Block())

    @block.sync
    def _(sp):
        work.sync(sp, a)
        first_load(sp)
        sp.wait_ge(rel_v.loaded, rel_v.loads)
        sp.dma_start(scr["relv"][0:P, :], rel_v.tiles[0][:, 0, :]).then_inc(relv_stored, 16)
        sp.dma_start(scr["relv"][P:EXT, :], rel_v.tiles[1][:, 0, :]).then_inc(relv_stored, 16)
        sp.wait_ge(even_out, NQ // U)
        sp.wait_ge(odd_out, NQ // U)
        sp.dma_start(scr["R"].rearrange("b j f -> j b f"), R[:, :, :, :].rearrange("j (b p) e i -> j b (p e i)", b=B)).then_inc(r_stored, 16)
        sp.wait_ge(relv_stored, 32)
        sp.wait_ge(r_stored, 16)

    @block.gpsimd
    def _(pool):
        pool.memset(table[0][:, :, :], 0.0).then_inc(zeroed, 1)
        pool.memset(table[1][:, :, :], 0.0).then_inc(zeroed, 1)

    @block.tensor
    def _(pe):
        pe.wait_ge(rel_k.loaded, rel_k.loads)
        pe.transpose(tbank[:, 0:P], ext[0][:, :, :].rearrange("r e d -> r (e d)"), ident[:, :])
        pe.transpose(tbank[:, P:EXT], ext[1][:, :, :].rearrange("r e d -> r (e d)"), ident[0:EXT - P, 0:EXT - P]).then_inc(turned, 1)
        pe.wait_ge(table_lo, 2)

        def group(g, u):
            for e, ready in ((0, even_ready), (1, odd_ready)):
                for v in range(U):
                    lhs = [t[:, e, bass.ds(g * (-2 * U) + (NQ - 1 - U * u - v), TXT)] for t in table]
                    rhs = [q[:, :, :].rearrange("d p (b i) -> d b p i", i=NQ)[:, :, :, bass.ds(g * (2 * U) + (U * u + v), 1)].squeeze(3) for q in qT]
                    mm = mm3(pe, bank[0:TXT, 2 * u + e, v * P:(v + 1) * P], lhs, rhs)
                mm.then_inc(ready, 1)

        group(0, 0)
        group(0, 1)
        with pe.Fori(1, NQ // (2 * U)) as g:
            for u in range(2):
                pe.wait_ge(even_out, g * 2 + (u - 1))
                pe.wait_ge(odd_out, g * 2 + (u - 1))
                group(g, u)
        pe.wait_ge(even_out, NQ // U)
        pe.wait_ge(odd_out, NQ // U)
        work.tensor(pe, ident)

    def R_at(g, u, e):
        return R[:, :, e, bass.ds(g * (2 * U) + U * u, U)].rearrange("j q i -> j i q")

    def bank_of(u, e):
        return bank[0:TXT, 2 * u + e, :].rearrange("j (i q) -> j i q", i=U)

    @block.scalar
    def _(act):
        act.wait_ge(zeroed, 2)
        act.wait_ge(turned, 1)
        for e in range(2):
            h = slice(e * HD, (e + 1) * HD)
            split_hi(act, table[0][h, e, :], tbank[h, 0:EXT], SA).then_inc(table_hi, 1)
        with act.Fori(0, NQ // (2 * U)) as g:
            for u in range(2):
                act.wait_ge(even_ready, g * 2 + (u + 1))
                act.activation(R_at(g, u, 0), bank_of(u, 0), ACT.Copy, scale=1 / (SA * SA)).then_inc(even_out, 1)
        work.scalar(act)

    @block.vector
    def _(dve):
        for e in range(2):
            h = slice(e * HD, (e + 1) * HD)
            dve.wait_ge(table_hi, 2)
            split_lo(dve, table[1][h, e, :], tbank[h, 0:EXT], table[0][h, e, :], SA).then_inc(table_lo, 1)
        with dve.Fori(0, NQ // (2 * U)) as g:
            for u in range(2):
                dve.wait_ge(odd_ready, g * 2 + (u + 1))
                dve.tensor_scalar(R_at(g, u, 1), bank_of(u, 1), 1 / (SA * SA), None, ALU.mult).then_inc(odd_out, 1)
        work.vector(dve)


def cross_attention(nc, m, scr, qT, OT, audio, context, ident):
    NPREP = NCH // 2
    wkT, wv, gains = audio.wkT, audio.wv, audio.gains
    nat, nat_loaded = context.nat, context.loaded
    ctx_s = [[m.sb(f"ctx_{s}{i}", [P, NCH, D], F16) for s in "hl"] for i in range(2)]
    ctxT = [[m.sb(f"ctxT_{s}{i}", [P, KD, NCH * P], F16) for s in "hl"] for i in range(2)]
    qf = [m.sb(f"q_fold_{s}", [P, KD, PAIRS, P], F16) for s in "hl"]
    prob = m.sb("prob", [P, AUD])
    PT = [m.sb(f"probT_{s}", [P, NCH, P], F16) for s in "hl"]
    BD = [[m.sb(f"q_diag_{s}{i}", [P, PAIRS, P], F16) for s in "hl"] for i in range(2)]
    u_sb = m.sb("u_sb", [P, D])
    UT = [m.sb(f"uT_{s}", [P, KD, P], F16) for s in "hl"]
    maxes = m.sb("maxes", [P, SB])
    top = m.sb("top", [P, 1])
    negmax = m.sb("negmax", [P, 1])
    den = m.sb("den", [P, 2])
    rden = m.sb("rden", [P, 1])
    KTb = m.sb("KT_b", [P, 2, PAIRS, TI], F16)
    Vb = m.sb("V_b", [TI, 2, INNER], F16)
    Rb = m.sb("R_b", [TI, 2 * 512])
    ST = m.sb("ST", [TI, 512])
    tprob = m.sb("tprob", [P, 4, TI])
    tmax = m.sb("tmax", [P, 2, 4])
    tsum = m.sb("tsum", [P, 2, 4])
    PTt = [m.sb(f"tprobT_{s}", [TI, 2, 512], F16) for s in "hl"]
    S = m.ps("S", [P, SB, 512])
    PTb = m.ps("PT_bank", [P, 2, 512])
    Ub = m.ps("U_bank", [P, 512])
    M0 = m.ps("M0", [P, 512])
    M1 = m.ps("M1", [P, 512])

    kt_loaded, v_loaded, r_loaded = m.sem("kt_loaded"), m.sem("v_loaded"), m.sem("r_loaded")
    pt_stored = m.sem("tprob_stored")
    zeroed = m.sem("zeroed")
    bd_ready = m.sem("q_diag_ready")
    scores_ready = m.sem("scores_ready")
    maxes_ready = m.sem("maxes_ready")
    top_ready = m.sem("top_ready")
    negmax_ready = m.sem("negmax_ready")
    prob_ready = m.sem("prob_ready")
    pt_ready, pt_hi, pt_lo = m.sem("pt_ready"), m.sem("pt_hi"), m.sem("pt_lo")
    u_ready, rden_ready, u_normed = m.sem("u_ready"), m.sem("rden_ready"), m.sem("u_normed")
    ut_ready, ut_hi, ut_lo = m.sem("ut_ready"), m.sem("ut_hi"), m.sem("ut_lo")
    proj_ready = m.sem("proj_ready")
    ot_added = m.sem("ot_added")
    fold_ready, fold_hi, fold_lo = m.sem("fold_ready"), m.sem("fold_hi"), m.sem("fold_lo")
    ctxt_ready, ctxt_hi, ctxt_lo = m.sem("ctxt_ready"), m.sem("ctxt_hi"), m.sem("ctxt_lo")
    csplit_hi, csplit_lo = m.sem("csplit_hi"), m.sem("csplit_lo")
    text_ready = m.sem("text_ready")
    text_added = m.sem("text_added")
    st_ready = m.sem("st_ready")
    tmax_ready, ts_ready, te_ready = m.sem("tmax_ready"), m.sem("ts_ready"), m.sem("te_ready")
    tsum_ready, trec_ready, tgain_ready, tp_ready = m.sem("tsum_ready"), m.sem("trec_ready"), m.sem("tgain_ready"), m.sem("tp_ready")
    ptt_hi, ptt_lo = m.sem("ptt_hi"), m.sem("ptt_lo")

    block = m.ctx.enter_context(nc.Block())
    MAIN = (NCH - 1) * P

    def rows_of(c):
        return TAIL if c == NCH - 1 else P

    def width(n):
        return min(512, AUD - 512 * n)

    def batches(eng, body):
        with eng.Fori(0, B // 2 - 1) as j:
            body(j * 2, 0, B)
            body(j * 2 + 1, 1, B)
        body(B - 2, 0, 1)
        body(B - 1, 1, 0)

    first_banks = [S[:, 0, :], S[:, 1, :], S[:, 2, :], PTb[:, 0, :], PTb[:, 1, :], M1]
    fold_banks = [M0, Ub]

    @block.sync
    def _(sp):
        def flat(t, offset, n):
            whole = t.rearrange(" ".join("abcd"[:len(t.shape)]) + " -> (" + " ".join("abcd"[:len(t.shape)]) + ")")
            return whole[bass.ds(offset, n)]

        def load_kt(at):
            sp.dma_start(KTb[:, :, :, :].rearrange("p s m j -> p (s m j)"),
                         flat(scr["kt"], at, P * KT_ROW).rearrange("(p f) -> p f", p=P)).then_inc(kt_loaded, 16)

        def load_r(at):
            sp.dma_start(Rb[0:TXT, :], flat(scr["R"], at, TXT * 1024).rearrange("(j f) -> j f", j=TXT)).then_inc(r_loaded, 16)

        def load_v(text_at, image_at):
            v = Vb[:, :, :].rearrange("j s n -> j (s n)")
            sp.dma_start(v[0:TXT, :], flat(scr["v"], text_at, TXT * V_ROW).rearrange("(j f) -> j f", j=TXT)).then_inc(v_loaded, 16)
            sp.dma_start(v[TXT:TI, :], flat(scr["v"], image_at, IMG * V_ROW).rearrange("(j f) -> j f", j=IMG)).then_inc(v_loaded, 16)

        V_ROW, KT_ROW = 2 * INNER, 2 * PAIRS * TI
        V_IMG = B * TXT * V_ROW
        NAT0 = TI * D
        load_kt(0)
        sp.wait_ge(zeroed, 1)
        load_r(0)
        load_v(0, V_IMG)
        sp.wait_ge(ctxt_ready, NPREP)
        sp.wait_ge(csplit_lo, NPREP)
        context.load(sp, NAT0 + CTX * D, NAT0 + (CTX + MAIN) * D)

        def body(b, parity, left):
            fixed = (lambda v: v) if isinstance(b, int) else sp.snap
            nat_at = fixed(b * (CTX * D) + (NAT0 + 2 * CTX * D))
            nat_tail_at = fixed(b * (CTX * D) + (NAT0 + 2 * CTX * D + MAIN * D))
            kt_at = fixed(b * (P * KT_ROW) + P * KT_ROW)
            r_at = fixed(b * (TXT * 1024) + TXT * 1024)
            vt_at = fixed(b * (TXT * V_ROW) + TXT * V_ROW)
            vi_at = fixed(b * (IMG * V_ROW) + (V_IMG + IMG * V_ROW))
            pt_at = fixed(b * (TXT * 2048))
            kt_read, v_read = fixed(b * 8 + 5), fixed(b * 8 + 8)
            r_read, prepared, stored = fixed(b * 2 + 2), fixed((b + 2) * NPREP), fixed((b + 1) * 32)
            if left:
                sp.wait_ge(text_ready, kt_read)
                load_kt(kt_at)
                sp.wait_ge(st_ready, r_read)
                load_r(r_at)
            if left > 1:
                sp.wait_ge(ctxt_ready, prepared)
                sp.wait_ge(csplit_lo, prepared)
                context.load(sp, nat_at, nat_tail_at)
            sp.wait_ge(text_ready, v_read)
            for s in range(2):
                sp.dma_start(flat(scr["pt"], pt_at, TXT * 2048).rearrange("(j s f) -> j s f", j=TXT, s=2)[:, s, :],
                             PTt[s][0:TXT, :, :].rearrange("j h f -> j (h f)")).then_inc(pt_stored, 16)
            if left:
                sp.wait_ge(pt_stored, stored)
                load_v(vt_at, vi_at)

        batches(sp, body)
        sp.wait_ge(pt_stored, B * 32)

    @block.gpsimd
    def _(pool):
        pool.memset(Rb[64:TI, :], 0.0).then_inc(zeroed, 1)
        pool.wait_ge(zeroed, 1)
        for i in range(2):
            for s in range(2):
                pool.memset(BD[i][s][:, :, :], 0.0).then_inc(zeroed, 1)
        pool.wait_ge(zeroed, 5)

        def diagonal(b, parity):
            for s in range(2):
                for e in range(2):
                    h = slice(e * HD, (e + 1) * HD)
                    pool.tensor_copy(BD[parity][s][h, :, h], qT[s][h, :, bass.ds(b * NQ, NQ)]).then_inc(bd_ready, 1)
                    pool.wait_ge(bd_ready, b * 4 + (2 * s + e + 1))

        diagonal(0, 0)
        diagonal(1, 1)

        def body(b, parity, left):
            if left > 1:
                pool.wait_ge(text_ready, b * 8 + 5)
                diagonal(b + 2, parity)

        batches(pool, body)

    @block.tensor
    def _(pe):
        def scores(r, p, parity, n):
            for k in range(KD):
                lhs = [q[:, k, p, :] for q in qf]
                rhs = [c[:, k, n * 512:n * 512 + width(n)] for c in ctxT[parity]]
                mm = mm3(pe, S[:, n, 0:width(n)], lhs, rhs, k == 0, k == KD - 1)
            mm.then_inc(scores_ready, 1)

        def turn_prob(r, j):
            for c in range(4 * j, 4 * j + 4):
                mm = pe.transpose(PTb[0:rows_of(c), j % 2, (c % 4) * P:(c % 4 + 1) * P],
                                  prob[:, c * P:c * P + rows_of(c)], ident[:, :])
            mm.then_inc(pt_ready, 1)

        def prob_ctx(r, parity, j):
            pe.wait_ge(pt_lo, r * 3 + (j + 1))
            for c in range(4 * j, 4 * j + 4):
                n = rows_of(c)
                mm = mm3(pe, Ub[:, 0:D], [t[0:n, c, :] for t in PT], [x[0:n, c, :] for x in ctx_s[parity]],
                         c == 0, c == NCH - 1)
            if j == 2:
                mm.then_inc(u_ready, 1)

        def turn_u(r):
            pe.wait_ge(u_normed, r + 1)
            for k in range(KD):
                mm = pe.transpose(M0[:, k * P:(k + 1) * P], u_sb[:, k * P:(k + 1) * P], ident[:, :])
            mm.then_inc(ut_ready, 1)

        def project_u(r, p):
            pe.wait_ge(ut_lo, r + 1)
            for k in range(KD):
                mm = mm3(pe, M0[:, 0:P], [w[:, k, p * P:(p + 1) * P] for w in wv], [u[:, k, :] for u in UT],
                         k == 0, k == KD - 1)
            mm.then_inc(proj_ready, 1)

        def fold(p, parity, bank=M0):
            for k in range(KD):
                mm = mm3(pe, bank[:, k * P:(k + 1) * P], [w[:, p, k * P:(k + 1) * P] for w in wkT],
                         [q[:, p, :] for q in BD[parity]])
            mm.then_inc(fold_ready, 1)

        def turn_ctx(j, bank=M1):
            for u in range(2):
                n = rows_of(2 * j + u)
                for k in range(KD):
                    at = (2 * k + u) * P
                    mm = pe.transpose(bank[:, at:at + n], nat[0:n, 2 * j + u, k * P:(k + 1) * P], ident[0:n, 0:n])
            mm.then_inc(ctxt_ready, 1)

        def text(b, p, parity):
            half, stage = divmod(p, 4)
            if stage == 0:
                if half == 0:
                    pe.wait_ge(kt_loaded, (b + 1) * 16)
                for q in range(4):
                    mm = mm3(pe, M1[0:TI, q * P:(q + 1) * P], [KTb[:, s, 4 * half + q, :] for s in range(2)],
                             [BD[parity][s][:, 4 * half + q, :] for s in range(2)])
            elif stage == 1:
                pe.wait_ge(st_ready, b * 2 + (half + 1))
                for q in range(4):
                    mm = pe.transpose(M1[:, q * TI:(q + 1) * TI], ST[:, q * P:(q + 1) * P], ident[0:TI, 0:TI])
            elif stage == 2:
                pe.wait_ge(tp_ready, b * 2 + (half + 1))
                for q in range(4):
                    mm = pe.transpose(M1[0:TI, q * P:(q + 1) * P], tprob[:, q, :], ident[:, :])
            else:
                pe.wait_ge(ptt_lo, b * 2 + (half + 1))
                if half == 0:
                    pe.wait_ge(v_loaded, (b + 1) * 32)
                for q in range(4):
                    at = (4 * half + q) * P
                    mm = mm3(pe, M1[:, q * P:(q + 1) * P], [Vb[:, s, at:at + P] for s in range(2)],
                             [t[:, half, q * P:(q + 1) * P] for t in PTt])
            mm.then_inc(text_ready, 1)

        def text_bank_free(b, p):
            half, stage = divmod(p - 1, 4)
            if p == 0:
                pe.wait_ge(text_added, b * 2 + 1)
            elif stage == 3:
                pe.wait_ge(text_added, b * 2 + (half + 2))
            else:
                pe.wait_ge((st_ready, ts_ready, ptt_lo)[stage], b * 2 + (half + 1))

        for j in range(NPREP):
            if j == 0:
                pe.wait_ge(nat_loaded, 32)
            turn_ctx(j, first_banks[j])
        pe.wait_ge(bd_ready, 4)
        for p in range(PAIRS):
            if p >= 2:
                pe.wait_ge(fold_lo, p - 1)
            fold(p, 0, fold_banks[p % 2])
        pe.wait_ge(ctxt_lo, NPREP)
        pe.wait_ge(fold_lo, 1)
        for n in range(SB):
            scores(0, 0, 0, n)
        pe.wait_ge(fold_lo, PAIRS)

        def turn_and_score(b, r, p, parity, left):
            follows = p < PAIRS - 1 or left
            np_, npar = (p + 1, parity) if p < PAIRS - 1 else (0, 1 - parity)

            def next_scores(n):
                if follows:
                    if p == PAIRS - 1:
                        pe.wait_ge(ctxt_lo, (b + 1) * NPREP + (2 * n + 2))
                    scores(r + 1, np_, npar, n)

            pe.wait_ge(prob_ready, r + 1)
            turn_prob(r, 0)
            turn_prob(r, 1)
            next_scores(0)
            if b is not None:
                if left:
                    pe.wait_ge(fold_lo, (b + 1) * 8 + (p or PAIRS))
                else:
                    pe.wait_ge(ot_added, r)
                turn_u(r - 1)
            pe.wait_ge(pt_lo, r * 3 + 1)
            turn_prob(r, 2)
            next_scores(1)
            if b is not None:
                project_u(r - 1, (p - 1) % PAIRS)
            next_scores(2)

        turn_and_score(None, 0, 0, 0, True)

        def body(b, parity, left):
            for p in range(PAIRS):
                r = b * 8 + p
                text_bank_free(b, p)
                if left and 1 <= p <= NPREP:
                    if p == 1:
                        pe.wait_ge(nat_loaded, (b + 2) * 32)
                    turn_ctx(p - 1)
                if p == 0:
                    pe.wait_ge(csplit_lo, (b + 1) * NPREP)
                prob_ctx(r, parity, 0)
                if left:
                    if p == 0:
                        pe.wait_ge(bd_ready, (b + 2) * 4)
                    pe.wait_ge(ot_added, r + 1)
                    fold(p, 1 - parity)
                prob_ctx(r, parity, 1)
                prob_ctx(r, parity, 2)
                if left and 1 <= p <= NPREP:
                    pe.wait_ge(ctxt_lo, (b + 1) * NPREP + p)
                text(b, p, parity)
                if p < PAIRS - 1:
                    turn_and_score(b, r + 1, p + 1, parity, left)
                elif left:
                    turn_and_score(b, r + 1, 0, 1 - parity, left)
            if not left:
                r = b * 8 + (PAIRS - 1)
                pe.wait_ge(ot_added, r + 1)
                turn_u(r)
                project_u(r, PAIRS - 1)

        batches(pe, body)

    def pt_io(j):
        full = 4 if j < 2 else 3
        bank = PTb[:, j % 2, :].rearrange("p (c q) -> p c q", c=4)
        io = [(bank[:, 0:full, :], [t[:, 4 * j:4 * j + full, :] for t in PT])]
        if full < 4:
            io.append((bank[0:TAIL, 3, :], [t[0:TAIL, 4 * j + 3, :] for t in PT]))
        return io

    def ctxt_io(j, parity, bank=M1):
        n = P + rows_of(2 * j + 1)
        return [(bank[:, 2 * k * P:2 * k * P + n], [t[:, k, 2 * j * P:2 * j * P + n] for t in ctxT[parity]]) for k in range(KD)]

    def each(io, f):
        for src, dst in io:
            ins = f(src, dst)
        return ins

    def by_k(bank):
        return bank[:, 0:KD * P].rearrange("p (k q) -> p k q", k=KD)

    M0_k = by_k(M0)

    @block.scalar
    def _(act):
        def prob_exp(r, p):
            act.wait_ge(negmax_ready, r + 1)
            act.activation(prob[:, :], S[:, :, :].rearrange("p n f -> p (n f)")[:, 0:AUD], ACT.Exp, bias=negmax[:, 0:1],
                           scale=1 / (SA * SA), accum_out=den[:, p % 2:p % 2 + 1]).then_inc(prob_ready, 1)

        def prob_hi(r, j):
            act.wait_ge(pt_ready, r * 3 + (j + 1))
            each(pt_io(j), lambda s, d: split_hi(act, d[0], s, SP)).then_inc(pt_hi, 1)

        def u_hi(r):
            act.wait_ge(ut_ready, r + 1)
            split_hi(act, UT[0][:, :, :], M0_k, SA).then_inc(ut_hi, 1)

        def fold_hi_(count, p, bank=M0):
            act.wait_ge(fold_ready, count)
            split_hi(act, qf[0][:, :, p, :], by_k(bank), SA / (SA * SW)).then_inc(fold_hi, 1)

        def ctxt_hi_(count, j, parity, bank=M1):
            act.wait_ge(ctxt_ready, count)
            each(ctxt_io(j, parity, bank), lambda s, d: split_hi(act, d[0], s, SA)).then_inc(ctxt_hi, 1)

        for j in range(NPREP):
            ctxt_hi_(j + 1, j, 0, first_banks[j])
        for p in range(PAIRS):
            fold_hi_(p + 1, p, fold_banks[p % 2])
        prob_exp(0, 0)

        def parts_hi(b, r):
            prob_hi(r, 0)
            prob_hi(r, 1)
            if b is not None:
                u_hi(r - 1)
            prob_hi(r, 2)

        parts_hi(None, 0)

        def body(b, parity, left):
            for p in range(PAIRS):
                r = b * 8 + p
                half, stage = divmod(p, 4)
                if left and 1 <= p <= NPREP:
                    ctxt_hi_((b + 1) * NPREP + p, p - 1, 1 - parity)
                if p < PAIRS - 1 or left:
                    prob_exp(r + 1, p + 1)
                if left:
                    fold_hi_((b + 1) * 8 + (p + 1), p)
                if stage == 1:
                    act.wait_ge(ts_ready, b * 2 + (half + 1))
                    act.activation(tprob[:, :, :], tprob[:, :, :], ACT.Exp).then_inc(te_ready, 1)
                if stage == 2:
                    if half == 0:
                        act.wait_ge(v_loaded, (b + 1) * 32)
                    act.wait_ge(text_ready, r + 1)
                    split_hi(act, PTt[0][:, half, :], M1[0:TI, :], SP).then_inc(ptt_hi, 1)
                if p < PAIRS - 1 or left:
                    parts_hi(b, r + 1)
            if not left:
                u_hi(b * 8 + (PAIRS - 1))

        batches(act, body)

    @block.vector
    def _(dve):
        def row_max(r, n):
            dve.wait_ge(scores_ready, r * 3 + (n + 1))
            dve.tensor_reduce(maxes[:, n:n + 1], S[:, n, 0:width(n)], X, ALU.max).then_inc(maxes_ready, 1)
            if n == SB - 1:
                dve.wait_ge(maxes_ready, r * 3 + SB)
                dve.tensor_reduce(top[:, :], maxes[:, :], X, ALU.max).then_inc(top_ready, 1)
                dve.wait_ge(top_ready, r + 1)
                dve.tensor_scalar(negmax[:, :], top[:, :], -1 / (SA * SA), None, ALU.mult).then_inc(negmax_ready, 1)

        def prob_lo(r, j):
            dve.wait_ge(pt_hi, r * 3 + (j + 1))
            each(pt_io(j), lambda s, d: split_lo(dve, d[1], s, d[0], SP)).then_inc(pt_lo, 1)

        def u_lo(r):
            dve.wait_ge(ut_hi, r + 1)
            split_lo(dve, UT[1][:, :, :], M0_k, UT[0][:, :, :], SA).then_inc(ut_lo, 1)

        def u_norm(r, p):
            dve.wait_ge(prob_ready, r + 1)
            dve.reciprocal(rden[:, :], den[:, p % 2:p % 2 + 1]).then_inc(rden_ready, 1)
            dve.wait_ge(rden_ready, r + 1)
            dve.wait_ge(u_ready, r + 1)
            dve.tensor_scalar(u_sb[:, :], Ub[:, 0:D], rden[:, 0:1], gains[:, 1:2], ALU.mult, ALU.mult).then_inc(u_normed, 1)

        def add_heads(b, pairs, src, scale):
            for e in range(2):
                h = slice(e * HD, (e + 1) * HD)
                dst = OT[h, pairs, bass.ds(b * NQ, NQ)]
                ins = dve.scalar_tensor_tensor(out=dst, in0=src[h, :, h], scalar=scale, in1=dst, op0=ALU.mult, op1=ALU.add)
            return ins

        def add_audio(b, r, p):
            dve.wait_ge(proj_ready, r + 1)
            dve.wait_ge(text_added, b * 2 + (1 if p < 3 else 2 if p < PAIRS - 1 else 3))
            add_heads(b, slice(p, p + 1), M0[:, 0:P].unsqueeze(1), 1 / (SA * SW)).then_inc(ot_added, 1)

        def fold_lo_(count, p, bank=M0):
            dve.wait_ge(fold_hi, count)
            split_lo(dve, qf[1][:, :, p, :], by_k(bank), qf[0][:, :, p, :], SA / (SA * SW)).then_inc(fold_lo, 1)

        def ctxt_lo_(count, j, parity, bank=M1):
            dve.wait_ge(ctxt_hi, count)
            each(ctxt_io(j, parity, bank), lambda s, d: split_lo(dve, d[1], s, d[0], SA)).then_inc(ctxt_lo, 1)

        def ctx_split(count, j, parity):
            parts = [(slice(0, P), slice(2 * j, 2 * j + 2))] if 2 * j + 2 < NCH else \
                [(slice(0, P), slice(2 * j, 2 * j + 1)), (slice(0, TAIL), slice(2 * j + 1, 2 * j + 2))]
            hi, lo = ctx_s[parity]
            for ps, cs in parts:
                ins = dve.tensor_scalar(hi[ps, cs, :], nat[ps, cs, :], SA, None, ALU.mult)
            ins.then_inc(csplit_hi, 1)
            dve.wait_ge(csplit_hi, count)
            for ps, cs in parts:
                ins = split_lo(dve, lo[ps, cs, :], nat[ps, cs, :], hi[ps, cs, :], SA)
            ins.then_inc(csplit_lo, 1)

        def text_probs(b, half):
            dve.wait_ge(te_ready, b * 2 + (half + 1))
            dve.tensor_reduce(tsum[:, 0, :], tprob[:, :, 0:TXT], X, ALU.add)
            dve.tensor_reduce(tsum[:, 1, :], tprob[:, :, TXT:TI], X, ALU.add).then_inc(tsum_ready, 1)
            dve.wait_ge(tsum_ready, b * 2 + (half + 1))
            dve.reciprocal(tsum[:, :, :], tsum[:, :, :]).then_inc(trec_ready, 1)
            dve.wait_ge(trec_ready, b * 2 + (half + 1))
            dve.tensor_scalar(tsum[:, 1, :], tsum[:, 1, :], gains[:, 0:1], None, ALU.mult).then_inc(tgain_ready, 1)
            dve.tensor_tensor(tprob[:, :, 0:TXT], tprob[:, :, 0:TXT], tsum[:, 0, :].unsqueeze(2).broadcast_to([P, 4, TXT]), ALU.mult)
            dve.wait_ge(tgain_ready, b * 2 + (half + 1))
            dve.tensor_tensor(tprob[:, :, TXT:TI], tprob[:, :, TXT:TI], tsum[:, 1, :].unsqueeze(2).broadcast_to([P, 4, IMG]),
                              ALU.mult).then_inc(tp_ready, 1)

        def text(b, r, p):
            half, stage = divmod(p, 4)
            n = b * 2 + (half + 1)
            if stage == 0:
                if half == 0:
                    dve.wait_ge(r_loaded, (b + 1) * 16)
                dve.wait_ge(text_ready, r + 1)
                dve.scalar_tensor_tensor(out=ST[:, :], in0=M1[0:TI, :], scalar=1 / (SA * SA), in1=Rb[:, half * 512:(half + 1) * 512],
                                         op0=ALU.mult, op1=ALU.add).then_inc(st_ready, 1)
            elif stage == 1:
                dve.wait_ge(text_ready, r + 1)
                s = M1[:, 0:4 * TI].rearrange("p (q j) -> p q j", q=4)
                dve.tensor_reduce(tmax[:, 0, :], s[:, :, 0:TXT], X, ALU.max)
                dve.tensor_reduce(tmax[:, 1, :], s[:, :, TXT:TI], X, ALU.max).then_inc(tmax_ready, 1)
                dve.wait_ge(tmax_ready, n)
                dve.tensor_tensor(tprob[:, :, 0:TXT], s[:, :, 0:TXT], tmax[:, 0, :].unsqueeze(2).broadcast_to([P, 4, TXT]), ALU.subtract)
                dve.tensor_tensor(tprob[:, :, TXT:TI], s[:, :, TXT:TI], tmax[:, 1, :].unsqueeze(2).broadcast_to([P, 4, IMG]),
                                  ALU.subtract).then_inc(ts_ready, 1)
            elif stage == 2:
                dve.wait_ge(ptt_hi, n)
                split_lo(dve, PTt[1][:, half, :], M1[0:TI, :], PTt[0][:, half, :], SP).then_inc(ptt_lo, 1)
            else:
                dve.wait_ge(text_ready, r + 1)
                dve.wait_ge(ot_added, r + 1)
                add_heads(b, slice(4 * half, 4 * half + 4), M1[:, :].rearrange("p (q c) -> p q c", q=4),
                          1 / (SP * SA)).then_inc(text_added, 1)

        dve.memset(OT[:, 0:PAIRS // 2, :], 0.0).then_inc(ot_added, 1)
        dve.memset(OT[:, PAIRS // 2:, :], 0.0).then_inc(text_added, 1)
        dve.wait_ge(nat_loaded, 32)
        for j in range(NPREP):
            ctx_split(j + 1, j, 0)
            ctxt_lo_(j + 1, j, 0, first_banks[j])
        for p in range(PAIRS):
            fold_lo_(p + 1, p, fold_banks[p % 2])
        for n in range(SB):
            row_max(0, n)

        def parts_lo(b, r, p, follows):
            prob_lo(r, 0)
            prob_lo(r, 1)
            if follows:
                row_max(r + 1, 0)
            if b is not None:
                u_lo(r - 1)
            prob_lo(r, 2)
            if follows:
                row_max(r + 1, 1)
            if b is not None:
                add_audio(b, r - 1, (p - 1) % PAIRS)
            if follows:
                row_max(r + 1, 2)

        parts_lo(None, 0, 0, True)

        def body(b, parity, left):
            for p in range(PAIRS):
                r = b * 8 + p
                if left and 1 <= p <= NPREP:
                    if p == 1:
                        dve.wait_ge(nat_loaded, (b + 2) * 32)
                    ctxt_lo_((b + 1) * NPREP + p, p - 1, 1 - parity)
                if left:
                    fold_lo_((b + 1) * 8 + (p + 1), p)
                if p % 4 == 2:
                    text_probs(b, p // 4)
                if left and 1 <= p <= NPREP:
                    ctx_split((b + 1) * NPREP + p, p - 1, 1 - parity)
                u_norm(r, p)
                text(b, r, p)
                if p < PAIRS - 1:
                    parts_lo(b, r + 1, p + 1, p < PAIRS - 2 or left)
                elif left:
                    parts_lo(b, r + 1, 0, True)
            if not left:
                r = b * 8 + (PAIRS - 1)
                u_lo(r)
                add_audio(b, r, PAIRS - 1)

        batches(dve, body)


def relative_values(nc, m, scr, OT, ident):
    probs = m.sb("tprob_all", [TXT, B, 2, PAIRS * 2 * NQ], F16)
    window_f = m.sb("relv_window_f", [TXT, NQ, HD])
    window = [m.sb(f"relv_window_{s}", [TXT, NQ, 2, HD], F16) for s in "hl"]
    U = 4
    bank = m.ps("relv_bank", [P, U, 512])
    probs_loaded, window_loaded = m.sem("tprobs_loaded"), m.sem("relv_window_loaded")
    window_hi, window_lo = m.sem("relv_window_hi"), m.sem("relv_window_lo")
    rel_ready, rel_added = m.sem("relv_ready"), m.sem("relv_added")
    block = m.ctx.enter_context(nc.Block())

    @block.sync
    def _(sp):
        rows = scr["relv"]
        overlapping = bass.AP(tensor=rows.tensor, offset=rows.offset, ap=[[HD, TXT], [1, NQ * HD]])
        sp.dma_start(window_f[:, :, :].rearrange("j i d -> j (i d)"), overlapping).then_inc(window_loaded, 16)
        sp.dma_start(probs[:, :, :, :].rearrange("j b s f -> j b (s f)"), scr["pt"].rearrange("b j s f -> j b (s f)")).then_inc(probs_loaded, 16)

    @block.tensor
    def _(pe):
        pe.wait_ge(window_lo, 1)
        pe.wait_ge(probs_loaded, 16)

        def group(g, u):
            for v in range(2):
                at = 2 * u + v
                lhs = [w[:, bass.ds(g * (-2 * U) + (NQ - 1 - at), 1), :, :].rearrange("j o e d -> j (o e d)") for w in window]
                rhs = [probs[:, :, s, :].rearrange("j b (h i) -> j h b i", i=NQ)[:, :, :, bass.ds(g * (2 * U) + at, 1)].squeeze(3)
                       for s in range(2)]
                mm = mm3(pe, bank[:, u, v * 256:(v + 1) * 256], lhs, rhs)
            mm.then_inc(rel_ready, 1)

        for u in range(U):
            group(0, u)
        with pe.Fori(1, NQ // (2 * U)) as g:
            for u in range(U):
                pe.wait_ge(rel_added, g * U + (u + 1 - U))
                group(g, u)

    @block.scalar
    def _(act):
        act.wait_ge(window_loaded, 16)
        for e in range(2):
            split_hi(act, window[0][:, :, e, :], window_f[:, :, :], SW).then_inc(window_hi, 1)

    @block.vector
    def _(dve):
        for e in range(2):
            dve.wait_ge(window_hi, e + 1)
            ins = split_lo(dve, window[1][:, :, e, :], window_f[:, :, :], window[0][:, :, e, :], SW)
        ins.then_inc(window_lo, 1)

        with dve.Fori(0, NQ // (2 * U)) as g:
            for u in range(U):
                dve.wait_ge(rel_ready, g * U + (u + 1))
                for e in range(2):
                    h = slice(e * HD, (e + 1) * HD)
                    for v in range(2):
                        dst = OT[h, :, :].rearrange("d p (b i) -> d p b i", i=NQ)[:, :, :, bass.ds(g * (2 * U) + (2 * u + v), 1)].squeeze(3)
                        src = bank[h, u, v * 256:(v + 1) * 256].rearrange("d (p e b) -> d p e b", p=PAIRS, e=2)[:, :, e, :]
                        ins = dve.scalar_tensor_tensor(out=dst, in0=src, scalar=1 / (SP * SW), in1=dst, op0=ALU.mult, op1=ALU.add)
                ins.then_inc(rel_added, 1)


def cross_output(nc, m, a, OT, x):
    O = [m.sb(f"O_{s}", [P, PAIRS, T], F16) for s in "hl"]
    wo_f = m.sb("wo_f", [P, PAIRS, D])
    wo = [m.sb(f"wo_{s}", [P, PAIRS, D], F16) for s in "hl"]
    bo = m.sb("bo", [P, D])
    bank = m.ps("out_bank", [P, TT, 512])
    wo_loaded, bo_loaded = m.sem("wo_loaded"), m.sem("bo_loaded")
    wo_hi, wo_lo, o_hi, o_lo = m.sem("wo_hi"), m.sem("wo_lo"), m.sem("o_hi"), m.sem("o_lo")
    xb_ready, y_ready, x_ready = m.sem("xb_ready"), m.sem("y_ready"), m.sem("x1_ready")
    block = m.ctx.enter_context(nc.Block())

    @block.sync
    def _(sp):
        sp.dma_start(wo_f[:, :, :], a["Wo"].rearrange("(m p) n -> p m n", p=P)).then_inc(wo_loaded, 16)
        sp.dma_start(bo[:, :], a["bo"].rearrange("(o n) -> o n", o=1).broadcast_to([P, D])).then_inc(bo_loaded, 16)

    @block.gpsimd
    def _(pool):
        pool.wait_ge(bo_loaded, 16)
        pool.tensor_tensor(x[:, :, :], x[:, :, :], bo[:, :].unsqueeze(1).broadcast_to([P, TT, D]), ALU.add).then_inc(xb_ready, 1)

    @block.scalar
    def _(act):
        act.wait_ge(wo_loaded, 16)
        split_hi(act, wo[0][:, :, :], wo_f[:, :, :], SW).then_inc(wo_hi, 1)
        for h in range(4):
            c = slice(h * 256, (h + 1) * 256)
            split_hi(act, O[0][:, :, c], OT[:, :, c], SA).then_inc(o_hi, 1)

    @block.vector
    def _(dve):
        dve.wait_ge(wo_hi, 1)
        split_lo(dve, wo[1][:, :, :], wo_f[:, :, :], wo[0][:, :, :], SW).then_inc(wo_lo, 1)
        for h in range(4):
            c = slice(h * 256, (h + 1) * 256)
            dve.wait_ge(o_hi, h + 1)
            split_lo(dve, O[1][:, :, c], OT[:, :, c], O[0][:, :, c], SA).then_inc(o_lo, 1)
        dve.wait_ge(xb_ready, 1)
        for t in range(TT):
            dve.wait_ge(y_ready, t + 1)
            dve.scalar_tensor_tensor(out=x[:, t, :], in0=bank[:, t, 0:D], scalar=1 / (SA * SW), in1=x[:, t, :],
                                     op0=ALU.mult, op1=ALU.add).then_inc(x_ready, 1)

    @block.tensor
    def _(pe):
        pe.wait_ge(wo_lo, 1)
        for t in range(TT):
            pe.wait_ge(o_lo, t // 2 + 1)
            for k in range(PAIRS):
                mm = mm3(pe, bank[:, t, 0:D], [o[:, k, t * P:(t + 1) * P] for o in O], [w[:, k, :] for w in wo],
                         k == 0, k == PAIRS - 1)
            mm.then_inc(y_ready, 1)


class TurnedTokens:

    def __init__(self, m, name, bank):
        self.T = [m.sb(f"{name}_T{s}", [P, KD, T], F16) for s in "hl"]
        self.bank = bank
        self.ready, self.hi, self.lo = m.sem(name + "_turned"), m.sem(name + "_T_hi"), m.sem(name + "_T_lo")

    def tensor(self, pe, xn, xn_ready, ident):
        for g in range(TT // 2):
            pe.wait_ge(xn_ready, 2 * g + 2)
            for k in range(KD):
                for t in range(2):
                    at = (2 * k + t) * P
                    mm = pe.transpose(self.bank[:, g, at:at + P], xn[:, 2 * g + t, k * P:(k + 1) * P], ident[:, :])
            mm.then_inc(self.ready, 1)

    def io(self, g, s):
        return self.T[s][:, :, g * 2 * P:(g + 1) * 2 * P], self.bank[:, g, :].rearrange("p (k t) -> p k t", k=KD)

    def scalar(self, act):
        for g in range(TT // 2):
            act.wait_ge(self.ready, g + 1)
            split_hi(act, *self.io(g, 0), SA).then_inc(self.hi, 1)

    def vector(self, dve):
        for g in range(TT // 2):
            dve.wait_ge(self.hi, g + 1)
            dst, src = self.io(g, 1)
            split_lo(dve, dst, src, self.io(g, 0)[0], SA).then_inc(self.lo, 1)


def self_attention(nc, m, a, x, ident, used):
    SH, SHD, G = 16, D // 16, 8
    NG = SH // G
    AHEAD = 3
    AW = D * 3
    w_f = m.sb("w_attn_f", [P, KD, AW])
    w = [m.sb(f"w_attn_{s}", [P, KD, AW], F16) for s in "hl"]
    wp_f = m.sb("w_proj_f", [P, KD, D])
    wp = [m.sb(f"w_proj_{s}", [P, KD, D], F16) for s in "hl"]
    b_rows = m.sb("b_attn_rows", [4, P])
    b_cols = m.sb("b_attn_cols", [P, 4])
    b_v = m.sb("b_v", [P, D])
    b_p = m.sb("b_proj", [P, D])
    xn = m.sb("xn_b", [P, TT, D])
    qk = m.sb("qk_T", [P, 2 * NG, T])
    spread = m.sb("head_mask", [P, G])
    kd = [m.sb(f"k_diag{i}", [P, G, NQ]) for i in range(2 * AHEAD)]
    vd = m.sb("v_diag", [P, B, SH // 2, 2, SHD])
    pr = [m.sb(f"self_prob{i}", [P, G, NQ]) for i in range(AHEAD)]
    prT = [m.sb(f"self_probT{i}", [P, 4, P]) for i in range(2)]
    top, total = m.sb("self_max", [P, 2, G]), m.sb("self_sum", [P, 2, G])
    o_sb = m.sb("self_o", [P, TT, D])
    oT = [m.sb(f"self_oT_{s}", [P, KD, T], F16) for s in "hl"]
    bank = m.ps("self_bank", [P, 8, 512])

    norm = Norm(m, "norm_b")
    turned = TurnedTokens(m, "xn_b", bank)
    w_loaded, wp_loaded, b_loaded = m.sem("w_attn_loaded"), m.sem("w_proj_loaded"), m.sem("b_attn_loaded")
    bv_loaded, bp_loaded = m.sem("b_v_loaded"), m.sem("b_proj_loaded")
    w_hi, w_lo = m.sem("w_attn_hi"), m.sem("w_attn_lo")
    mask_ready = m.sem("head_mask_ready")
    vd_cleared = m.sem("v_diag_cleared")
    bias_turned, bias_ready = m.sem("b_attn_turned"), m.sem("b_attn_ready")
    qk_ready, qk_out = m.sem("qk_ready"), m.sem("qk_out")
    v_ready, v_out = m.sem("self_v_ready"), m.sem("self_v_out")
    kd_ready = m.sem("k_diag_ready")
    s_ready, top_ready, sub_ready, exp_ready = m.sem("self_s_ready"), m.sem("self_top_ready"), m.sem("self_sub_ready"), m.sem("self_exp_ready")
    sum_ready, rec_ready, p_ready = m.sem("self_sum_ready"), m.sem("self_rec_ready"), m.sem("self_p_ready")
    pT_ready, pT_out = m.sem("self_pT_ready"), m.sem("self_pT_out")
    o_ready, o_out = m.sem("self_o_ready"), m.sem("self_o_out")
    oT_ready, oT_hi, oT_lo = m.sem("self_oT_ready"), m.sem("self_oT_hi"), m.sem("self_oT_lo")
    xb_ready, y_ready, y_added = m.sem("xb2_ready"), m.sem("self_y_ready"), m.sem("x2_ready")
    block = m.ctx.enter_context(nc.Block())
    NQK = 2 * NG * 2
    S_BANK, T_BANK, O_BANK = (0, 1, 6), (2, 3), (4, 5)

    @block.sync
    def _(sp):
        sp.dma_start(w_f[:, :, :], weight_rows(a["w_attn"])).then_inc(w_loaded, 16)
        sp.dma_start(b_rows[:, :], a["b_attn"][0:2 * D].rearrange("(m p) -> m p", p=P)).then_inc(b_loaded, 16)
        sp.dma_start(b_v[:, :], a["b_attn"][2 * D:3 * D].rearrange("(o n) -> o n", o=1).broadcast_to([P, D])).then_inc(bv_loaded, 16)
        sp.dma_start(b_p[:, :], a["b_proj"].rearrange("(o n) -> o n", o=1).broadcast_to([P, D])).then_inc(bp_loaded, 16)
        sp.dma_start(wp_f[:, :, :], weight_rows(a["w_proj"])).then_inc(wp_loaded, 16)
        sp.sem_clear(range(min(s.num for s in used), max(s.num for s in used) + 1))

    @block.gpsimd
    def _(pool):
        norm.pool(pool)
        pool.memset(spread[:, :], 1.0).then_inc(mask_ready, 1)
        pool.wait_ge(mask_ready, 1)
        pool.affine_select(out=spread[:, :], in_=spread[:, :], compare_op=ALU.is_ge, fill=0.0, base=0,
                           pattern=[[-SHD, G]], channel_multiplier=1).then_inc(mask_ready, 1)
        pool.wait_ge(mask_ready, 2)
        pool.affine_select(out=spread[:, :], in_=spread[:, :], compare_op=ALU.is_ge, fill=0.0, base=SHD - 1,
                           pattern=[[SHD, G]], channel_multiplier=-1).then_inc(mask_ready, 1)
        pool.memset(vd[:, :, :, :, :], 0.0).then_inc(vd_cleared, 1)
        pool.wait_ge(mask_ready, 3)
        pool.wait_ge(qk_out, NQK)
        for u in range(TT * NG):
            t, g = divmod(u, NG)
            if u >= AHEAD:
                pool.wait_ge(s_ready, u - (AHEAD - 1))
            for e in range(2):
                k = qk[:, NG + g, (2 * t + e) * NQ:(2 * t + e + 1) * NQ]
                pool.tensor_tensor(kd[(2 * u + e) % (2 * AHEAD)][:, :, :], k.unsqueeze(1).broadcast_to([P, G, NQ]),
                                   spread[:, :].unsqueeze(2).broadcast_to([P, G, NQ]), ALU.mult).then_inc(kd_ready, 1)
            if u == 0:
                pool.wait_ge(norm.xn_ready, TT)
                pool.wait_ge(bp_loaded, 16)
                pool.tensor_tensor(x[:, :, :], x[:, :, :], b_p[:, :].unsqueeze(1).broadcast_to([P, TT, D]), ALU.add).then_inc(xb_ready, 1)

    @block.tensor
    def _(pe):
        turned.tensor(pe, xn, norm.xn_ready, ident)
        pe.wait_ge(b_loaded, 16)
        pe.transpose(bank[:, 4, 0:4], b_rows[:, :], ident[0:4, 0:4]).then_inc(bias_turned, 1)
        pe.wait_ge(turned.lo, TT // 2)
        pe.wait_ge(w_lo, 1)
        for job in range(NQK):
            c, n = divmod(job, 2)
            if job >= 3:
                pe.wait_ge(qk_out, job - 2)
            if job == 0:
                pe.wait_ge(bias_ready, 1)
            for k in range(KD):
                mm = mm3(pe, bank[:, 4 + job % 3, :], [x_[:, k, c * P:(c + 1) * P] for x_ in w],
                         [x_[:, k, n * 512:(n + 1) * 512] for x_ in turned.T], k == 0, k == KD - 1)
            mm.then_inc(qk_ready, 1)
        for b in range(B):
            if b >= 2:
                pe.wait_ge(v_out, b - 1)
            for e in range(2):
                for k in range(KD):
                    mm = mm3(pe, bank[e * NQ:(e + 1) * NQ, b % 2, 0:D], [x_[:, k, b * NQ:(b + 1) * NQ] for x_ in turned.T],
                             [x_[:, k, 2 * D:3 * D] for x_ in w], k == 0, k == KD - 1)
            mm.then_inc(v_ready, 1)

        def scores(u):
            t, g = divmod(u, NG)
            pe.wait_ge(kd_ready, 2 * u + 2)
            if u >= AHEAD:
                pe.wait_ge(sub_ready, u - (AHEAD - 1))
            for e in range(2):
                h = slice(e * NQ, (e + 1) * NQ)
                mm = pe.matmul(bank[h, S_BANK[u % AHEAD], :], qk[:, g, (2 * t + e) * NQ:(2 * t + e + 1) * NQ],
                               kd[(2 * u + e) % (2 * AHEAD)][:, :, :].rearrange("p h k -> p (h k)"), start=True, stop=True)
            mm.then_inc(s_ready, 1)

        def values(u):
            t, g = divmod(u, NG)
            pe.wait_ge(p_ready, u + 1)
            if u >= 2:
                pe.wait_ge(pT_out, u - 1)
            for c in range(4):
                mm = pe.transpose(bank[:, T_BANK[u % 2], c * P:(c + 1) * P],
                                  pr[u % AHEAD][:, 2 * c:2 * c + 2, :].rearrange("p h k -> p (h k)"), ident[:, :])
            mm.then_inc(pT_ready, 1)

        def outputs(u):
            t, g = divmod(u, NG)
            pe.wait_ge(pT_out, u + 1)
            if t >= 2:
                pe.wait_ge(o_out, t - 1)
            for e in range(2):
                h = slice(e * NQ, (e + 1) * NQ)
                for c in range(4):
                    pair = 4 * g + c
                    mm = pe.matmul(bank[h, O_BANK[t % 2], pair * 32:(pair + 1) * 32], prT[u % 2][:, c, h],
                                   vd[:, 2 * t + e, pair, :, :].rearrange("p e d -> p (e d)"), start=True, stop=True)
            mm.then_inc(o_ready, 1)

        pe.wait_ge(v_out, B)
        for u in range(AHEAD - 1):
            scores(u)
        for u in range(TT * NG):
            if u + AHEAD - 1 < TT * NG:
                scores(u + AHEAD - 1)
            values(u)
            if u:
                outputs(u - 1)
        outputs(TT * NG - 1)
        for t in range(TT):
            pe.wait_ge(o_out, t + 1)
            if t >= 2:
                pe.wait_ge(oT_lo, t - 1)
            for k in range(KD):
                mm = pe.transpose(bank[:, S_BANK[t % 2], k * P:(k + 1) * P], o_sb[:, t, k * P:(k + 1) * P], ident[:, :])
            mm.then_inc(oT_ready, 1)
        for t in range(TT):
            pe.wait_ge(oT_lo, t + 1)
            pe.wait_ge(w_lo, 2)
            if t >= 2:
                pe.wait_ge(y_added, t - 1)
            for k in range(KD):
                mm = mm3(pe, bank[:, 6 + t % 2, 0:D], [o[:, k, t * P:(t + 1) * P] for o in oT],
                         [x_[:, k, :] for x_ in wp], k == 0, k == KD - 1)
            mm.then_inc(y_ready, 1)

    @block.scalar
    def _(act):
        act.wait_ge(w_loaded, 16)
        split_hi(act, w[0][:, :, :], w_f[:, :, :], SW).then_inc(w_hi, 1)
        turned.scalar(act)
        act.wait_ge(bias_turned, 1)
        act.activation(b_cols[:, :], bank[:, 4, 0:4], ACT.Copy).then_inc(bias_ready, 1)
        act.wait_ge(bias_ready, 1)
        act.mul(b_cols[:, 0:NG], b_cols[:, 0:NG], SHD ** -0.5).then_inc(bias_ready, 1)
        act.wait_ge(bias_ready, 2)
        for job in range(NQK):
            c, n = divmod(job, 2)
            act.wait_ge(qk_ready, job + 1)
            scale = (SHD ** -0.5 if c < NG else 1.0) / (SA * SW)
            act.activation(qk[:, c, n * 512:(n + 1) * 512], bank[:, 4 + job % 3, :], ACT.Identity, bias=b_cols[:, c:c + 1],
                           scale=scale).then_inc(qk_out, 1)
        act.wait_ge(wp_loaded, 16)
        split_hi(act, wp[0][:, :, :], wp_f[:, :, :], SW).then_inc(w_hi, 1)
        def exponent(u):
            act.wait_ge(sub_ready, u + 1)
            act.activation(pr[u % AHEAD][:, :, :], pr[u % AHEAD][:, :, :], ACT.Exp).then_inc(exp_ready, 1)

        for u in range(AHEAD - 1):
            exponent(u)
        for u in range(TT * NG):
            t, g = divmod(u, NG)
            act.wait_ge(pT_ready, u + 1)
            if u >= 2:
                act.wait_ge(o_ready, u - 1)
            act.activation(prT[u % 2][:, :, :].rearrange("p c q -> p (c q)"), bank[:, T_BANK[u % 2], :], ACT.Copy).then_inc(pT_out, 1)
            if u + AHEAD - 1 < TT * NG:
                exponent(u + AHEAD - 1)
            if u >= 2 and g == 0:
                act.wait_ge(o_ready, u)
                act.activation(o_sb[:, t - 1, :], bank[:, O_BANK[(t - 1) % 2], 0:D], ACT.Copy).then_inc(o_out, 1)
        act.wait_ge(o_ready, TT * NG)
        act.activation(o_sb[:, TT - 1, :], bank[:, O_BANK[(TT - 1) % 2], 0:D], ACT.Copy).then_inc(o_out, 1)
        for t in range(TT):
            act.wait_ge(oT_ready, t + 1)
            split_hi(act, oT[0][:, :, t * P:(t + 1) * P], bank[:, S_BANK[t % 2], 0:D].rearrange("p (k q) -> p k q", k=KD), SA).then_inc(oT_hi, 1)

    @block.vector
    def _(dve):
        norm.vector(dve, xn, x)
        dve.wait_ge(w_hi, 1)
        split_lo(dve, w[1][:, :, :], w_f[:, :, :], w[0][:, :, :], SW).then_inc(w_lo, 1)
        turned.vector(dve)
        dve.wait_ge(vd_cleared, 1)
        dve.wait_ge(bv_loaded, 16)
        for b in range(B):
            dve.wait_ge(v_ready, b + 1)
            for e in range(2):
                h = slice(e * NQ, (e + 1) * NQ)
                src = bank[h, b % 2, 0:D].rearrange("p (c e d) -> p c e d", e=2, d=SHD)[:, :, e, :]
                bias = b_v[h, :].rearrange("p (c e d) -> p c e d", e=2, d=SHD)[:, :, e, :]
                ins = dve.scalar_tensor_tensor(out=vd[h, b, :, e, :], in0=src, scalar=1 / (SA * SW), in1=bias,
                                               op0=ALU.mult, op1=ALU.add)
            ins.then_inc(v_out, 1)
        dve.wait_ge(w_hi, 2)
        split_lo(dve, wp[1][:, :, :], wp_f[:, :, :], wp[0][:, :, :], SW).then_inc(w_lo, 1)

        def shift(u):
            s = bank[:, S_BANK[u % AHEAD], :].rearrange("p (h k) -> p h k", h=G)
            dve.wait_ge(s_ready, u + 1)
            dve.tensor_reduce(top[:, u % 2, :], s, X, ALU.max).then_inc(top_ready, 1)
            dve.wait_ge(top_ready, u + 1)
            if u >= AHEAD:
                dve.wait_ge(pT_ready, u - (AHEAD - 1))
            dve.tensor_tensor(pr[u % AHEAD][:, :, :], s, top[:, u % 2, :].unsqueeze(2).broadcast_to([P, G, NQ]), ALU.subtract).then_inc(sub_ready, 1)

        def scale(u):
            dve.wait_ge(exp_ready, u + 1)
            dve.tensor_reduce(total[:, u % 2, :], pr[u % AHEAD][:, :, :], X, ALU.add).then_inc(sum_ready, 1)
            dve.wait_ge(sum_ready, u + 1)
            dve.reciprocal(total[:, u % 2, :], total[:, u % 2, :]).then_inc(rec_ready, 1)
            dve.wait_ge(rec_ready, u + 1)
            dve.tensor_tensor(pr[u % AHEAD][:, :, :], pr[u % AHEAD][:, :, :], total[:, u % 2, :].unsqueeze(2).broadcast_to([P, G, NQ]),
                              ALU.mult).then_inc(p_ready, 1)

        for u in range(AHEAD - 1):
            shift(u)
        for u in range(TT * NG):
            scale(u)
            if u + AHEAD - 1 < TT * NG:
                shift(u + AHEAD - 1)
        for t in range(TT):
            dve.wait_ge(oT_hi, t + 1)
            io = [o[:, :, t * P:(t + 1) * P] for o in oT]
            split_lo(dve, io[1], bank[:, S_BANK[t % 2], 0:D].rearrange("p (k q) -> p k q", k=KD), io[0], SA).then_inc(oT_lo, 1)
        dve.wait_ge(xb_ready, 1)
        for t in range(TT):
            dve.wait_ge(y_ready, t + 1)
            dve.scalar_tensor_tensor(out=x[:, t, :], in0=bank[:, 6 + t % 2, 0:D], scalar=1 / (SA * SW), in1=x[:, t, :],
                                     op0=ALU.mult, op1=ALU.add).then_inc(y_added, 1)


def experts(nc, m, a, x, out, ident):
    E, HID, SHID = 8, 256, 512
    KH, KS = HID // P, SHID // P
    HALF = T // 2
    NU = 2 * E
    xn = m.sb("xn_c", [P, TT, D])
    gate_rows = m.sb("gate_rows", [E, D])
    gate = [m.sb(f"gate_{s}", [P, KD, E], F16) for s in "hl"]
    bias_rows = m.sb("bias_rows", [3 * E * KH, P])
    bias = m.sb("bias", [P, 3, E, KH])
    b1_now = [m.sb(f"b1_now{i}", [P, KH]) for i in range(2)]
    select = m.sb("select", [E, E, P], F16)
    before = m.sb("before", [P, E, E])
    gs = m.sb("gate_scores", [P, TT, E])
    gmax, gsum = m.sb("gate_max", [P, TT]), m.sb("gate_sum", [P, TT])
    above = m.sb("above", [P, TT, E, E])
    equal = m.sb("equal", [P, TT, E, E])
    rank = m.sb("rank", [P, TT, E])
    mask = m.sb("mask", [P, TT, E])
    wT = [m.sb(f"gate_T{s}", [E, T], F16) for s in "hl"]
    mT = m.sb("mask_T", [E, T], F16)
    WB = m.sb("weight_all", [P, E, T])
    MB = m.sb("mask_all", [P, E, T], F16)
    wf = [m.sb(f"expert_f{i}", [P, 3, KD, HID]) for i in range(2)]
    we = [[m.sb(f"expert_{s}{i}", [P, 3, KD, HID], F16) for s in "hl"] for i in range(2)]
    sf = m.sb("shared_f", [P, 3, 1024])
    ws = [m.sb(f"shared_w_{s}", [P, 3, 1024], F16) for s in "hl"]
    ta = [m.sb(f"ta{i}", [P, KH, HALF]) for i in range(2)]
    tb = [m.sb(f"tb{i}", [P, KH, HALF]) for i in range(2)]
    hT = [[m.sb(f"hT_{s}{i}", [P, KH, HALF], F16) for s in "hl"] for i in range(2)]
    acc = m.sb("acc", [P, KD, T])
    sg = m.sb("shared_prod", [P, KS, HALF])
    sh = [m.sb(f"shared_prod_{s}", [P, KS, HALF], F16) for s in "hl"]
    bank = m.ps("ffn_bank", [P, 8, 512])

    norm = Norm(m, "norm_c")
    turned = TurnedTokens(m, "xn_c", bank)
    gate_loaded, bias_loaded, shared_loaded = m.sem("gate_loaded"), m.sem("bias_loaded"), m.sem("shared_loaded")
    wf_loaded = [m.sem(f"expert_loaded{i}") for i in range(2)]
    consts = m.sem("select_before")
    rows_turned, bias_out, gate_hi, gate_lo = m.sem("rows_turned"), m.sem("bias_out"), m.sem("gate_hi"), m.sem("gate_lo")
    logits_ready, shifted, gexp_ready = m.sem("logits_ready"), m.sem("logits_shifted"), m.sem("gate_exp_ready")
    gstep = m.sem("gate_step")
    gates_ready, gT_ready, gT_hi, gT_lo, mT_out = m.sem("gates_ready"), m.sem("gate_T_ready"), m.sem("gate_T_hi"), m.sem("gate_T_lo"), m.sem("mask_T_out")
    wb_ready, mb_ready, wb_out, mb_out = m.sem("wb_ready"), m.sem("mb_ready"), m.sem("wb_out"), m.sem("mb_out")
    ws_turned, ws_hi, ws_lo = m.sem("shared_turned"), m.sem("shared_w_hi"), m.sem("shared_w_lo")
    sg_ready, sg_out, su_ready, su_out = m.sem("sg_ready"), m.sem("sg_out"), m.sem("su_ready"), m.sem("su_out")
    sh_hi, sh_lo, sz_ready, sz_out = m.sem("shared_h_hi"), m.sem("shared_h_lo"), m.sem("sz_ready"), m.sem("sz_out")
    b1_ready = m.sem("b1_now_ready")
    we_turned, we_hi, we_lo = m.sem("expert_turned"), m.sem("expert_w_hi"), m.sem("expert_w_lo")
    a_ready, ta_ready, h_ready, h_hi, h_lo = m.sem("a_ready"), m.sem("ta_ready"), m.sem("h_ready"), m.sem("h_hi"), m.sem("h_lo")
    b_ready, tb_ready, x3_ready = m.sem("b_ready"), m.sem("tb_ready"), m.sem("x3_ready")
    y_ready, yt_ready, acc_ready = m.sem("ffn_y_ready"), m.sem("yt_ready"), m.sem("acc_ready")
    fin_ready, fin_added, stored = m.sem("fin_ready"), m.sem("fin_added"), m.sem("out_stored")
    block = m.ctx.enter_context(nc.Block())
    names = ("w1", "w3", "w2")
    NT2 = 2 * E
    W_BANK, M_BANK = (0, 1, 2), (3, 6, 7)

    def units(eng, body):
        def pair(i, e, last):
            for v in range(4):
                body(i * 4 + v, e + v // 2, v % 2, v // 2, last and v == 3, last)
        with eng.Fori(0, E // 2 - 1) as i:
            pair(i, i * 2, False)
        pair(E // 2 - 1, E - 2, True)

    def next_of(e, half, parity):
        return (e, 1, parity) if half == 0 else (e + 1, 0, 1 - parity)

    @block.sync
    def _(sp):
        sp.dma_start(gate_rows[:, :], a["gate_w"]).then_inc(gate_loaded, 16)
        for n, b in enumerate(("b1", "b2", "b3")):
            sp.dma_start(bias_rows[n * E * KH:(n + 1) * E * KH, :], a[b].rearrange("e (k p) -> (e k) p", p=P)).then_inc(bias_loaded, 16)
        sp.dma_start(sf[:, 0, :].rearrange("p (j d) -> p j d", j=KS), a["sw1"].rearrange("(j p) d -> p j d", p=P)).then_inc(shared_loaded, 16)
        sp.dma_start(sf[:, 1, :].rearrange("p (j d) -> p j d", j=KS), a["sw2"].rearrange("(j p) d -> p j d", p=P)).then_inc(shared_loaded, 16)
        sp.dma_start(sf[:, 2, :].rearrange("p (k i) -> p k i", k=KD), a["sw3"].rearrange("(k p) i -> p k i", p=P)).then_inc(shared_loaded, 16)

        def load_expert(at, parity):
            for n, w in enumerate(names):
                flat = a[w].rearrange("e h d -> (e h d)")[bass.ds(at, HID * D)]
                sp.dma_start(wf[parity][:, n, :, :], flat.rearrange("(k p d) -> p k d", k=KH, p=P)).then_inc(wf_loaded[parity], 16)

        load_expert(0, 0)
        load_expert(HID * D, 1)

        def pair(i, last):
            for parity in range(2):
                if not last:
                    at = i * (2 * HID * D) + (parity + 2) * HID * D
                    at = at if isinstance(i, int) else sp.snap(at)
                    sp.wait_ge(we_lo, i * 6 + (3 * parity + 3))
                    load_expert(at, parity)

        with sp.Fori(0, E // 2 - 1) as i:
            pair(i, False)
        for t in range(TT):
            sp.wait_ge(fin_added, t + 1)
            sp.dma_start(out.rearrange("(t b) q d -> (b q) t d", b=2)[:, t, :], xn[:, t, :]).then_inc(stored, 16)
        sp.wait_ge(stored, 16 * TT)

    @block.gpsimd
    def _(pool):
        norm.pool(pool)
        pool.memset(select[:, :, :], 0.0).then_inc(consts, 1)
        pool.wait_ge(consts, 1)
        pool.affine_select(out=select[:, :, :], in_=select[:, :, :], compare_op=ALU.not_equal, fill=1.0, base=0,
                           pattern=[[-1, E], [0, P]], channel_multiplier=1).then_inc(consts, 1)
        pool.wait_ge(consts, 2)
        pool.memset(before[:, :, :], 1.0).then_inc(consts, 1)
        pool.wait_ge(consts, 3)
        pool.affine_select(out=before[:, :, :], in_=before[:, :, :], compare_op=ALU.is_gt, fill=0.0, base=0,
                           pattern=[[1, E], [-1, E]], channel_multiplier=0).then_inc(consts, 1)
        pool.wait_ge(sz_out, 2 * KD)

        def body(u, e, half, parity, very_last, last):
            at = acc[:, :, half * HALF:(half + 1) * HALF]
            pool.wait_ge(yt_ready, u + 1)
            pool.tensor_tensor(at, at, tb[half][:, :, :], ALU.add).then_inc(acc_ready, 1)

        units(pool, body)

    def shared_turn(job):
        n, half = divmod(job, 2)
        if n < 2:
            src = [sf[:, n, j * D + half * P:j * D + (half + 1) * P] for j in range(KS)]
        else:
            src = [sf[:, 2, k * SHID + j * P:k * SHID + (j + 1) * P] for j in (2 * half, 2 * half + 1) for k in range(KD)]
        return src, [w[:, n, half * 512:(half + 1) * 512] for w in ws]

    @block.tensor
    def _(pe):
        pe.wait_ge(bias_loaded, 48)
        pe.wait_ge(gate_loaded, 16)
        pe.transpose(bank[:, 4, 0:3 * E * KH], bias_rows[:, :], ident[0:3 * E * KH, 0:3 * E * KH])
        for k in range(KD):
            mm = pe.transpose(bank[:, 4, 64 + k * E:64 + (k + 1) * E], gate_rows[:, k * P:(k + 1) * P], ident[0:E, 0:E])
        mm.then_inc(rows_turned, 1)
        pe.wait_ge(shared_loaded, 48)
        for job in range(6):
            if job >= 3:
                pe.wait_ge(ws_lo, job - 2)
            for q, src in enumerate(shared_turn(job)[0]):
                mm = pe.transpose(bank[:, 5 + job % 3, q * P:(q + 1) * P], src, ident[:, :])
            mm.then_inc(ws_turned, 1)
        turned.tensor(pe, xn, norm.xn_ready, ident)
        pe.wait_ge(turned.lo, TT // 2)
        pe.wait_ge(gate_lo, 1)
        pe.wait_ge(bias_out, 2)
        for t in range(TT):
            for k in range(KD):
                mm = mm3(pe, bank[:, 4, t * E:(t + 1) * E], [x_[:, k, t * P:(t + 1) * P] for x_ in turned.T],
                         [g[:, k, :] for g in gate], k == 0, k == KD - 1)
        mm.then_inc(logits_ready, 1)
        pe.wait_ge(ws_lo, 6)
        for n in range(2):
            rhs = [[x_[:, k, n * HALF:(n + 1) * HALF] for x_ in turned.T] for k in range(KD)]
            for j in range(KS):
                at = n * KS + j
                if at >= 2:
                    pe.wait_ge(sg_out, at - 1)
                for k in range(KD):
                    mm = mm3(pe, bank[:, at % 2, :], [w[:, 0, k * SHID + j * P:k * SHID + (j + 1) * P] for w in ws], rhs[k],
                             k == 0, k == KD - 1)
                mm.then_inc(sg_ready, 1)
                if at >= 2:
                    pe.wait_ge(su_out, at - 1)
                for k in range(KD):
                    mm = mm3(pe, bank[:, 2 + at % 2, :], [w[:, 1, k * SHID + j * P:k * SHID + (j + 1) * P] for w in ws], rhs[k],
                             k == 0, k == KD - 1)
                mm.then_inc(su_ready, 1)
            for k in range(KD):
                if k == 0:
                    pe.wait_ge(sh_lo, KS * (n + 1))
                if n:
                    pe.wait_ge(sz_out, k + 1)
                for j in range(KS):
                    mm = mm3(pe, bank[:, 5 + k, :], [w[:, 2, j * D + k * P:j * D + (k + 1) * P] for w in ws],
                             [h[:, j, :] for h in sh], j == 0, j == KS - 1)
                mm.then_inc(sz_ready, 1)
        pe.wait_ge(gates_ready, 1)
        pe.wait_ge(sz_out, 2 * KD)
        for n, (src, at) in enumerate(((gs, 6), (mask, 4))):
            for t in range(TT):
                mm = pe.transpose(bank[0:E, at + t // 4, (t % 4) * P:(t % 4 + 1) * P], src[:, t, :], ident[:, :])
            mm.then_inc(gT_ready, 1)
        pe.wait_ge(gT_lo, 1)
        pe.wait_ge(mT_out, 1)
        pe.wait_ge(su_out, 2 * KS)
        for job in range(NT2):
            e, n = divmod(job, 2)
            if job >= 3:
                pe.wait_ge(wb_out, job - 2)
                pe.wait_ge(mb_out, job - 2)
            at = slice(n * HALF, (n + 1) * HALF)
            wb, mb = W_BANK[job % 3], M_BANK[job % 3]
            pe.matmul(bank[:, wb, :], select[:, e, :], wT[0][:, at], start=True, stop=False)
            pe.matmul(bank[:, wb, :], select[:, e, :], wT[1][:, at], start=False, stop=True).then_inc(wb_ready, 1)
            pe.matmul(bank[:, mb, :], select[:, e, :], mT[:, at], start=True, stop=True).then_inc(mb_ready, 1)

        def first_two(u, e, half, parity):
            for n, (at, free, ready) in enumerate(((0, ta_ready, a_ready), (2, tb_ready, b_ready))):
                if not isinstance(u, int) or u > 0:
                    pe.wait_ge(free, u)
                for c in range(KH):
                    for k in range(KD):
                        mm = mm3(pe, bank[:, at + c, :], [w[:, n, k, c * P:(c + 1) * P] for w in we[parity]],
                                 [x_[:, k, half * HALF:(half + 1) * HALF] for x_ in turned.T], k == 0, k == KD - 1)
                mm.then_inc(ready, 1)

        def last_one(u, half, parity):
            pe.wait_ge(h_lo, u + 1)
            if not isinstance(u, int) or u > 0:
                pe.wait_ge(yt_ready, u)
            for c in range(KD):
                for k in range(KH):
                    mm = mm3(pe, bank[:, 6 + c, :], [w[:, 2, k, c * P:(c + 1) * P] for w in we[parity]],
                             [h[:, k, :] for h in hT[half]], k == 0, k == KH - 1)
            mm.then_inc(y_ready, 1)

        def turn_weights(e, parity, which):
            for n in which:
                if not (isinstance(e, int) and e == 0 and n < 2):
                    pe.wait_ge(we_lo, e * 3 + (n - 1))
                for r in range(KD):
                    for c in range(2):
                        mm = pe.transpose(bank[:, 4 + (3 * parity + n) % 2, (2 * r + c) * P:(2 * r + c + 1) * P],
                                          wf[parity][:, n, c, r * P:(r + 1) * P], ident[:, :])
                mm.then_inc(we_turned, 1)

        pe.wait_ge(wf_loaded[0], 48)
        turn_weights(0, 0, (0, 1, 2))
        pe.wait_ge(wb_out, NT2)
        pe.wait_ge(mb_out, NT2)
        pe.wait_ge(we_lo, 3)
        first_two(0, 0, 0, 0)

        def body(u, e, half, parity, very_last, last):
            if not (last and parity == 1):
                if half == 0:
                    pe.wait_ge(wf_loaded[1 - parity], e * 24 + (72 if parity else 48))
                turn_weights(e + 1, 1 - parity, (0, 1) if half == 0 else (2,))
            if not very_last:
                ne, nhalf, nparity = next_of(e, half, parity)
                if nhalf == 0:
                    pe.wait_ge(we_lo, e * 3 + 5)
                first_two(u + 1, ne, nhalf, nparity)
            if half == 0:
                pe.wait_ge(we_lo, e * 3 + 3)
            last_one(u, half, parity)

        units(pe, body)
        pe.wait_ge(acc_ready, NU)
        for t in range(TT):
            for k in range(KD):
                mm = pe.transpose(bank[:, t, k * P:(k + 1) * P], acc[:, k, t * P:(t + 1) * P], ident[:, :])
            mm.then_inc(fin_ready, 1)

    @block.scalar
    def _(act):
        act.wait_ge(rows_turned, 1)
        act.activation(bias[:, :, :, :].rearrange("p n e k -> p (n e k)"), bank[:, 4, 0:3 * E * KH], ACT.Copy).then_inc(bias_out, 1)
        act.wait_ge(bias_out, 1)
        act.mul(bias[:, 1, :, :], bias[:, 1, :, :], SA * SW).then_inc(bias_out, 1)
        split_hi(act, gate[0][:, :, :], bank[:, 4, 64:64 + KD * E].rearrange("p (k e) -> p k e", k=KD), SW).then_inc(gate_hi, 1)
        for job in range(6):
            act.wait_ge(ws_turned, job + 1)
            split_hi(act, shared_turn(job)[1][0], bank[:, 5 + job % 3, :], SW).then_inc(ws_hi, 1)
        turned.scalar(act)
        act.wait_ge(shifted, 1)
        act.activation(gs[:, :, :], gs[:, :, :], ACT.Exp, scale=1 / (SA * SW)).then_inc(gexp_ready, 1)
        for n in range(2):
            for j in range(KS):
                at = n * KS + j
                act.wait_ge(sg_ready, at + 1)
                if n and j == 0:
                    act.wait_ge(sh_lo, KS)
                act.activation(sg[:, j, :], bank[:, at % 2, :], ACT.Silu, scale=1 / (SA * SW)).then_inc(sg_out, 1)
                act.wait_ge(su_out, at + 1)
                if n and j == 0:
                    act.wait_ge(sz_ready, KD)
                split_hi(act, sh[0][:, j, :], sg[:, j, :], SA).then_inc(sh_hi, 1)
            for k in range(KD):
                act.wait_ge(sz_ready, n * KD + k + 1)
                act.activation(acc[:, k, n * HALF:(n + 1) * HALF], bank[:, 5 + k, :], ACT.Copy, scale=1 / (SA * SW)).then_inc(sz_out, 1)
        act.wait_ge(gT_ready, 1)
        split_hi(act, wT[0][:, :], bank[0:E, 6:8, :].rearrange("p a b -> p (a b)"), SP).then_inc(gT_hi, 1)
        act.wait_ge(gT_ready, 2)
        act.activation(mT[:, :], bank[0:E, 4:6, :].rearrange("p a b -> p (a b)"), ACT.Copy).then_inc(mT_out, 1)
        for job in range(NT2):
            e, n = divmod(job, 2)
            act.wait_ge(wb_ready, job + 1)
            act.activation(WB[:, e, n * HALF:(n + 1) * HALF], bank[:, W_BANK[job % 3], :], ACT.Copy, scale=1 / (SP * SA * SW)).then_inc(wb_out, 1)

        def weights_hi(e, parity, which):
            src = bias[:, 0, e, :] if isinstance(e, int) else bias[:, 0, bass.ds(e, 1), :].squeeze(1)
            if 0 in which:
                act.activation(b1_now[parity][:, :], src, ACT.Copy).then_inc(b1_ready, 1)
            for n in which:
                act.wait_ge(we_turned, e * 3 + (n + 1))
                split_hi(act, we[parity][0][:, n, :, :], bank[:, 4 + (3 * parity + n) % 2, :].rearrange("p (k c) -> p k c", k=KD), SW).then_inc(we_hi, 1)

        def hidden(u, e, half, parity):
            if half == 0:
                act.wait_ge(b1_ready, e + 1)
            act.wait_ge(ta_ready, u + 1)
            for k in range(KH):
                ins = act.activation(ta[half][:, k, :], ta[half][:, k, :], ACT.Silu, bias=b1_now[parity][:, k:k + 1])
            ins.then_inc(h_ready, 1)
            act.wait_ge(h_ready, u + 1)
            split_hi(act, hT[half][0][:, :, :], ta[half][:, :, :], SA).then_inc(h_hi, 1)

        weights_hi(0, 0, (0, 1, 2))
        hidden(0, 0, 0, 0)

        def body(u, e, half, parity, very_last, last):
            if not (last and parity == 1):
                weights_hi(e + 1, 1 - parity, (0, 1) if half == 0 else (2,))
            if not very_last:
                hidden(u + 1, *next_of(e, half, parity))

        units(act, body)

    @block.vector
    def _(dve):
        norm.vector(dve, xn, x)
        dve.wait_ge(gate_hi, 1)
        split_lo(dve, gate[1][:, :, :], bank[:, 4, 64:64 + KD * E].rearrange("p (k e) -> p k e", k=KD), gate[0][:, :, :], SW).then_inc(gate_lo, 1)
        for job in range(6):
            dve.wait_ge(ws_hi, job + 1)
            dst = shared_turn(job)[1]
            split_lo(dve, dst[1], bank[:, 5 + job % 3, :], dst[0], SW).then_inc(ws_lo, 1)
        turned.vector(dve)
        logits = bank[:, 4, 0:TT * E].rearrange("p (t e) -> p t e", t=TT)
        by_token = lambda v: v.unsqueeze(2).broadcast_to([P, TT, E])
        dve.wait_ge(logits_ready, 1)
        dve.tensor_reduce(gmax[:, :], logits, X, ALU.max).then_inc(gstep, 1)
        dve.wait_ge(gstep, 1)
        dve.tensor_tensor(gs[:, :, :], logits, by_token(gmax[:, :]), ALU.subtract).then_inc(shifted, 1)
        dve.wait_ge(gexp_ready, 1)
        dve.tensor_reduce(gsum[:, :], gs[:, :, :], X, ALU.add).then_inc(gstep, 1)
        dve.wait_ge(gstep, 2)
        dve.reciprocal(gsum[:, :], gsum[:, :]).then_inc(gstep, 1)
        dve.wait_ge(gstep, 3)
        dve.tensor_tensor(gs[:, :, :], gs[:, :, :], by_token(gsum[:, :]), ALU.mult).then_inc(gstep, 1)
        dve.wait_ge(gstep, 4)
        dve.wait_ge(consts, 4)
        for t in range(TT):
            own = gs[:, t, :].unsqueeze(2).broadcast_to([P, E, E])
            other = gs[:, t, :].unsqueeze(1).broadcast_to([P, E, E])
            dve.tensor_tensor(above[:, t, :, :], other, own, ALU.is_gt)
            dve.tensor_tensor(equal[:, t, :, :], other, own, ALU.is_equal).then_inc(gstep, 1)
        dve.wait_ge(gstep, 4 + TT)
        dve.tensor_tensor(equal[:, :, :, :].rearrange("p t e j -> p t (e j)"), equal[:, :, :, :].rearrange("p t e j -> p t (e j)"),
                          before[:, :, :].rearrange("p e j -> p (e j)").unsqueeze(1).broadcast_to([P, TT, E * E]), ALU.mult).then_inc(gstep, 1)
        dve.wait_ge(gstep, 5 + TT)
        dve.tensor_tensor(above[:, :, :, :].rearrange("p t e j -> p (t e j)"), above[:, :, :, :].rearrange("p t e j -> p (t e j)"),
                          equal[:, :, :, :].rearrange("p t e j -> p (t e j)"), ALU.add).then_inc(gstep, 1)
        dve.wait_ge(gstep, 6 + TT)
        dve.tensor_reduce(rank[:, :, :], above[:, :, :, :], X, ALU.add).then_inc(gstep, 1)
        dve.wait_ge(gstep, 7 + TT)
        dve.tensor_scalar(mask[:, :, :], rank[:, :, :], 1.5, None, ALU.is_lt).then_inc(gstep, 1)
        dve.wait_ge(gstep, 8 + TT)
        dve.tensor_tensor(gs[:, :, :], gs[:, :, :], mask[:, :, :], ALU.mult).then_inc(gates_ready, 1)
        for n in range(2):
            for j in range(KS):
                at = n * KS + j
                dve.wait_ge(su_ready, at + 1)
                dve.wait_ge(sg_out, at + 1)
                dve.scalar_tensor_tensor(out=sg[:, j, :], in0=bank[:, 2 + at % 2, :], scalar=1 / (SA * SW), in1=sg[:, j, :],
                                         op0=ALU.mult, op1=ALU.mult).then_inc(su_out, 1)
                dve.wait_ge(sh_hi, at + 1)
                split_lo(dve, sh[1][:, j, :], sg[:, j, :], sh[0][:, j, :], SA).then_inc(sh_lo, 1)
        dve.wait_ge(gT_hi, 1)
        split_lo(dve, wT[1][:, :], bank[0:E, 6:8, :].rearrange("p a b -> p (a b)"), wT[0][:, :], SP).then_inc(gT_lo, 1)
        for job in range(NT2):
            e, n = divmod(job, 2)
            dve.wait_ge(mb_ready, job + 1)
            dve.tensor_scalar(MB[:, e, n * HALF:(n + 1) * HALF], bank[:, M_BANK[job % 3], :], 1 / (SA * SW), None, ALU.mult).then_inc(mb_out, 1)

        def weights_lo(e, parity, which):
            for n in which:
                dve.wait_ge(we_hi, e * 3 + (n + 1))
                split_lo(dve, we[parity][1][:, n, :, :], bank[:, 4 + (3 * parity + n) % 2, :].rearrange("p (k c) -> p k c", k=KD),
                         we[parity][0][:, n, :, :], SW).then_inc(we_lo, 1)

        def at_tokens(tile, e, half):
            t = tile[:, e, half * HALF:(half + 1) * HALF].unsqueeze(1) if isinstance(e, int) else \
                tile[:, bass.ds(e, 1), half * HALF:(half + 1) * HALF]
            return t.broadcast_to([P, KH, HALF])

        def column(n, e, k):
            return bias[:, n, e, k:k + 1] if isinstance(e, int) else bias[:, n, bass.ds(e, 1), k]

        def weigh(u, e, half, first):
            dve.wait_ge(a_ready, u + 1)
            dve.tensor_tensor(ta[half][:, :, :], bank[:, 0:2, :], at_tokens(WB, e, half), ALU.mult).then_inc(ta_ready, 1)
            dve.wait_ge(b_ready, u + 1)
            if not first:
                dve.wait_ge(acc_ready, u - 1)
            dve.tensor_tensor(tb[half][:, :, :], bank[:, 2:4, :], at_tokens(WB, e, half), ALU.mult).then_inc(tb_ready, 1)
            dve.wait_ge(tb_ready, u + 1)
            for k in range(KH):
                m_at = MB[:, e, half * HALF:(half + 1) * HALF] if isinstance(e, int) else \
                    MB[:, bass.ds(e, 1), half * HALF:(half + 1) * HALF].squeeze(1)
                ins = dve.scalar_tensor_tensor(out=tb[half][:, k, :], in0=tb[half][:, k, :], scalar=column(2, e, k), in1=m_at,
                                               op0=ALU.add, op1=ALU.mult)
            ins.then_inc(x3_ready, 1)
            dve.wait_ge(h_hi, u + 1)
            split_lo(dve, hT[half][1][:, :, :], ta[half][:, :, :], hT[half][0][:, :, :], SA).then_inc(h_lo, 1)

        weights_lo(0, 0, (0, 1, 2))
        weigh(0, 0, 0, True)

        def body(u, e, half, parity, very_last, last):
            if not (last and parity == 1):
                weights_lo(e + 1, 1 - parity, (0, 1) if half == 0 else (2,))
            if not very_last:
                ne, nhalf, _ = next_of(e, half, parity)
                weigh(u + 1, ne, nhalf, False)
            dve.wait_ge(y_ready, u + 1)
            dve.wait_ge(x3_ready, u + 1)
            for k in range(KD):
                ins = dve.scalar_tensor_tensor(out=tb[half][:, k, :], in0=bank[:, 6 + k, :], scalar=column(1, e, k),
                                               in1=tb[half][:, k, :], op0=ALU.add, op1=ALU.mult)
            ins.then_inc(yt_ready, 1)

        units(dve, body)
        for t in range(TT):
            dve.wait_ge(fin_ready, t + 1)
            dve.tensor_tensor(xn[:, t, :], bank[:, t, 0:D], x[:, t, :], ALU.add).then_inc(fin_added, 1)


INPUTS = {"x": "x", "ctx": "ctx_1024", "Wq": "L0_xattn_Wq", "Wk": "L0_xattn_Wk", "Wv": "L0_xattn_Wv",
          "Wk_ip": "L0_xattn_Wk_ip", "Wv_ip": "L0_xattn_Wv_ip", "Wk_ap": "L0_xattn_Wk_ap", "Wv_ap": "L0_xattn_Wv_ap",
          "Wo": "L0_xattn_Wo", "bo": "L0_xattn_bo", "rel_k": "L0_xattn_rel_k", "rel_v": "L0_xattn_rel_v",
          "alpha": "L0_xattn_alpha", "beta": "L0_xattn_beta", "w_attn": "L0_attn_w_attn", "b_attn": "L0_attn_b_attn",
          "w_proj": "L0_attn_w_proj", "b_proj": "L0_attn_b_proj", "gate_w": "L0_ffn_gate_w", "w1": "L0_ffn_w1",
          "b1": "L0_ffn_b1", "w2": "L0_ffn_w2", "b2": "L0_ffn_b2", "w3": "L0_ffn_w3", "b3": "L0_ffn_b3",
          "sw1": "L0_ffn_sw1", "sw2": "L0_ffn_sw2", "sw3": "L0_ffn_sw3"}


def perceiver_layer(nc, a, out):
    scr = {
        "kt": nc.dram_tensor("kt_scratch", [B, P, 2 * PAIRS * TI], F16).ap(),
        "v": nc.dram_tensor("v_scratch", [B * TI, 2 * INNER], F16).ap(),
        "R": nc.dram_tensor("rel_scratch", [B, TXT, PAIRS * 2 * NQ], F32).ap(),
        "relv": nc.dram_tensor("relv_scratch", [EXT, HD], F32).ap(),
        "pt": nc.dram_tensor("prob_scratch", [B, TXT, 2, PAIRS * 2 * NQ], F16).ap(),
    }
    with ExitStack() as whole:
        m = Mem(nc, whole)
        ident = m.sb("ident", [P, P])
        x = m.sb("x_res", [P, TT, D])

        used = []

        def phase(f, *args):
            with ExitStack() as ctx:
                m = Mem(nc, ctx)
                f(nc, m, *args)
                used.extend(m.sems)

        with ExitStack() as attending:
            keep = Mem(nc, attending)
            qT = [keep.sb(f"qT_{s}", [P, PAIRS, T], F16) for s in "hl"]
            rel_k = ExtendedRows(keep, "relk", a["rel_k"], 2)
            rel_v = ExtendedRows(keep, "relv", a["rel_v"], 1)
            phase(project, a, scr, x, qT, rel_k, rel_v, ident)
            OT = keep.sb("OT", [P, PAIRS, T])
            with ExitStack() as streaming:
                s = Mem(nc, streaming)
                audio, context = AudioWeights(s), AudioContext(s, a["ctx"])
                phase(relative_scores, a, scr, qT, rel_k, rel_v, audio, context.load_first, ident)
                phase(cross_attention, scr, qT, OT, audio, context, ident)
            phase(relative_values, scr, OT, ident)
            phase(cross_output, a, OT, x)
        phase(self_attention, a, x, ident, used)
        phase(experts, a, x, out, ident)


def kernel(**inputs):
    import concourse.bacc as bacc
    from concourse.bass_utils import run_bass_kernel_spmd

    nc = bacc.Bacc("TRN2", target_bir_lowering=False, num_devices=1)
    arrays, a = {}, {}
    for name, key in INPUTS.items():
        v = np.ascontiguousarray(inputs[key])
        v = v.reshape(1) if v.ndim == 0 else v
        arrays["in_" + name] = v
        a[name] = nc.dram_tensor("in_" + name, v.shape, mybir.dt.from_np(v.dtype), kind="ExternalInput").ap()
    out = nc.dram_tensor("out_x", [B, NQ, D], F32, kind="ExternalOutput").ap()
    perceiver_layer(nc, a, out)
    r = run_bass_kernel_spmd(nc, [arrays], core_ids=[0])
    return r.results[0]["out_x"]
```

```python
from contextlib import ExitStack

import numpy as np
import concourse.bass as bass
from concourse import mybir
from concourse.alu_op_type import AluOpType as ALU

F32 = mybir.dt.float32
F16 = mybir.dt.float16
ACT = mybir.ActivationFunctionType
X = mybir.AxisListType.X

P = 128
B, NQ, D = 16, 64, 256
T = B * NQ
TT = T // P
KD = D // P
H, HD = 16, 64
INNER = H * HD
PAIRS = H // 2
TXT, IMG, CTX = 77, 16, 1601
TI = TXT + IMG
AUD = CTX - TI
NCH = -(-AUD // P)
TAIL = AUD - (NCH - 1) * P
SB = 3
MAXREL = 16
NREL = 2 * MAXREL + 1
EXT = NQ + TXT - 1
REL0 = NQ - 1 - MAXREL
SCALE = HD ** -0.5
SA, SW, SP = 16.0, 256.0, 4096.0
EPS = 1e-5


def mm3(pe, out, lhs, rhs, first=True, last=True):
    (lh, ll), (rh, rl) = lhs, rhs
    pe.matmul(out, lh, rh, start=first, stop=False)
    pe.matmul(out, lh, rl, start=False, stop=False)
    return pe.matmul(out, ll, rh, start=False, stop=last)


def split_hi(act, hi, src, scale):
    return act.activation(hi, src, ACT.Copy, scale=scale)


def split_lo(dve, lo, src, hi, scale):
    return dve.scalar_tensor_tensor(out=lo, in0=src, scalar=scale, in1=hi, op0=ALU.mult, op1=ALU.subtract)


def split_hi_in_place(act, hi, src, scale, scaled):
    act.activation(src, src, ACT.Copy, scale=scale).then_inc(scaled[0], 1)
    act.wait_ge(*scaled)
    return act.activation(hi, src, ACT.Copy)


class Mem:

    def __init__(self, nc, ctx):
        self.nc, self.ctx, self.sems = nc, ctx, []

    def sb(self, name, shape, dt=F32):
        return self.ctx.enter_context(self.nc.sbuf_tensor(name, shape, dt))

    def ps(self, name, shape, dt=F32):
        return self.ctx.enter_context(self.nc.psum_tensor(name, shape, dt))

    def sem(self, name):
        handle = self.ctx.enter_context(self.nc.semaphore(name))
        self.sems.append(handle)
        return handle


def make_identity(pool, ident, made):
    pool.memset(ident, 0.0).then_inc(made, 1)
    pool.wait_ge(made, 1)
    pool.affine_select(out=ident, in_=ident, compare_op=ALU.not_equal, fill=1.0, base=0,
                       pattern=[[-1, ident.shape[1]]], channel_multiplier=1).then_inc(made, 1)


class Norm:

    def __init__(self, m, name):
        self.stats = m.sb(name + "_stats", [P, TT, 6])
        self.mean_var = m.sb(name + "_mean_var", [P, TT, 2])
        self.rstd = m.sb(name + "_rstd", [P, TT])
        self.power = m.sb(name + "_power", [P, TT])
        self.stats_ready = m.sem(name + "_stats_ready")
        self.moments_ready = m.sem(name + "_moments_ready")
        self.rstd_ready = m.sem(name + "_rstd_ready")
        self.xn_ready = m.sem(name + "_xn_ready")

    def pool(self, pool):
        pool.memset(self.power[:, :], -0.5).then_inc(self.rstd_ready, 1)
        pool.wait_ge(self.moments_ready, TT)
        pool.tensor_scalar(self.rstd[:, :], self.mean_var[:, :, 1], EPS, None, ALU.add).then_inc(self.rstd_ready, 1)
        pool.wait_ge(self.rstd_ready, 2)
        pool.tensor_tensor(self.rstd[:, :], self.rstd[:, :], self.power[:, :], ALU.pow).then_inc(self.rstd_ready, 1)

    def tile_statistics(self, dve, x, t):
        dve.bn_stats(self.stats[:, t, :], x[:, t, :]).then_inc(self.stats_ready, 1)

    def moments(self, dve):
        for t in range(TT):
            dve.wait_ge(self.stats_ready, t + 1)
            dve.bn_aggr(self.mean_var[:, t, :], self.stats[:, t, :]).then_inc(self.moments_ready, 1)

    def normalize(self, dve, xn, x):
        dve.wait_ge(self.rstd_ready, 3)
        for t in range(TT):
            dve.tensor_scalar(xn[:, t, :], x[:, t, :], self.mean_var[:, t, 0:1], self.rstd[:, t:t + 1],
                              ALU.subtract, ALU.mult).then_inc(self.xn_ready, 1)


def weight_rows(w):
    return w.rearrange("(k p) n -> p k n", p=P)


def project(nc, m, a, scr, x, qT, rel_k, rel_v, ident):
    xn = m.sb("xn_a", [P, TT, D])
    xnT = [m.sb(f"xnT_a{s}", [P, KD, T], F16) for s in "hl"]
    ctx_ti = m.sb("ctx_ti", [TI, B, D])
    txtT = [m.sb(f"txtT_{s}", [P, KD, B, TXT], F16) for s in "hl"]
    imgT = [m.sb(f"imgT_{s}", [P, KD, B, IMG], F16) for s in "hl"]
    staged = [m.sb(f"staged{i}", [P, KD, INNER]) for i in range(2)]
    names = ["Wq", "Wk", "Wk_ip", "Wv", "Wv_ip"]
    W = {n: [m.sb(f"{n}_{s}", [P, KD, INNER], F16) for s in "hl"] for n in names}
    VB = 4
    KT = m.sb("KT", [P, B, 2, PAIRS, TI], F16)
    v_out = [m.sb(f"v_out{i}", [P, 2, INNER], F16) for i in range(VB)]
    bank = m.ps("bank_a", [P, 8, 512])

    norm = Norm(m, "norm_a")
    ident_made = m.sem("ident_a_made")
    x_loaded = m.sem("x_a_loaded")
    ctx_loaded = m.sem("ctx_ti_loaded")
    w_loaded = {n: m.sem(f"{n}_loaded") for n in names}
    w_hi = m.sem("w_hi")
    w_lo = m.sem("w_lo")
    w_scaled = m.sem("w_scaled")
    job_ready = m.sem("job_a_ready")
    job_hi = m.sem("job_a_hi")
    job_lo = m.sem("job_a_lo")
    v_stored = [m.sem(f"v_stored{i}") for i in range(VB)]
    kt_stored = m.sem("kt_stored")

    XN, CT, Q, K = 0, TT // 2, TT // 2 + B // 2, TT // 2 + B // 2 + 2 * PAIRS
    G = 4
    NK = B // G + 1
    V = K + NK * PAIRS
    v_chunks = [("Wv", txtT, c * P, min(P, B * TXT - c * P)) for c in range(-(-B * TXT // P))]
    v_chunks += [("Wv_ip", imgT, c * P, P) for c in range(B * IMG // P)]

    block = m.ctx.enter_context(nc.Block())

    @block.sync
    def _(sp):
        sp.dma_start(x[:, :, :], a["x"].rearrange("(t b) q d -> (b q) t d", b=2)).then_inc(x_loaded, 16)
        for n, name in enumerate(names):
            if n >= 2:
                sp.wait_ge(w_lo, n - 1)
            sp.dma_start(staged[n % 2][:, :, :], weight_rows(a[name])).then_inc(w_loaded[name], 16)
            if n == 0:
                sp.dma_start(ctx_ti[:, :, :], a["ctx"][:, 0:TI, :].rearrange("b j d -> j b d")).then_inc(ctx_loaded, 16)
            if n == 1:
                rel_k.load(sp)
                rel_v.load(sp)
        HALF = PAIRS // 2
        for half in range(2):
            sp.wait_ge(job_hi, K + (half + 1) * HALF * NK)
            sp.wait_ge(job_lo, K + (half + 1) * HALF * NK)
            for s in range(2):
                dst = scr["kt"].rearrange("b p (s m j) -> p b s m j", s=2, m=PAIRS)[:, :, s, half * HALF:(half + 1) * HALF, :]
                sp.dma_start(dst, KT[:, :, s, half * HALF:(half + 1) * HALF, :]).then_inc(kt_stored, 16)
        row = 0
        for c, (_, _, _, n) in enumerate(v_chunks):
            sp.wait_ge(job_lo, V + 2 * c + 2)
            sp.dma_start(scr["v"][row:row + n, :], v_out[c % VB][0:n, :, :].rearrange("p s n -> p (s n)")).then_inc(v_stored[c % VB], 16)
            row += n
        for i in range(VB):
            sp.wait_ge(v_stored[i], 16 * (len(v_chunks) // VB))
        sp.wait_ge(kt_stored, 64)

    @block.gpsimd
    def _(pool):
        make_identity(pool, ident[:, :], ident_made)
        norm.pool(pool)
        for n in range(1, len(names)):
            pool.wait_ge(w_lo, n)
            pool.wait_ge(w_hi, n + 1)
            pool.tensor_tensor(W[names[n]][1][:, :, :], staged[n % 2][:, :, :], W[names[n]][0][:, :, :], ALU.subtract).then_inc(w_lo, 1)

    def xn_dst(s, g):
        return xnT[s][:, :, g * 2 * P:(g + 1) * 2 * P]

    def ctx_job(g):
        src = bank[:, (CT + g) % 8, 0:4 * TI].rearrange("p (k b j) -> p k b j", k=KD, b=2)
        return src[:, :, :, 0:TXT], src[:, :, :, TXT:TI]

    @block.tensor
    def _(pe):
        pe.wait_ge(ident_made, 2)
        for g in range(TT // 2):
            pe.wait_ge(norm.xn_ready, 2 * g + 2)
            for k in range(KD):
                for t in range(2):
                    at = (2 * k + t) * P
                    mm = pe.transpose(bank[:, XN + g, at:at + P], xn[:, 2 * g + t, k * P:(k + 1) * P], ident[:, :])
            mm.then_inc(job_ready, 1)
        pe.wait_ge(ctx_loaded, 16)
        for g in range(B // 2):
            if CT + g >= 8:
                pe.wait_ge(job_lo, CT + g - 7)
            for k in range(KD):
                for b in range(2):
                    at = (2 * k + b) * TI
                    mm = pe.transpose(bank[:, (CT + g) % 8, at:at + TI], ctx_ti[:, 2 * g + b, k * P:(k + 1) * P],
                                      ident[0:TI, 0:TI])
            mm.then_inc(job_ready, 1)
        pe.wait_ge(w_lo, 1)
        pe.wait_ge(w_hi, 1)
        with pe.Fori(0, PAIRS // 4) as i:
            for u in range(4):
                for n in range(2):
                    job = Q + 2 * u + n
                    pe.wait_ge(job_lo, i * 8 + (job - 7))
                    for k in range(KD):
                        lhs = [w[:, k, bass.ds(i * (4 * P) + u * P, P)] for w in W["Wq"]]
                        rhs = [x_[:, k, n * 512:(n + 1) * 512] for x_ in xnT]
                        mm = mm3(pe, bank[:, job % 8, :], lhs, rhs, k == 0, k == KD - 1)
                    mm.then_inc(job_ready, 1)
        pe.wait_ge(w_lo, 3)
        pe.wait_ge(w_hi, 3)
        with pe.Fori(0, PAIRS) as i:
            for n in range(NK):
                pe.wait_ge(job_lo, i * NK + (K + n - NK + 1))
                name, src = ("Wk", txtT) if n < NK - 1 else ("Wk_ip", imgT)
                for k in range(KD):
                    lhs = [w[:, k, bass.ds(i * P, P)] for w in W[name]]
                    rhs = [(s[:, k, n * G:(n + 1) * G, :] if n < NK - 1 else s[:, k, :, :]).rearrange("p b j -> p (b j)") for s in src]
                    mm = mm3(pe, bank[:, (n + 4) % 8, 0:rhs[0].shape[1]], lhs, rhs, k == 0, k == KD - 1)
                mm.then_inc(job_ready, 1)
        pe.wait_ge(w_lo, 5)
        pe.wait_ge(w_hi, 5)
        for c, (name, src, at, rows) in enumerate(v_chunks):
            for n in range(2):
                job = V + 2 * c + n
                pe.wait_ge(job_lo, job - 4)
                for k in range(KD):
                    lhs = [s[:, k, :, :].rearrange("p b j -> p (b j)")[:, at:at + rows] for s in src]
                    rhs = [w[:, k, n * 512:(n + 1) * 512] for w in W[name]]
                    mm = mm3(pe, bank[0:rows, (4 + (job - V) % 5) % 8, :], lhs, rhs, k == 0, k == KD - 1)
                mm.then_inc(job_ready, 1)

    @block.scalar
    def _(act):
        def hi(job, dst, src, scale):
            act.wait_ge(job_ready, job)
            split_hi(act, dst, src, scale).then_inc(job_hi, 1)

        def weight(n):
            act.wait_ge(w_loaded[names[n]], 16)
            split_hi_in_place(act, W[names[n]][0][:, :, :], staged[n % 2][:, :, :], SW, (w_scaled, n + 1)).then_inc(w_hi, 1)

        weight(0)
        for g in range(TT // 2):
            hi(XN + g + 1, xn_dst(0, g), bank[:, XN + g, :].rearrange("p (k t) -> p k t", k=KD), SA)
        for g in range(B // 2):
            act.wait_ge(job_ready, CT + g + 1)
            txt, img = ctx_job(g)
            split_hi(act, txtT[0][:, :, 2 * g:2 * g + 2, :], txt, SA)
            split_hi(act, imgT[0][:, :, 2 * g:2 * g + 2, :], img, SA).then_inc(job_hi, 1)
        weight(1)
        for pair in range(PAIRS):
            if pair in (PAIRS // 4, PAIRS * 5 // 8):
                weight(2 if pair == PAIRS // 4 else 3)
            for n in range(2):
                job = Q + 2 * pair + n
                hi(job + 1, qT[0][:, pair, n * 512:(n + 1) * 512], bank[:, job % 8, :], SCALE * SA / (SA * SW))
        weight(4)
        with act.Fori(0, PAIRS) as i:
            for n in range(NK):
                src, dst = (bank[:, (n + 4) % 8, 0:G * TXT], KT[:, n * G:(n + 1) * G, 0, :, 0:TXT]) if n < NK - 1 else \
                    (bank[:, (n + 4) % 8, 0:B * IMG], KT[:, :, 0, :, TXT:TI])
                hi(i * NK + (K + n + 1), dst[:, :, bass.ds(i, 1), :].squeeze(2), src.rearrange("p (b j) -> p b j", j=dst.shape[3]),
                   SA / (SA * SW))
        for c, (_, _, _, rows) in enumerate(v_chunks):
            if c >= VB:
                act.wait_ge(v_stored[c % VB], 16 * (c // VB))
            for n in range(2):
                job = V + 2 * c + n
                hi(job + 1, v_out[c % VB][0:rows, 0, n * 512:(n + 1) * 512], bank[0:rows, (4 + (job - V) % 5) % 8, :], SA / (SA * SW))

    @block.vector
    def _(dve):
        def lo(job, dst, src, hi_, scale):
            dve.wait_ge(job_hi, job)
            split_lo(dve, dst, src, hi_, scale).then_inc(job_lo, 1)

        dve.wait_ge(x_loaded, 16)
        for t in range(TT):
            norm.tile_statistics(dve, x, t)
        norm.moments(dve)
        norm.normalize(dve, xn, x)
        dve.wait_ge(w_hi, 1)
        dve.tensor_tensor(W[names[0]][1][:, :, :], staged[0][:, :, :], W[names[0]][0][:, :, :], ALU.subtract).then_inc(w_lo, 1)
        for g in range(TT // 2):
            lo(XN + g + 1, xn_dst(1, g), bank[:, XN + g, :].rearrange("p (k t) -> p k t", k=KD), xn_dst(0, g), SA)
        for g in range(B // 2):
            dve.wait_ge(job_hi, CT + g + 1)
            for k in range(KD):
                for part, (src, dst) in enumerate(zip(ctx_job(g), (txtT, imgT))):
                    io = [s[:, k, 2 * g:2 * g + 2, :] for s in dst]
                    ins = split_lo(dve, io[1], src[:, k, :, :], io[0], SA)
            ins.then_inc(job_lo, 1)
        with dve.Fori(0, PAIRS // 4) as i:
            for u in range(4):
                for n in range(2):
                    job = Q + 2 * u + n
                    dst = [q[:, bass.ds(i * 4 + u, 1), n * 512:(n + 1) * 512] for q in qT]
                    lo(i * 8 + (job + 1), dst[1], bank[:, job % 8, :].unsqueeze(1), dst[0], SCALE * SA / (SA * SW))
        with dve.Fori(0, PAIRS) as i:
            for n in range(NK):
                if n < NK - 1:
                    src, dst = bank[:, (n + 4) % 8, 0:G * TXT], [KT[:, n * G:(n + 1) * G, s, :, 0:TXT] for s in range(2)]
                else:
                    src, dst = bank[:, (n + 4) % 8, 0:B * IMG], [KT[:, :, s, :, TXT:TI] for s in range(2)]
                dst = [d[:, :, bass.ds(i, 1), :].squeeze(2) for d in dst]
                lo(i * NK + (K + n + 1), dst[1], src.rearrange("p (b j) -> p b j", j=dst[0].shape[2]), dst[0], SA / (SA * SW))
        for c, (_, _, _, rows) in enumerate(v_chunks):
            if c >= VB:
                dve.wait_ge(v_stored[c % VB], 16 * (c // VB))
            for n in range(2):
                job = V + 2 * c + n
                io = [v_out[c % VB][0:rows, s, n * 512:(n + 1) * 512] for s in range(2)]
                lo(job + 1, io[1], bank[0:rows, (4 + (job - V) % 5) % 8, :], io[0], SA / (SA * SW))


class ExtendedRows:

    def __init__(self, m, name, source, copies):
        self.tiles = [m.sb(name + "_rows0", [P, copies, HD]), m.sb(name + "_rows1", [EXT - P, copies, HD])]
        self.loaded = m.sem(name + "_rows_loaded")
        parts = [(0, REL0, source[0:1, :]), (REL0, NREL, source[:, :]), (REL0 + NREL, EXT - REL0 - NREL, source[NREL - 1:NREL, :])]
        self.transfers = []
        for first, n, rows in parts:
            for tile, low, high in ((self.tiles[0], 0, P), (self.tiles[1], P, EXT)):
                start, end = max(first, low), min(first + n, high)
                if start < end:
                    src = rows.broadcast_to([end - start, HD]) if rows.shape[0] == 1 else rows[start - first:end - first, :]
                    self.transfers += [(tile[start - low:end - low, c, :], src) for c in range(copies)]
        self.loads = 16 * len(self.transfers)

    def load(self, sp):
        for dst, src in self.transfers:
            sp.dma_start(dst, src).then_inc(self.loaded, 16)


class AudioWeights:

    def __init__(self, m):
        self.wkT = [m.sb(f"wkT_{n}", [P, PAIRS, D], F16) for n in "hl"]
        self.wv = [m.sb(f"wv_{n}", [P, KD, INNER], F16) for n in "hl"]
        self.gains = m.sb("gains", [P, 2])


class AudioWeightsWork:

    def __init__(self, m, audio, bank):
        self.to, self.bank = audio, bank
        self.wk_f = m.sb("wk_ap_f", [P, KD, INNER])
        self.wv_f = m.sb("wv_ap_f", [P, KD, INNER])
        self.wk_loaded, self.wv_loaded, self.ab_loaded = m.sem("wk_ap_loaded"), m.sem("wv_ap_loaded"), m.sem("alpha_beta_loaded")
        self.turned, self.wk_hi, self.wk_lo = m.sem("wkT_turned"), m.sem("wkT_hi"), m.sem("wkT_lo")
        self.wv_hi, self.wv_lo = m.sem("wv_ap_hi"), m.sem("wv_ap_lo")
        self.tanh_ready, self.gain_ready = m.sem("tanh_ready"), m.sem("gain_ready")

    def sync(self, sp, a):
        sp.dma_start(self.wv_f[:, :, :], weight_rows(a["Wv_ap"])).then_inc(self.wv_loaded, 16)
        sp.dma_start(self.wk_f[:, :, :], weight_rows(a["Wk_ap"])).then_inc(self.wk_loaded, 16)
        for n, name in enumerate(("alpha", "beta")):
            sp.dma_start(self.to.gains[:, n:n + 1], a[name].rearrange("(a b) -> a b", a=1).broadcast_to([P, 1])).then_inc(self.ab_loaded, 16)

    def job(self, g):
        return self.bank[:, g, :].rearrange("p (m d) -> p m d", m=2), [w[:, 2 * g:2 * g + 2, :] for w in self.to.wkT]

    def tensor(self, pe, ident):
        pe.wait_ge(self.wk_loaded, 16)
        for g in range(PAIRS // 2):
            for u in range(2):
                for k in range(KD):
                    mm = pe.transpose(self.bank[:, g, (2 * u + k) * P:(2 * u + k + 1) * P],
                                      self.wk_f[:, k, (2 * g + u) * P:(2 * g + u + 1) * P], ident[:, :])
            mm.then_inc(self.turned, 1)

    def scalar(self, act):
        act.wait_ge(self.wv_loaded, 16)
        split_hi(act, self.to.wv[0][:, :, :], self.wv_f[:, :, :], SW).then_inc(self.wv_hi, 1)
        for g in range(PAIRS // 2):
            act.wait_ge(self.turned, g + 1)
            src, dst = self.job(g)
            split_hi(act, dst[0], src, SW).then_inc(self.wk_hi, 1)
        act.wait_ge(self.ab_loaded, 32)
        act.activation(self.to.gains[:, :], self.to.gains[:, :], ACT.Tanh).then_inc(self.tanh_ready, 1)

    def vector(self, dve):
        dve.wait_ge(self.wv_hi, 1)
        split_lo(dve, self.to.wv[1][:, :, :], self.wv_f[:, :, :], self.to.wv[0][:, :, :], SW).then_inc(self.wv_lo, 1)
        for g in range(PAIRS // 2):
            dve.wait_ge(self.wk_hi, g + 1)
            src, dst = self.job(g)
            split_lo(dve, dst[1], src, dst[0], SW).then_inc(self.wk_lo, 1)
        dve.wait_ge(self.tanh_ready, 1)
        gains = self.to.gains
        dve.tensor_scalar(gains[:, 0:1], gains[:, 0:1], 1.0, None, ALU.add)
        dve.tensor_scalar(gains[:, 1:2], gains[:, 1:2], 1.0, 1 / (SP * SA), ALU.add, ALU.mult).then_inc(self.gain_ready, 1)


class AudioContext:

    def __init__(self, m, ctx):
        self.nat = m.sb("ctx_nat", [P, NCH, D])
        self.loaded = m.sem("nat_loaded")
        self.ctx = ctx.rearrange("b j d -> (b j d)")

    def load(self, sp, at, tail_at):
        sp.dma_start(self.nat[:, 0:NCH - 1, :], self.ctx[bass.ds(at, (NCH - 1) * P * D)].rearrange("(p c d) -> p c d", p=P, d=D)).then_inc(self.loaded, 16)
        sp.dma_start(self.nat[0:TAIL, NCH - 1, :], self.ctx[bass.ds(tail_at, TAIL * D)].rearrange("(p d) -> p d", p=TAIL)).then_inc(self.loaded, 16)

    def load_first(self, sp):
        self.load(sp, TI * D, TI * D + (NCH - 1) * P * D)


def relative_scores(nc, m, a, scr, qT, OT, rel_k, rel_v, audio, first_load, ident):
    ext = rel_k.tiles
    table = [[m.sb(f"relk_table_{s}{e}", [P, EXT], F16) for e in range(2)] for s in "hl"]
    HI = NQ // 2
    R = [m.sb(f"R{i}", [TXT, B * PAIRS, 2, HI]) for i in range(2)]
    tbank = m.ps("relk_bank", [P, 512])
    bank = m.ps("R_bank", [P, 4, 512])
    relv_stored = m.sem("relv_ext_stored")
    zeroed = m.sem("relk_zeroed")
    turned = m.sem("relk_turned")
    table_hi = m.sem("relk_table_hi")
    table_lo = m.sem("relk_table_lo")
    even_ready, odd_ready = m.sem("R_even_ready"), m.sem("R_odd_ready")
    even_out, odd_out = m.sem("R_even_out"), m.sem("R_odd_out")
    r_stored = m.sem("R_stored")
    U = 4
    work = AudioWeightsWork(m, audio, bank)

    block = m.ctx.enter_context(nc.Block())

    @block.sync
    def _(sp):
        work.sync(sp, a)
        first_load(sp)
        sp.wait_ge(rel_v.loaded, rel_v.loads)
        sp.dma_start(scr["relv"][0:P, :], rel_v.tiles[0][:, 0, :]).then_inc(relv_stored, 16)
        sp.dma_start(scr["relv"][P:EXT, :], rel_v.tiles[1][:, 0, :]).then_inc(relv_stored, 16)
        for half in range(2):
            sp.wait_ge(even_out, (half + 1) * HI // U)
            sp.wait_ge(odd_out, (half + 1) * HI // U)
            sp.dma_start(scr["R"][:, :, half, :].rearrange("b j f -> j b f"),
                         R[half][:, :, :, :].rearrange("j (b p) e i -> j b (p e i)", b=B)).then_inc(r_stored, 16)
        sp.wait_ge(relv_stored, 32)
        sp.wait_ge(r_stored, 32)

    @block.gpsimd
    def _(pool):
        for e in range(2):
            for s in range(2):
                pool.memset(table[s][e][:, :], 0.0).then_inc(zeroed, 1)
        pool.memset(OT[:, :, :], 0.0)

    @block.tensor
    def _(pe):
        pe.wait_ge(rel_k.loaded, rel_k.loads)
        pe.transpose(tbank[:, 0:P], ext[0][:, :, :].rearrange("r e d -> r (e d)"), ident[:, :])
        pe.transpose(tbank[:, P:EXT], ext[1][:, :, :].rearrange("r e d -> r (e d)"), ident[0:EXT - P, 0:EXT - P]).then_inc(turned, 1)
        pe.wait_ge(table_lo, 2)

        def group(g, u):
            for e, ready in ((0, even_ready), (1, odd_ready)):
                for v in range(U):
                    i = g * (2 * U) + U * u + v
                    lhs = [t[e][:, NQ - 1 - i:NQ - 1 - i + TXT] for t in table]
                    rhs = [q[:, :, :].rearrange("d p (b i) -> d b p i", i=NQ)[:, :, :, i] for q in qT]
                    mm = mm3(pe, bank[0:TXT, 2 * u + e, v * P:(v + 1) * P], lhs, rhs)
                mm.then_inc(ready, 1)

        for g in range(NQ // (2 * U)):
            for u in range(2):
                if g:
                    pe.wait_ge(even_out, g * 2 + (u - 1))
                    pe.wait_ge(odd_out, g * 2 + (u - 1))
                group(g, u)
        pe.wait_ge(even_out, NQ // U)
        pe.wait_ge(odd_out, NQ // U)
        work.tensor(pe, ident)

    def R_at(half, g, u, e):
        return R[half][:, :, e, bass.ds(g * (2 * U) + U * u, U)].rearrange("j q i -> j i q")

    GH = HI // (2 * U)

    def bank_of(u, e):
        return bank[0:TXT, 2 * u + e, :].rearrange("j (i q) -> j i q", i=U)

    @block.scalar
    def _(act):
        act.wait_ge(zeroed, 4)
        act.wait_ge(turned, 1)
        for e in range(2):
            h = slice(e * HD, (e + 1) * HD)
            split_hi(act, table[0][e][h, :], tbank[h, 0:EXT], SA).then_inc(table_hi, 1)
        for half in range(2):
            with act.Fori(0, GH) as g:
                for u in range(2):
                    act.wait_ge(even_ready, g * 2 + (half * 2 * GH + u + 1))
                    act.activation(R_at(half, g, u, 0), bank_of(u, 0), ACT.Copy, scale=1 / (SA * SA)).then_inc(even_out, 1)
        work.scalar(act)

    @block.vector
    def _(dve):
        for e in range(2):
            h = slice(e * HD, (e + 1) * HD)
            dve.wait_ge(table_hi, 2)
            split_lo(dve, table[1][e][h, :], tbank[h, 0:EXT], table[0][e][h, :], SA).then_inc(table_lo, 1)
        for half in range(2):
            with dve.Fori(0, GH) as g:
                for u in range(2):
                    dve.wait_ge(odd_ready, g * 2 + (half * 2 * GH + u + 1))
                    dve.tensor_scalar(R_at(half, g, u, 1), bank_of(u, 1), 1 / (SA * SA), None, ALU.mult).then_inc(odd_out, 1)
        work.vector(dve)


def cross_attention(nc, m, scr, qT, OT, audio, context, ident):
    NPREP = NCH // 2
    wkT, wv, gains = audio.wkT, audio.wv, audio.gains
    nat, nat_loaded = context.nat, context.loaded
    ctx_s = [[m.sb(f"ctx_{s}{i}", [P, NCH, D], F16) for s in "hl"] for i in range(2)]
    ctxT = [[m.sb(f"ctxT_{s}{i}", [P, KD, NCH * P], F16) for s in "hl"] for i in range(2)]
    qf = [m.sb(f"q_fold_{s}", [P, KD, PAIRS, P], F16) for s in "hl"]
    prob = m.sb("prob", [P, AUD])
    PT = [m.sb(f"probT_{s}", [P, NCH, P], F16) for s in "hl"]
    BD = [[m.sb(f"q_diag_{s}{i}", [P, PAIRS, P], F16) for s in "hl"] for i in range(2)]
    u_sb = m.sb("u_sb", [P, D])
    UT = [m.sb(f"uT_{s}", [P, KD, P], F16) for s in "hl"]
    maxes = m.sb("maxes", [P, SB])
    top = m.sb("top", [P, 1])
    negmax = m.sb("negmax", [P, 1])
    den = m.sb("den", [P, 2])
    rden = m.sb("rden", [P, 1])
    KTb = m.sb("KT_b", [P, 2, PAIRS, TI], F16)
    Vb = m.sb("V_b", [TI, 2, INNER], F16)
    Rb = m.sb("R_b", [TI, 2 * 512])
    ST = m.sb("ST", [TI, 512])
    tprob = m.sb("tprob", [P, 4, TI])
    tmax = m.sb("tmax", [P, 2, 4])
    tsum = m.sb("tsum", [P, 2, 4])
    PTt = [m.sb(f"tprobT_{s}", [TI, 2, 512], F16) for s in "hl"]
    S = m.ps("S", [P, SB, 512])
    PTb = m.ps("PT_bank", [P, 2, 512])
    Ub = m.ps("U_bank", [P, 512])
    M0 = m.ps("M0", [P, 512])
    M1 = m.ps("M1", [P, 512])

    kt_loaded, v_loaded, r_loaded = m.sem("kt_loaded"), m.sem("v_loaded"), m.sem("r_loaded")
    pt_stored = m.sem("tprob_stored")
    zeroed = m.sem("zeroed")
    bd_ready = m.sem("q_diag_ready")
    scores_ready = m.sem("scores_ready")
    maxes_ready = m.sem("maxes_ready")
    top_ready = m.sem("top_ready")
    negmax_ready = m.sem("negmax_ready")
    prob_ready = m.sem("prob_ready")
    pt_ready, pt_hi, pt_lo = m.sem("pt_ready"), m.sem("pt_hi"), m.sem("pt_lo")
    u_ready, rden_ready, u_normed = m.sem("u_ready"), m.sem("rden_ready"), m.sem("u_normed")
    ut_ready, ut_hi, ut_lo = m.sem("ut_ready"), m.sem("ut_hi"), m.sem("ut_lo")
    proj_ready = m.sem("proj_ready")
    ot_added = m.sem("ot_added")
    fold_ready, fold_hi, fold_lo = m.sem("fold_ready"), m.sem("fold_hi"), m.sem("fold_lo")
    ctxt_ready, ctxt_hi, ctxt_lo = m.sem("ctxt_ready"), m.sem("ctxt_hi"), m.sem("ctxt_lo")
    csplit_hi, csplit_lo = m.sem("csplit_hi"), m.sem("csplit_lo")
    text_ready = m.sem("text_ready")
    text_added = m.sem("text_added")
    st_ready = m.sem("st_ready")
    tmax_ready, ts_ready, te_ready = m.sem("tmax_ready"), m.sem("ts_ready"), m.sem("te_ready")
    tsum_ready, trec_ready, tgain_ready, tp_ready = m.sem("tsum_ready"), m.sem("trec_ready"), m.sem("tgain_ready"), m.sem("tp_ready")
    ptt_hi, ptt_lo = m.sem("ptt_hi"), m.sem("ptt_lo")

    block = m.ctx.enter_context(nc.Block())
    MAIN = (NCH - 1) * P

    def rows_of(c):
        return TAIL if c == NCH - 1 else P

    def width(n):
        return min(512, AUD - 512 * n)

    def batches(eng, body):
        with eng.Fori(0, B // 2 - 1) as j:
            body(j * 2, 0, B)
            body(j * 2 + 1, 1, B)
        body(B - 2, 0, 1)
        body(B - 1, 1, 0)

    first_banks = [S[:, 0, :], S[:, 1, :], S[:, 2, :], PTb[:, 0, :], PTb[:, 1, :], M1]
    fold_banks = [M0, Ub, PTb[:, 0, :], PTb[:, 1, :], M1]

    @block.sync
    def _(sp):
        def flat(t, offset, n):
            whole = t.rearrange(" ".join("abcd"[:len(t.shape)]) + " -> (" + " ".join("abcd"[:len(t.shape)]) + ")")
            return whole[bass.ds(offset, n)]

        def load_kt(at):
            sp.dma_start(KTb[:, :, :, :].rearrange("p s m j -> p (s m j)"),
                         flat(scr["kt"], at, P * KT_ROW).rearrange("(p f) -> p f", p=P)).then_inc(kt_loaded, 16)

        def load_r(at):
            for half in range(2):
                rows = flat(scr["R"], at, TXT * 1024).rearrange("(j s h i) -> j s h i", j=TXT, s=2, h=H)
                dst = Rb[0:TXT, :].rearrange("j (h s i) -> j s h i", h=H, s=2)
                sp.dma_start(dst[:, half, :, :], rows[:, half, :, :]).then_inc(r_loaded, 16)

        def load_v(text_at, image_at):
            v = Vb[:, :, :].rearrange("j s n -> j (s n)")
            sp.dma_start(v[0:TXT, :], flat(scr["v"], text_at, TXT * V_ROW).rearrange("(j f) -> j f", j=TXT)).then_inc(v_loaded, 16)
            sp.dma_start(v[TXT:TI, :], flat(scr["v"], image_at, IMG * V_ROW).rearrange("(j f) -> j f", j=IMG)).then_inc(v_loaded, 16)

        V_ROW, KT_ROW = 2 * INNER, 2 * PAIRS * TI
        V_IMG = B * TXT * V_ROW
        NAT0 = TI * D
        load_kt(0)
        sp.wait_ge(zeroed, 1)
        load_r(0)
        load_v(0, V_IMG)
        sp.wait_ge(ctxt_ready, NPREP)
        sp.wait_ge(csplit_lo, NPREP)
        context.load(sp, NAT0 + CTX * D, NAT0 + (CTX + MAIN) * D)

        def body(b, parity, left):
            fixed = (lambda v: v) if isinstance(b, int) else sp.snap
            nat_at = fixed(b * (CTX * D) + (NAT0 + 2 * CTX * D))
            nat_tail_at = fixed(b * (CTX * D) + (NAT0 + 2 * CTX * D + MAIN * D))
            kt_at = fixed(b * (P * KT_ROW) + P * KT_ROW)
            r_at = fixed(b * (TXT * 1024) + TXT * 1024)
            vt_at = fixed(b * (TXT * V_ROW) + TXT * V_ROW)
            vi_at = fixed(b * (IMG * V_ROW) + (V_IMG + IMG * V_ROW))
            pt_at = fixed(b * (TXT * 2048))
            kt_read, v_read = fixed(b * 8 + 5), fixed(b * 8 + 8)
            r_read, prepared, stored = fixed(b * 2 + 2), fixed((b + 2) * NPREP), fixed((b + 1) * 32)
            if left:
                sp.wait_ge(text_ready, kt_read)
                load_kt(kt_at)
                sp.wait_ge(st_ready, r_read)
                load_r(r_at)
            if left > 1:
                sp.wait_ge(ctxt_ready, prepared)
                sp.wait_ge(csplit_lo, prepared)
                context.load(sp, nat_at, nat_tail_at)
            sp.wait_ge(text_ready, v_read)
            for s in range(2):
                sp.dma_start(flat(scr["pt"], pt_at, TXT * 2048).rearrange("(j s f) -> j s f", j=TXT, s=2)[:, s, :],
                             PTt[s][0:TXT, :, :].rearrange("j h f -> j (h f)")).then_inc(pt_stored, 16)
            if left:
                sp.wait_ge(pt_stored, stored)
                load_v(vt_at, vi_at)

        batches(sp, body)
        sp.wait_ge(pt_stored, B * 32)

    @block.gpsimd
    def _(pool):
        pool.memset(Rb[64:TI, :], 0.0).then_inc(zeroed, 1)
        pool.wait_ge(zeroed, 1)
        for i in range(2):
            for s in range(2):
                pool.memset(BD[i][s][:, :, :], 0.0).then_inc(zeroed, 1)

        def diagonal(b, parity):
            for s in range(2):
                for e in range(2):
                    h = slice(e * HD, (e + 1) * HD)
                    pool.tensor_copy(BD[parity][s][h, :, h], qT[s][h, :, bass.ds(b * NQ, NQ)]).then_inc(bd_ready, 1)
                    pool.wait_ge(bd_ready, b * 4 + (2 * s + e + 1))

        pool.wait_ge(zeroed, 5)
        pool.wait_ge(bd_ready, 4)
        diagonal(1, 1)

        def body(b, parity, left):
            if left > 1:
                pool.wait_ge(text_ready, b * 8 + 5)
                diagonal(b + 2, parity)

        batches(pool, body)

    @block.tensor
    def _(pe):
        def scores(r, p, parity, n):
            for k in range(KD):
                lhs = [q[:, k, p, :] for q in qf]
                rhs = [c[:, k, n * 512:n * 512 + width(n)] for c in ctxT[parity]]
                mm = mm3(pe, S[:, n, 0:width(n)], lhs, rhs, k == 0, k == KD - 1)
            mm.then_inc(scores_ready, 1)

        def turn_prob(r, j):
            for c in range(4 * j, 4 * j + 4):
                mm = pe.transpose(PTb[0:rows_of(c), j % 2, (c % 4) * P:(c % 4 + 1) * P],
                                  prob[:, c * P:c * P + rows_of(c)], ident[:, :])
            mm.then_inc(pt_ready, 1)

        def prob_ctx(r, parity, j):
            pe.wait_ge(pt_lo, r * 3 + (j + 1))
            for c in range(4 * j, 4 * j + 4):
                n = rows_of(c)
                mm = mm3(pe, Ub[:, 0:D], [t[0:n, c, :] for t in PT], [x[0:n, c, :] for x in ctx_s[parity]],
                         c == 0, c == NCH - 1)
            if j == 2:
                mm.then_inc(u_ready, 1)

        def turn_u(r):
            pe.wait_ge(u_normed, r + 1)
            for k in range(KD):
                mm = pe.transpose(M0[:, k * P:(k + 1) * P], u_sb[:, k * P:(k + 1) * P], ident[:, :])
            mm.then_inc(ut_ready, 1)

        def project_u(r, p):
            pe.wait_ge(ut_lo, r + 1)
            for k in range(KD):
                mm = mm3(pe, M0[:, 0:P], [w[:, k, p * P:(p + 1) * P] for w in wv], [u[:, k, :] for u in UT],
                         k == 0, k == KD - 1)
            mm.then_inc(proj_ready, 1)

        def fold(p, parity, bank=M0):
            for k in range(KD):
                mm = mm3(pe, bank[:, k * P:(k + 1) * P], [w[:, p, k * P:(k + 1) * P] for w in wkT],
                         [q[:, p, :] for q in BD[parity]])
            mm.then_inc(fold_ready, 1)

        def turn_ctx(j, bank=M1):
            for u in range(2):
                n = rows_of(2 * j + u)
                for k in range(KD):
                    at = (2 * k + u) * P
                    mm = pe.transpose(bank[:, at:at + n], nat[0:n, 2 * j + u, k * P:(k + 1) * P], ident[0:n, 0:n])
            mm.then_inc(ctxt_ready, 1)

        def text(b, p, parity):
            half, stage = divmod(p, 4)
            if stage == 0:
                if half == 0:
                    pe.wait_ge(kt_loaded, (b + 1) * 16)
                for q in range(4):
                    mm = mm3(pe, M1[0:TI, q * P:(q + 1) * P], [KTb[:, s, 4 * half + q, :] for s in range(2)],
                             [BD[parity][s][:, 4 * half + q, :] for s in range(2)])
            elif stage == 1:
                pe.wait_ge(st_ready, b * 2 + (half + 1))
                for q in range(4):
                    mm = pe.transpose(M1[:, q * TI:(q + 1) * TI], ST[:, q * P:(q + 1) * P], ident[0:TI, 0:TI])
            elif stage == 2:
                pe.wait_ge(tp_ready, b * 2 + (half + 1))
                for q in range(4):
                    mm = pe.transpose(M1[0:TI, q * P:(q + 1) * P], tprob[:, q, :], ident[:, :])
            else:
                pe.wait_ge(ptt_lo, b * 2 + (half + 1))
                if half == 0:
                    pe.wait_ge(v_loaded, (b + 1) * 32)
                for q in range(4):
                    at = (4 * half + q) * P
                    mm = mm3(pe, M1[:, q * P:(q + 1) * P], [Vb[:, s, at:at + P] for s in range(2)],
                             [t[:, half, q * P:(q + 1) * P] for t in PTt])
            mm.then_inc(text_ready, 1)

        def text_bank_free(b, p):
            half, stage = divmod(p - 1, 4)
            if p == 0:
                pe.wait_ge(text_added, b * 2 + 1)
            elif stage == 3:
                pe.wait_ge(text_added, b * 2 + (half + 2))
            else:
                pe.wait_ge((st_ready, ts_ready, ptt_lo)[stage], b * 2 + (half + 1))

        for j in range(NPREP):
            if j == 0:
                pe.wait_ge(nat_loaded, 32)
            turn_ctx(j, first_banks[j])
        pe.wait_ge(bd_ready, 4)
        for p in range(PAIRS):
            if 2 <= p < len(fold_banks):
                pe.wait_ge(ctxt_lo, p + 2)
            elif p >= len(fold_banks):
                pe.wait_ge(fold_lo, p + 1 - len(fold_banks))
            fold(p, 0, fold_banks[p % len(fold_banks)])
        pe.wait_ge(ctxt_lo, NPREP)
        pe.wait_ge(fold_lo, 1)
        for n in range(SB):
            scores(0, 0, 0, n)
        pe.wait_ge(fold_lo, PAIRS)

        def turn_and_score(b, r, p, parity, left):
            follows = p < PAIRS - 1 or left
            np_, npar = (p + 1, parity) if p < PAIRS - 1 else (0, 1 - parity)

            def next_scores(n):
                if follows:
                    if p == PAIRS - 1:
                        pe.wait_ge(ctxt_lo, (b + 1) * NPREP + (2 * n + 2))
                    scores(r + 1, np_, npar, n)

            pe.wait_ge(prob_ready, r + 1)
            turn_prob(r, 0)
            turn_prob(r, 1)
            next_scores(0)
            if b is not None:
                if left:
                    pe.wait_ge(fold_lo, (b + 1) * 8 + (p or PAIRS))
                else:
                    pe.wait_ge(ot_added, r)
                turn_u(r - 1)
            pe.wait_ge(pt_lo, r * 3 + 1)
            turn_prob(r, 2)
            next_scores(1)
            if b is not None:
                project_u(r - 1, (p - 1) % PAIRS)
            next_scores(2)

        turn_and_score(None, 0, 0, 0, True)

        def body(b, parity, left):
            for p in range(PAIRS):
                r = b * 8 + p
                text_bank_free(b, p)
                if left and 1 <= p <= NPREP:
                    if p == 1:
                        pe.wait_ge(nat_loaded, (b + 2) * 32)
                    turn_ctx(p - 1)
                if p == 0:
                    pe.wait_ge(csplit_lo, (b + 1) * NPREP)
                prob_ctx(r, parity, 0)
                if left:
                    if p == 0:
                        pe.wait_ge(bd_ready, (b + 2) * 4)
                    pe.wait_ge(ot_added, r + 1)
                    fold(p, 1 - parity)
                prob_ctx(r, parity, 1)
                prob_ctx(r, parity, 2)
                if left and 1 <= p <= NPREP:
                    pe.wait_ge(ctxt_lo, (b + 1) * NPREP + p)
                text(b, p, parity)
                if p < PAIRS - 1:
                    turn_and_score(b, r + 1, p + 1, parity, left)
                elif left:
                    turn_and_score(b, r + 1, 0, 1 - parity, left)
            if not left:
                r = b * 8 + (PAIRS - 1)
                pe.wait_ge(ot_added, r + 1)
                turn_u(r)
                project_u(r, PAIRS - 1)

        batches(pe, body)

    def pt_io(j):
        full = 4 if j < 2 else 3
        bank = PTb[:, j % 2, :].rearrange("p (c q) -> p c q", c=4)
        io = [(bank[:, 0:full, :], [t[:, 4 * j:4 * j + full, :] for t in PT])]
        if full < 4:
            io.append((bank[0:TAIL, 3, :], [t[0:TAIL, 4 * j + 3, :] for t in PT]))
        return io

    def ctxt_io(j, parity, bank=M1):
        n = P + rows_of(2 * j + 1)
        return [(bank[:, 2 * k * P:2 * k * P + n], [t[:, k, 2 * j * P:2 * j * P + n] for t in ctxT[parity]]) for k in range(KD)]

    def each(io, f):
        for src, dst in io:
            ins = f(src, dst)
        return ins

    def chunks(j):
        if 2 * j + 2 < NCH:
            return [(slice(0, P), slice(2 * j, 2 * j + 2))]
        return [(slice(0, P), slice(2 * j, 2 * j + 1)), (slice(0, TAIL), slice(2 * j + 1, 2 * j + 2))]

    def by_k(bank):
        return bank[:, 0:KD * P].rearrange("p (k q) -> p k q", k=KD)

    M0_k = by_k(M0)

    @block.scalar
    def _(act):
        def prob_exp(r, p):
            act.wait_ge(negmax_ready, r + 1)
            act.activation(prob[:, :], S[:, :, :].rearrange("p n f -> p (n f)")[:, 0:AUD], ACT.Exp, bias=negmax[:, 0:1],
                           scale=1 / (SA * SA), accum_out=den[:, p % 2:p % 2 + 1]).then_inc(prob_ready, 1)

        def prob_hi(r, j):
            act.wait_ge(pt_ready, r * 3 + (j + 1))
            each(pt_io(j), lambda s, d: split_hi(act, d[0], s, SP)).then_inc(pt_hi, 1)

        def u_hi(r):
            act.wait_ge(ut_ready, r + 1)
            split_hi(act, UT[0][:, :, :], M0_k, SA).then_inc(ut_hi, 1)

        def fold_hi_(count, p, bank=M0):
            act.wait_ge(fold_ready, count)
            split_hi(act, qf[0][:, :, p, :], by_k(bank), SA / (SA * SW)).then_inc(fold_hi, 1)

        def ctxt_hi_(count, j, parity, bank=M1):
            act.wait_ge(ctxt_ready, count)
            each(ctxt_io(j, parity, bank), lambda s, d: split_hi(act, d[0], s, SA)).then_inc(ctxt_hi, 1)

        for j in range(NPREP):
            ctxt_hi_(j + 1, j, 0, first_banks[j])
        for p in range(PAIRS):
            fold_hi_(p + 1, p, fold_banks[p % len(fold_banks)])
        act.wait_ge(nat_loaded, 32)
        for j in range(NPREP):
            for ps, cs in chunks(j):
                ins = split_hi(act, ctx_s[0][0][ps, cs, :], nat[ps, cs, :], SA)
            ins.then_inc(csplit_hi, 1)
        prob_exp(0, 0)

        def parts_hi(b, r):
            prob_hi(r, 0)
            prob_hi(r, 1)
            if b is not None:
                u_hi(r - 1)
            prob_hi(r, 2)

        parts_hi(None, 0)

        def body(b, parity, left):
            for p in range(PAIRS):
                r = b * 8 + p
                half, stage = divmod(p, 4)
                if left and 1 <= p <= NPREP:
                    ctxt_hi_((b + 1) * NPREP + p, p - 1, 1 - parity)
                if p < PAIRS - 1 or left:
                    prob_exp(r + 1, p + 1)
                if left:
                    fold_hi_((b + 1) * 8 + (p + 1), p)
                if stage == 2:
                    if half == 0:
                        act.wait_ge(v_loaded, (b + 1) * 32)
                    act.wait_ge(text_ready, r + 1)
                    split_hi(act, PTt[0][:, half, :], M1[0:TI, :], SP).then_inc(ptt_hi, 1)
                if p < PAIRS - 1 or left:
                    parts_hi(b, r + 1)
                if stage == 1:
                    act.wait_ge(ts_ready, b * 2 + (half + 1))
                    act.activation(tprob[:, :, :], tprob[:, :, :], ACT.Exp).then_inc(te_ready, 1)
            if not left:
                u_hi(b * 8 + (PAIRS - 1))

        batches(act, body)

    @block.vector
    def _(dve):
        def row_max(r, n):
            dve.wait_ge(scores_ready, r * 3 + (n + 1))
            dve.tensor_reduce(maxes[:, n:n + 1], S[:, n, 0:width(n)], X, ALU.max).then_inc(maxes_ready, 1)
            if n == SB - 1:
                dve.wait_ge(maxes_ready, r * 3 + SB)
                dve.tensor_reduce(top[:, :], maxes[:, :], X, ALU.max).then_inc(top_ready, 1)
                dve.wait_ge(top_ready, r + 1)
                dve.tensor_scalar(negmax[:, :], top[:, :], -1 / (SA * SA), None, ALU.mult).then_inc(negmax_ready, 1)

        def prob_lo(r, j):
            dve.wait_ge(pt_hi, r * 3 + (j + 1))
            each(pt_io(j), lambda s, d: split_lo(dve, d[1], s, d[0], SP)).then_inc(pt_lo, 1)

        def u_lo(r):
            dve.wait_ge(ut_hi, r + 1)
            split_lo(dve, UT[1][:, :, :], M0_k, UT[0][:, :, :], SA).then_inc(ut_lo, 1)

        def u_norm(r, p):
            dve.wait_ge(prob_ready, r + 1)
            dve.reciprocal(rden[:, :], den[:, p % 2:p % 2 + 1]).then_inc(rden_ready, 1)
            dve.wait_ge(rden_ready, r + 1)
            dve.wait_ge(u_ready, r + 1)
            dve.tensor_scalar(u_sb[:, :], Ub[:, 0:D], rden[:, 0:1], gains[:, 1:2], ALU.mult, ALU.mult).then_inc(u_normed, 1)

        def add_heads(b, pairs, src, scale):
            for e in range(2):
                h = slice(e * HD, (e + 1) * HD)
                dst = OT[h, pairs, bass.ds(b * NQ, NQ)]
                ins = dve.scalar_tensor_tensor(out=dst, in0=src[h, :, h], scalar=scale, in1=dst, op0=ALU.mult, op1=ALU.add)
            return ins

        def add_audio(b, r, p):
            dve.wait_ge(proj_ready, r + 1)
            dve.wait_ge(text_added, b * 2 + (1 if p < 3 else 2 if p < PAIRS - 1 else 3))
            add_heads(b, slice(p, p + 1), M0[:, 0:P].unsqueeze(1), 1 / (SA * SW)).then_inc(ot_added, 1)

        def fold_lo_(count, p, bank=M0):
            dve.wait_ge(fold_hi, count)
            split_lo(dve, qf[1][:, :, p, :], by_k(bank), qf[0][:, :, p, :], SA / (SA * SW)).then_inc(fold_lo, 1)

        def ctxt_lo_(count, j, parity, bank=M1):
            dve.wait_ge(ctxt_hi, count)
            each(ctxt_io(j, parity, bank), lambda s, d: split_lo(dve, d[1], s, d[0], SA)).then_inc(ctxt_lo, 1)

        def ctx_split(count, j, parity):
            hi, lo = ctx_s[parity]
            if count is None:
                dve.wait_ge(csplit_hi, j + 1)
            else:
                for ps, cs in chunks(j):
                    ins = dve.tensor_scalar(hi[ps, cs, :], nat[ps, cs, :], SA, None, ALU.mult)
                ins.then_inc(csplit_hi, 1)
                dve.wait_ge(csplit_hi, count)
            for ps, cs in chunks(j):
                ins = split_lo(dve, lo[ps, cs, :], nat[ps, cs, :], hi[ps, cs, :], SA)
            ins.then_inc(csplit_lo, 1)

        def text_probs(b, half):
            dve.wait_ge(te_ready, b * 2 + (half + 1))
            dve.tensor_reduce(tsum[:, 0, :], tprob[:, :, 0:TXT], X, ALU.add)
            dve.tensor_reduce(tsum[:, 1, :], tprob[:, :, TXT:TI], X, ALU.add).then_inc(tsum_ready, 1)
            dve.wait_ge(tsum_ready, b * 2 + (half + 1))
            dve.reciprocal(tsum[:, :, :], tsum[:, :, :]).then_inc(trec_ready, 1)
            dve.wait_ge(trec_ready, b * 2 + (half + 1))
            dve.tensor_scalar(tsum[:, 1, :], tsum[:, 1, :], gains[:, 0:1], None, ALU.mult).then_inc(tgain_ready, 1)
            dve.tensor_tensor(tprob[:, :, 0:TXT], tprob[:, :, 0:TXT], tsum[:, 0, :].unsqueeze(2).broadcast_to([P, 4, TXT]), ALU.mult)
            dve.wait_ge(tgain_ready, b * 2 + (half + 1))
            dve.tensor_tensor(tprob[:, :, TXT:TI], tprob[:, :, TXT:TI], tsum[:, 1, :].unsqueeze(2).broadcast_to([P, 4, IMG]),
                              ALU.mult).then_inc(tp_ready, 1)

        def text(b, r, p):
            half, stage = divmod(p, 4)
            n = b * 2 + (half + 1)
            if stage == 0:
                if half == 0:
                    dve.wait_ge(r_loaded, (b + 1) * 32)
                dve.wait_ge(text_ready, r + 1)
                dve.scalar_tensor_tensor(out=ST[:, :], in0=M1[0:TI, :], scalar=1 / (SA * SA), in1=Rb[:, half * 512:(half + 1) * 512],
                                         op0=ALU.mult, op1=ALU.add).then_inc(st_ready, 1)
            elif stage == 1:
                dve.wait_ge(text_ready, r + 1)
                s = M1[:, 0:4 * TI].rearrange("p (q j) -> p q j", q=4)
                dve.tensor_reduce(tmax[:, 0, :], s[:, :, 0:TXT], X, ALU.max)
                dve.tensor_reduce(tmax[:, 1, :], s[:, :, TXT:TI], X, ALU.max).then_inc(tmax_ready, 1)
                dve.wait_ge(tmax_ready, n)
                dve.tensor_tensor(tprob[:, :, 0:TXT], s[:, :, 0:TXT], tmax[:, 0, :].unsqueeze(2).broadcast_to([P, 4, TXT]), ALU.subtract)
                dve.tensor_tensor(tprob[:, :, TXT:TI], s[:, :, TXT:TI], tmax[:, 1, :].unsqueeze(2).broadcast_to([P, 4, IMG]),
                                  ALU.subtract).then_inc(ts_ready, 1)
            elif stage == 2:
                dve.wait_ge(ptt_hi, n)
                split_lo(dve, PTt[1][:, half, :], M1[0:TI, :], PTt[0][:, half, :], SP).then_inc(ptt_lo, 1)
            else:
                dve.wait_ge(text_ready, r + 1)
                dve.wait_ge(ot_added, r + 1)
                add_heads(b, slice(4 * half, 4 * half + 4), M1[:, :].rearrange("p (q c) -> p q c", q=4),
                          1 / (SP * SA)).then_inc(text_added, 1)

        dve.sem_inc(ot_added, 1)
        dve.sem_inc(text_added, 1)
        for j in range(NPREP):
            ctxt_lo_(j + 1, j, 0, first_banks[j])
        dve.wait_ge(zeroed, 3)
        for s in range(2):
            for e in range(2):
                h = slice(e * HD, (e + 1) * HD)
                dve.tensor_copy(BD[0][s][h, :, h], qT[s][h, :, 0:NQ]).then_inc(bd_ready, 1)
        for p in range(PAIRS):
            fold_lo_(p + 1, p, fold_banks[p % len(fold_banks)])
        for n in range(SB):
            row_max(0, n)
        for j in range(NPREP):
            ctx_split(None, j, 0)

        def parts_lo(b, r, p, follows):
            prob_lo(r, 0)
            prob_lo(r, 1)
            if follows:
                row_max(r + 1, 0)
            if b is not None:
                u_lo(r - 1)
            prob_lo(r, 2)
            if follows:
                row_max(r + 1, 1)
            if b is not None:
                add_audio(b, r - 1, (p - 1) % PAIRS)
            if follows:
                row_max(r + 1, 2)

        parts_lo(None, 0, 0, True)

        def body(b, parity, left):
            for p in range(PAIRS):
                r = b * 8 + p
                if left and 1 <= p <= NPREP:
                    if p == 1:
                        dve.wait_ge(nat_loaded, (b + 2) * 32)
                    ctxt_lo_((b + 1) * NPREP + p, p - 1, 1 - parity)
                if p % 4 == 2:
                    text_probs(b, p // 4)
                if left:
                    fold_lo_((b + 1) * 8 + (p + 1), p)
                if left and 1 <= p <= NPREP:
                    ctx_split((b + 1) * NPREP + p, p - 1, 1 - parity)
                u_norm(r, p)
                text(b, r, p)
                if p < PAIRS - 1:
                    parts_lo(b, r + 1, p + 1, p < PAIRS - 2 or left)
                elif left:
                    parts_lo(b, r + 1, 0, True)
            if not left:
                r = b * 8 + (PAIRS - 1)
                u_lo(r)
                add_audio(b, r, PAIRS - 1)

        batches(dve, body)


class OutputWeights:

    def __init__(self, m):
        self.wo_f = m.sb("wo_f", [P, PAIRS, D])
        self.wo = [m.sb(f"wo_{s}", [P, PAIRS, D], F16) for s in "hl"]
        self.bo = m.sb("bo", [P, D])
        self.wo_loaded, self.bo_loaded = m.sem("wo_loaded"), m.sem("bo_loaded")
        self.wo_scaled = m.sem("wo_scaled")
        self.wo_hi, self.wo_lo, self.xb_ready = m.sem("wo_hi"), m.sem("wo_lo"), m.sem("xb_ready")

    def load(self, sp, a):
        sp.dma_start(self.wo_f[:, :, :], a["Wo"].rearrange("(m p) n -> p m n", p=P)).then_inc(self.wo_loaded, 16)
        sp.dma_start(self.bo[:, :], a["bo"].rearrange("(o n) -> o n", o=1).broadcast_to([P, D])).then_inc(self.bo_loaded, 16)

    def pool(self, pool, x):
        pool.wait_ge(self.bo_loaded, 16)
        pool.tensor_tensor(x[:, :, :], x[:, :, :], self.bo[:, :].unsqueeze(1).broadcast_to([P, TT, D]), ALU.add).then_inc(self.xb_ready, 1)
        pool.wait_ge(self.wo_hi, 1)
        pool.tensor_tensor(self.wo[1][:, :, :], self.wo_f[:, :, :], self.wo[0][:, :, :], ALU.subtract).then_inc(self.wo_lo, 1)

    def scalar(self, act):
        act.wait_ge(self.wo_loaded, 16)
        split_hi_in_place(act, self.wo[0][:, :, :], self.wo_f[:, :, :], SW, (self.wo_scaled, 1)).then_inc(self.wo_hi, 1)


def relative_values(nc, m, a, scr, OT, x, out_weights):
    probs = m.sb("tprob_all", [TXT, B, 2, PAIRS * 2 * NQ], F16)
    window_f = m.sb("relv_window_f", [TXT, NQ, HD])
    window = [m.sb(f"relv_window_{s}", [TXT, NQ, 2, HD], F16) for s in "hl"]
    U = 4
    bank = m.ps("relv_bank", [P, U, 512])
    probs_loaded, window_loaded = m.sem("tprobs_loaded"), m.sem("relv_window_loaded")
    window_hi, window_lo = m.sem("relv_window_hi"), m.sem("relv_window_lo")
    rel_ready, rel_added = m.sem("relv_ready"), m.sem("relv_added")
    block = m.ctx.enter_context(nc.Block())

    @block.sync
    def _(sp):
        rows = scr["relv"]
        overlapping = bass.AP(tensor=rows.tensor, offset=rows.offset, ap=[[HD, TXT], [1, NQ * HD]])
        sp.dma_start(window_f[:, :, :].rearrange("j i d -> j (i d)"), overlapping).then_inc(window_loaded, 16)
        sp.dma_start(probs[:, :, :, :].rearrange("j b s f -> j b (s f)"), scr["pt"].rearrange("b j s f -> j b (s f)")).then_inc(probs_loaded, 16)
        out_weights.load(sp, a)

    @block.gpsimd
    def _(pool):
        out_weights.pool(pool, x)

    @block.tensor
    def _(pe):
        pe.wait_ge(window_lo, 1)
        pe.wait_ge(probs_loaded, 16)

        def group(g, u):
            for v in range(2):
                at = 2 * u + v
                lhs = [w[:, bass.ds(g * (-2 * U) + (NQ - 1 - at), 1), :, :].rearrange("j o e d -> j (o e d)") for w in window]
                rhs = [probs[:, :, s, :].rearrange("j b (h i) -> j h b i", i=NQ)[:, :, :, bass.ds(g * (2 * U) + at, 1)].squeeze(3)
                       for s in range(2)]
                mm = mm3(pe, bank[:, u, v * 256:(v + 1) * 256], lhs, rhs)
            mm.then_inc(rel_ready, 1)

        for u in range(U):
            group(0, u)
        with pe.Fori(1, NQ // (2 * U)) as g:
            for u in range(U):
                pe.wait_ge(rel_added, g * U + (u + 1 - U))
                group(g, u)

    @block.scalar
    def _(act):
        act.wait_ge(window_loaded, 16)
        for e in range(2):
            split_hi(act, window[0][:, :, e, :], window_f[:, :, :], SW).then_inc(window_hi, 1)
        out_weights.scalar(act)

    @block.vector
    def _(dve):
        for e in range(2):
            dve.wait_ge(window_hi, e + 1)
            ins = split_lo(dve, window[1][:, :, e, :], window_f[:, :, :], window[0][:, :, e, :], SW)
        ins.then_inc(window_lo, 1)
        with dve.Fori(0, NQ // (2 * U)) as g:
            for u in range(U):
                dve.wait_ge(rel_ready, g * U + (u + 1))
                for e in range(2):
                    h = slice(e * HD, (e + 1) * HD)
                    for v in range(2):
                        dst = OT[h, :, :].rearrange("d p (b i) -> d p b i", i=NQ)[:, :, :, bass.ds(g * (2 * U) + (2 * u + v), 1)].squeeze(3)
                        src = bank[h, u, v * 256:(v + 1) * 256].rearrange("d (p e b) -> d p e b", p=PAIRS, e=2)[:, :, e, :]
                        ins = dve.scalar_tensor_tensor(out=dst, in0=src, scalar=1 / (SP * SW), in1=dst, op0=ALU.mult, op1=ALU.add)
                ins.then_inc(rel_added, 1)


class SelfWeights:

    def __init__(self, m):
        self.w_f = m.sb("w_attn_f", [P, KD, 3 * D])
        self.w = [m.sb(f"w_attn_{s}", [P, KD, 3 * D], F16) for s in "hl"]
        self.loaded, self.hi, self.lo = m.sem("w_attn_loaded"), m.sem("w_attn_hi"), m.sem("w_attn_lo")

    def load(self, sp, a):
        sp.dma_start(self.w_f[:, :, :], weight_rows(a["w_attn"])).then_inc(self.loaded, 16)

    def scalar(self, act):
        act.wait_ge(self.loaded, 16)
        split_hi(act, self.w[0][:, :, :], self.w_f[:, :, :], SW).then_inc(self.hi, 1)

    def vector(self, dve):
        dve.wait_ge(self.hi, 1)
        split_lo(dve, self.w[1][:, :, :], self.w_f[:, :, :], self.w[0][:, :, :], SW).then_inc(self.lo, 1)


def cross_output(nc, m, a, OT, x, weights, self_weights, norm):
    O = [m.sb(f"O_{s}", [P, PAIRS, T], F16) for s in "hl"]
    bank = m.ps("out_bank", [P, TT, 512])
    o_hi, o_lo = m.sem("o_hi"), m.sem("o_lo")
    y_ready, x_ready = m.sem("y_ready"), m.sem("x1_ready")
    block = m.ctx.enter_context(nc.Block())
    QUARTER = T // 4

    @block.sync
    def _(sp):
        self_weights.load(sp, a)

    @block.gpsimd
    def _(pool):
        norm.pool(pool)

    @block.scalar
    def _(act):
        for h in range(4):
            c = slice(h * QUARTER, (h + 1) * QUARTER)
            split_hi(act, O[0][:, :, c], OT[:, :, c], SA).then_inc(o_hi, 1)
        self_weights.scalar(act)

    @block.vector
    def _(dve):
        for h in range(4):
            c = slice(h * QUARTER, (h + 1) * QUARTER)
            dve.wait_ge(o_hi, h + 1)
            split_lo(dve, O[1][:, :, c], OT[:, :, c], O[0][:, :, c], SA).then_inc(o_lo, 1)
        self_weights.vector(dve)
        dve.wait_ge(weights.xb_ready, 1)
        for t in range(TT):
            dve.wait_ge(y_ready, t + 1)
            dve.scalar_tensor_tensor(out=x[:, t, :], in0=bank[:, t, 0:D], scalar=1 / (SA * SW), in1=x[:, t, :],
                                     op0=ALU.mult, op1=ALU.add).then_inc(x_ready, 1)
            dve.wait_ge(x_ready, t + 1)
            norm.tile_statistics(dve, x, t)
        norm.moments(dve)

    @block.tensor
    def _(pe):
        pe.wait_ge(weights.wo_lo, 1)
        for t in range(TT):
            pe.wait_ge(o_lo, t // 2 + 1)
            for k in range(PAIRS):
                mm = mm3(pe, bank[:, t, 0:D], [o[:, k, t * P:(t + 1) * P] for o in O], [w[:, k, :] for w in weights.wo],
                         k == 0, k == PAIRS - 1)
            mm.then_inc(y_ready, 1)


class TurnedTokens:

    def __init__(self, m, name, bank):
        self.T = [m.sb(f"{name}_T{s}", [P, KD, T], F16) for s in "hl"]
        self.bank = bank
        self.ready, self.hi, self.lo = m.sem(name + "_turned"), m.sem(name + "_T_hi"), m.sem(name + "_T_lo")

    def tensor(self, pe, xn, xn_ready, ident):
        for g in range(TT // 2):
            pe.wait_ge(xn_ready, 2 * g + 2)
            for k in range(KD):
                for t in range(2):
                    at = (2 * k + t) * P
                    mm = pe.transpose(self.bank[:, g, at:at + P], xn[:, 2 * g + t, k * P:(k + 1) * P], ident[:, :])
            mm.then_inc(self.ready, 1)

    def io(self, g, s):
        return self.T[s][:, :, g * 2 * P:(g + 1) * 2 * P], self.bank[:, g, :].rearrange("p (k t) -> p k t", k=KD)

    def scalar(self, act):
        for g in range(TT // 2):
            act.wait_ge(self.ready, g + 1)
            split_hi(act, *self.io(g, 0), SA).then_inc(self.hi, 1)

    def vector(self, dve):
        for g in range(TT // 2):
            dve.wait_ge(self.hi, g + 1)
            dst, src = self.io(g, 1)
            split_lo(dve, dst, src, self.io(g, 0)[0], SA).then_inc(self.lo, 1)


def self_attention(nc, m, a, x, weights, norm, next_norm, ident, used):
    SH, SHD, G = 16, D // 16, 8
    NG = SH // G
    AHEAD = 3
    w = weights.w
    wp_f = m.sb("w_proj_f", [P, KD, D])
    wp = [m.sb(f"w_proj_{s}", [P, KD, D], F16) for s in "hl"]
    b_rows = m.sb("b_attn_rows", [4, P])
    b_cols = m.sb("b_attn_cols", [P, 4])
    b_v = m.sb("b_v", [P, D])
    b_p = m.sb("b_proj", [P, D])
    xn = m.sb("xn_b", [P, TT, D])
    qk = m.sb("qk_T", [P, 2 * NG, T])
    spread = m.sb("head_mask", [P, G])
    kd = [m.sb(f"k_diag{i}", [P, G, NQ]) for i in range(2 * AHEAD)]
    vd = m.sb("v_diag", [P, B, SH // 2, 2, SHD])
    pr = [m.sb(f"self_prob{i}", [P, G, NQ]) for i in range(AHEAD)]
    prT = [m.sb(f"self_probT{i}", [P, 4, P]) for i in range(2)]
    top = m.sb("self_max", [P, 2, G])
    total = m.sb("self_sum", [P, TT, SH])
    o_sb = m.sb("self_o", [P, TT, D])
    oT = [m.sb(f"self_oT_{s}", [P, KD, T], F16) for s in "hl"]
    swapped = [m.sb(f"xn_b_swapped_{s}", [P, KD, T], F16) for s in "hl"]
    bank = m.ps("self_bank", [P, 8, 512])

    turned = TurnedTokens(m, "xn_b", bank)
    wp_loaded, b_loaded = m.sem("w_proj_loaded"), m.sem("b_attn_loaded")
    bv_loaded, bp_loaded = m.sem("b_v_loaded"), m.sem("b_proj_loaded")
    wp_hi, wp_lo = m.sem("w_proj_hi"), m.sem("w_proj_lo")
    mask_ready = m.sem("head_mask_ready")
    swapped_ready = m.sem("self_swapped_ready")
    vd_cleared = m.sem("v_diag_cleared")
    bias_turned, bias_ready = m.sem("b_attn_turned"), m.sem("b_attn_ready")
    qk_ready, qk_out = m.sem("qk_ready"), m.sem("qk_out")
    v_ready, v_out = m.sem("self_v_ready"), m.sem("self_v_out")
    kd_ready = m.sem("k_diag_ready")
    s_ready, top_ready, sub_ready, exp_ready = m.sem("self_s_ready"), m.sem("self_top_ready"), m.sem("self_sub_ready"), m.sem("self_exp_ready")
    sum_ready, rec_ready = m.sem("self_sum_ready"), m.sem("self_rec_ready")
    pT_ready, pT_out = m.sem("self_pT_ready"), m.sem("self_pT_out")
    o_ready, o_out = m.sem("self_o_ready"), m.sem("self_o_out")
    oT_ready, oT_hi, oT_lo = m.sem("self_oT_ready"), m.sem("self_oT_hi"), m.sem("self_oT_lo")
    xb_ready, y_ready, y_added = m.sem("xb2_ready"), m.sem("self_y_ready"), m.sem("x2_ready")
    block = m.ctx.enter_context(nc.Block())
    NQK = 2 * NG * 2
    S_BANK, T_BANK, O_BANK = (0, 1, 6), (2, 3), (4, 5)

    @block.sync
    def _(sp):
        sp.dma_start(b_rows[:, :], a["b_attn"][0:2 * D].rearrange("(m p) -> m p", p=P)).then_inc(b_loaded, 16)
        sp.dma_start(b_v[:, :], a["b_attn"][2 * D:3 * D].rearrange("(o n) -> o n", o=1).broadcast_to([P, D])).then_inc(bv_loaded, 16)
        sp.dma_start(b_p[:, :], a["b_proj"].rearrange("(o n) -> o n", o=1).broadcast_to([P, D])).then_inc(bp_loaded, 16)
        sp.dma_start(wp_f[:, :, :], weight_rows(a["w_proj"])).then_inc(wp_loaded, 16)
        for sem in used:
            sp.sem_clear(sem)

    @block.gpsimd
    def _(pool):
        pool.memset(spread[:, :], 1.0).then_inc(mask_ready, 1)
        pool.wait_ge(mask_ready, 1)
        pool.affine_select(out=spread[:, :], in_=spread[:, :], compare_op=ALU.is_ge, fill=0.0, base=0,
                           pattern=[[-SHD, G]], channel_multiplier=1).then_inc(mask_ready, 1)
        pool.wait_ge(mask_ready, 2)
        pool.affine_select(out=spread[:, :], in_=spread[:, :], compare_op=ALU.is_ge, fill=0.0, base=SHD - 1,
                           pattern=[[SHD, G]], channel_multiplier=-1).then_inc(mask_ready, 1)
        pool.memset(vd[:, :, :, :, :], 0.0).then_inc(vd_cleared, 1)
        pool.wait_ge(mask_ready, 3)
        pool.wait_ge(qk_out, NQK)
        for u in range(TT * NG):
            t, g = divmod(u, NG)
            if u >= AHEAD:
                pool.wait_ge(s_ready, u - (AHEAD - 1))
            for e in range(2):
                k = qk[:, NG + g, (2 * t + e) * NQ:(2 * t + e + 1) * NQ]
                pool.tensor_tensor(kd[(2 * u + e) % (2 * AHEAD)][:, :, :], k.unsqueeze(1).broadcast_to([P, G, NQ]),
                                   spread[:, :].unsqueeze(2).broadcast_to([P, G, NQ]), ALU.mult).then_inc(kd_ready, 1)
            if u == 0:
                pool.wait_ge(norm.xn_ready, TT)
                pool.wait_ge(bp_loaded, 16)
                pool.tensor_tensor(x[:, :, :], x[:, :, :], b_p[:, :].unsqueeze(1).broadcast_to([P, TT, D]), ALU.add).then_inc(xb_ready, 1)
        next_norm.pool(pool)

    @block.tensor
    def _(pe):
        turned.tensor(pe, xn, norm.xn_ready, ident)
        pe.wait_ge(b_loaded, 16)
        pe.transpose(bank[:, 4, 0:4], b_rows[:, :], ident[0:4, 0:4]).then_inc(bias_turned, 1)
        pe.wait_ge(turned.lo, TT // 2)
        pe.wait_ge(weights.lo, 1)
        for job in range(NQK):
            c, n = divmod(job, 2)
            if job >= 3:
                pe.wait_ge(qk_out, job - 2)
            if job == 0:
                pe.wait_ge(bias_ready, 1)
            for k in range(KD):
                mm = mm3(pe, bank[:, 4 + job % 3, :], [x_[:, k, c * P:(c + 1) * P] for x_ in w],
                         [x_[:, k, n * 512:(n + 1) * 512] for x_ in turned.T], k == 0, k == KD - 1)
            mm.then_inc(qk_ready, 1)
        for job in range(2 * TT):
            t, other = divmod(job, 2)
            if job == 0:
                pe.wait_ge(swapped_ready, 4)
            if job >= 2:
                pe.wait_ge(v_out, job - 1)
            for k in range(KD):
                lhs = [x_[:, k, t * P:(t + 1) * P] for x_ in (swapped if other else turned.T)]
                mm = mm3(pe, bank[:, job % 2, 0:D], lhs, [x_[:, k, 2 * D:3 * D] for x_ in w], k == 0, k == KD - 1)
            mm.then_inc(v_ready, 1)

        def scores(u):
            t, g = divmod(u, NG)
            pe.wait_ge(kd_ready, 2 * u + 2)
            if u >= AHEAD:
                pe.wait_ge(sub_ready, u - (AHEAD - 1))
            for e in range(2):
                h = slice(e * NQ, (e + 1) * NQ)
                mm = pe.matmul(bank[h, S_BANK[u % AHEAD], :], qk[:, g, (2 * t + e) * NQ:(2 * t + e + 1) * NQ],
                               kd[(2 * u + e) % (2 * AHEAD)][:, :, :].rearrange("p h k -> p (h k)"), start=True, stop=True)
            mm.then_inc(s_ready, 1)

        def values(u):
            t, g = divmod(u, NG)
            pe.wait_ge(exp_ready, u + 1)
            if u >= 2:
                pe.wait_ge(pT_out, u - 1)
            for c in range(4):
                mm = pe.transpose(bank[:, T_BANK[u % 2], c * P:(c + 1) * P],
                                  pr[u % AHEAD][:, 2 * c:2 * c + 2, :].rearrange("p h k -> p (h k)"), ident[:, :])
            mm.then_inc(pT_ready, 1)

        def outputs(u):
            t, g = divmod(u, NG)
            pe.wait_ge(pT_out, u + 1)
            if t >= 2:
                pe.wait_ge(o_out, t - 1)
            for e in range(2):
                h = slice(e * NQ, (e + 1) * NQ)
                for c in range(4):
                    pair = 4 * g + c
                    mm = pe.matmul(bank[h, O_BANK[t % 2], pair * 32:(pair + 1) * 32], prT[u % 2][:, c, h],
                                   vd[:, 2 * t + e, pair, :, :].rearrange("p e d -> p (e d)"), start=True, stop=True)
            mm.then_inc(o_ready, 1)

        pe.wait_ge(v_out, 2 * TT)
        for u in range(AHEAD - 1):
            scores(u)
        for u in range(TT * NG):
            if u + AHEAD - 1 < TT * NG:
                scores(u + AHEAD - 1)
            values(u)
            if u:
                outputs(u - 1)
        outputs(TT * NG - 1)
        for t in range(TT):
            pe.wait_ge(o_out, t + 1)
            if t >= 2:
                pe.wait_ge(oT_lo, t - 1)
            for k in range(KD):
                mm = pe.transpose(bank[:, S_BANK[t % 2], k * P:(k + 1) * P], o_sb[:, t, k * P:(k + 1) * P], ident[:, :])
            mm.then_inc(oT_ready, 1)
        for t in range(TT):
            pe.wait_ge(oT_lo, t + 1)
            pe.wait_ge(wp_lo, 1)
            if t >= 2:
                pe.wait_ge(y_added, t - 1)
            for k in range(KD):
                mm = mm3(pe, bank[:, 6 + t % 2, 0:D], [o[:, k, t * P:(t + 1) * P] for o in oT],
                         [x_[:, k, :] for x_ in wp], k == 0, k == KD - 1)
            mm.then_inc(y_ready, 1)

    @block.scalar
    def _(act):
        turned.scalar(act)
        act.wait_ge(bias_turned, 1)
        act.activation(b_cols[:, :], bank[:, 4, 0:4], ACT.Copy).then_inc(bias_ready, 1)
        act.wait_ge(bias_ready, 1)
        act.mul(b_cols[:, 0:NG], b_cols[:, 0:NG], SHD ** -0.5).then_inc(bias_ready, 1)
        act.wait_ge(bias_ready, 2)
        for job in range(NQK):
            c, n = divmod(job, 2)
            act.wait_ge(qk_ready, job + 1)
            scale = (SHD ** -0.5 if c < NG else 1.0) / (SA * SW)
            act.activation(qk[:, c, n * 512:(n + 1) * 512], bank[:, 4 + job % 3, :], ACT.Identity, bias=b_cols[:, c:c + 1],
                           scale=scale).then_inc(qk_out, 1)
        act.wait_ge(wp_loaded, 16)
        split_hi(act, wp[0][:, :, :], wp_f[:, :, :], SW).then_inc(wp_hi, 1)
        def exponent(u):
            act.wait_ge(sub_ready, u + 1)
            act.activation(pr[u % AHEAD][:, :, :], pr[u % AHEAD][:, :, :], ACT.Exp).then_inc(exp_ready, 1)

        for u in range(AHEAD - 1):
            exponent(u)
        for u in range(TT * NG):
            t, g = divmod(u, NG)
            act.wait_ge(pT_ready, u + 1)
            if u >= 2:
                act.wait_ge(o_ready, u - 1)
            act.activation(prT[u % 2][:, :, :].rearrange("p c q -> p (c q)"), bank[:, T_BANK[u % 2], :], ACT.Copy).then_inc(pT_out, 1)
            if u + AHEAD - 1 < TT * NG:
                exponent(u + AHEAD - 1)
        for t in range(TT):
            act.wait_ge(oT_ready, t + 1)
            split_hi(act, oT[0][:, :, t * P:(t + 1) * P], bank[:, S_BANK[t % 2], 0:D].rearrange("p (k q) -> p k q", k=KD), SA).then_inc(oT_hi, 1)

    @block.vector
    def _(dve):
        norm.normalize(dve, xn, x)
        turned.vector(dve)
        dve.wait_ge(turned.lo, TT // 2)
        for src, dst in zip(turned.T, swapped):
            src, dst = [v[:, :, :].rearrange("p k (t e q) -> p (k t) e q", e=2, q=NQ) for v in (src, dst)]
            for e in range(2):
                dve.tensor_copy(dst[:, :, e, :], src[:, :, 1 - e, :]).then_inc(swapped_ready, 1)
        dve.wait_ge(vd_cleared, 1)
        dve.wait_ge(bv_loaded, 16)
        for job in range(2 * TT):
            t, other = divmod(job, 2)
            dve.wait_ge(v_ready, job + 1)
            for e in range(2):
                h = slice(e * NQ, (e + 1) * NQ)
                src = bank[h, job % 2, 0:D].rearrange("p (c e d) -> p c e d", e=2, d=SHD)[:, :, e, :]
                bias = b_v[h, :].rearrange("p (c e d) -> p c e d", e=2, d=SHD)[:, :, e, :]
                ins = dve.scalar_tensor_tensor(out=vd[h, 2 * t + (e ^ other), :, e, :], in0=src, scalar=1 / (SA * SW), in1=bias,
                                               op0=ALU.mult, op1=ALU.add)
            ins.then_inc(v_out, 1)
        dve.wait_ge(wp_hi, 1)
        split_lo(dve, wp[1][:, :, :], wp_f[:, :, :], wp[0][:, :, :], SW).then_inc(wp_lo, 1)

        def shift(u):
            s = bank[:, S_BANK[u % AHEAD], :].rearrange("p (h k) -> p h k", h=G)
            dve.wait_ge(s_ready, u + 1)
            dve.tensor_reduce(top[:, u % 2, :], s, X, ALU.max).then_inc(top_ready, 1)
            dve.wait_ge(top_ready, u + 1)
            if u >= AHEAD:
                dve.wait_ge(pT_ready, u - (AHEAD - 1))
            dve.tensor_tensor(pr[u % AHEAD][:, :, :], s, top[:, u % 2, :].unsqueeze(2).broadcast_to([P, G, NQ]), ALU.subtract).then_inc(sub_ready, 1)

        def add_up(u):
            t, g = divmod(u, NG)
            dve.wait_ge(exp_ready, u + 1)
            dve.tensor_reduce(total[:, t, g * G:(g + 1) * G], pr[u % AHEAD][:, :, :], X, ALU.add).then_inc(sum_ready, 1)

        def output(t):
            dve.wait_ge(sum_ready, NG * (t + 1))
            dve.reciprocal(total[:, t, :], total[:, t, :]).then_inc(rec_ready, 1)
            dve.wait_ge(rec_ready, t + 1)
            dve.wait_ge(o_ready, NG * (t + 1))
            dve.tensor_tensor(o_sb[:, t, :].rearrange("p (h d) -> p h d", h=SH), bank[:, O_BANK[t % 2], 0:D].rearrange("p (h d) -> p h d", h=SH),
                              total[:, t, :].unsqueeze(2).broadcast_to([P, SH, SHD]), ALU.mult).then_inc(o_out, 1)

        for u in range(AHEAD - 1):
            shift(u)
        for u in range(TT * NG):
            add_up(u)
            if u + AHEAD - 1 < TT * NG:
                shift(u + AHEAD - 1)
            if u % NG == NG - 1 and u > NG:
                output(u // NG - 1)
        output(TT - 1)
        for t in range(TT):
            dve.wait_ge(oT_hi, t + 1)
            io = [o[:, :, t * P:(t + 1) * P] for o in oT]
            split_lo(dve, io[1], bank[:, S_BANK[t % 2], 0:D].rearrange("p (k q) -> p k q", k=KD), io[0], SA).then_inc(oT_lo, 1)
        dve.wait_ge(xb_ready, 1)
        for t in range(TT):
            dve.wait_ge(y_ready, t + 1)
            dve.scalar_tensor_tensor(out=x[:, t, :], in0=bank[:, 6 + t % 2, 0:D], scalar=1 / (SA * SW), in1=x[:, t, :],
                                     op0=ALU.mult, op1=ALU.add).then_inc(y_added, 1)
            dve.wait_ge(y_added, t + 1)
            next_norm.tile_statistics(dve, x, t)
        next_norm.moments(dve)


def experts(nc, m, a, x, norm, out, ident):
    E, HID, SHID = 8, 256, 512
    KH, KS = HID // P, SHID // P
    HALF = T // 2
    NU = 2 * E
    xn = m.sb("xn_c", [P, TT, D])
    gate_rows = m.sb("gate_rows", [E, D])
    gate = [m.sb(f"gate_{s}", [P, KD, E], F16) for s in "hl"]
    bias_rows = m.sb("bias_rows", [3 * E * KH, P])
    bias = m.sb("bias", [P, 3, E, KH])
    b1_now = [m.sb(f"b1_now{i}", [P, KH]) for i in range(2)]
    select = m.sb("select", [E, E, P], F16)
    before = m.sb("before", [P, E, E])
    gs = m.sb("gate_scores", [P, TT, E])
    gmax, gsum = m.sb("gate_max", [P, TT]), m.sb("gate_sum", [P, TT])
    above = m.sb("above", [P, TT, E, E])
    equal = m.sb("equal", [P, TT, E, E])
    rank = m.sb("rank", [P, TT, E])
    mask = m.sb("mask", [P, TT, E])
    wT = [m.sb(f"gate_T{s}", [E, T], F16) for s in "hl"]
    mT = m.sb("mask_T", [E, T], F16)
    WB = m.sb("weight_all", [P, E, T])
    MB = m.sb("mask_all", [P, E, T], F16)
    wf = [m.sb(f"expert_f{i}", [P, 3, KD, HID]) for i in range(2)]
    we = [[m.sb(f"expert_{s}{i}", [P, 3, KD, HID], F16) for s in "hl"] for i in range(2)]
    sf = m.sb("shared_f", [P, 3, 1024])
    ws = [m.sb(f"shared_w_{s}", [P, 3, 1024], F16) for s in "hl"]
    ta = [m.sb(f"ta{i}", [P, KH, HALF]) for i in range(2)]
    tb = [m.sb(f"tb{i}", [P, KH, HALF]) for i in range(2)]
    hT = [[m.sb(f"hT_{s}{i}", [P, KH, HALF], F16) for s in "hl"] for i in range(2)]
    acc = m.sb("acc", [P, KD, T])
    sg = m.sb("shared_prod", [P, KS, HALF])
    sh = [m.sb(f"shared_prod_{s}", [P, KS, HALF], F16) for s in "hl"]
    bank = m.ps("ffn_bank", [P, 8, 512])

    turned = TurnedTokens(m, "xn_c", bank)
    gate_loaded, bias_loaded, shared_loaded = m.sem("gate_loaded"), m.sem("bias_loaded"), m.sem("shared_loaded")
    wf_loaded = [m.sem(f"expert_loaded{i}") for i in range(2)]
    consts = m.sem("select_before")
    rows_turned, bias_out, gate_hi, gate_lo = m.sem("rows_turned"), m.sem("bias_out"), m.sem("gate_hi"), m.sem("gate_lo")
    logits_ready, shifted, gexp_ready = m.sem("logits_ready"), m.sem("logits_shifted"), m.sem("gate_exp_ready")
    rank_step = m.sem("rank_step")
    gstep = m.sem("gate_step")
    gates_ready, gT_ready, gT_hi, gT_lo, mT_out = m.sem("gates_ready"), m.sem("gate_T_ready"), m.sem("gate_T_hi"), m.sem("gate_T_lo"), m.sem("mask_T_out")
    wb_ready, mb_ready, wb_out, mb_out = m.sem("wb_ready"), m.sem("mb_ready"), m.sem("wb_out"), m.sem("mb_out")
    ws_turned, ws_hi, ws_lo = m.sem("shared_turned"), m.sem("shared_w_hi"), m.sem("shared_w_lo")
    sg_ready, sg_out, su_ready, su_out = m.sem("sg_ready"), m.sem("sg_out"), m.sem("su_ready"), m.sem("su_out")
    sh_hi, sh_lo, sz_ready, sz_out = m.sem("shared_h_hi"), m.sem("shared_h_lo"), m.sem("sz_ready"), m.sem("sz_out")
    b1_ready = m.sem("b1_now_ready")
    we_turned, we_hi, we_lo = m.sem("expert_turned"), m.sem("expert_w_hi"), m.sem("expert_w_lo")
    a_ready, ta_ready, h_ready, h_hi, h_lo = m.sem("a_ready"), m.sem("ta_ready"), m.sem("h_ready"), m.sem("h_hi"), m.sem("h_lo")
    b_ready, tb_ready, x3_ready = m.sem("b_ready"), m.sem("tb_ready"), m.sem("x3_ready")
    y_ready = m.sem("ffn_y_ready")
    yt_ready, acc_ready = m.sem("yt_ready"), m.sem("acc_ready")
    fin_ready, fin_added, stored = m.sem("fin_ready"), m.sem("fin_added"), m.sem("out_stored")
    block = m.ctx.enter_context(nc.Block())
    names = ("w1", "w3", "w2")
    NT2 = 2 * E
    W_BANK, M_BANK = (0, 1, 2), (3, 6, 7)

    def units(eng, body):
        def pair(i, e, last):
            for v in range(4):
                body(i * 4 + v, e + v // 2, v % 2, v // 2, last and v == 3, last)
        with eng.Fori(0, E // 2 - 1) as i:
            pair(i, i * 2, False)
        pair(E // 2 - 1, E - 2, True)

    def next_of(e, half, parity):
        return (e, 1, parity) if half == 0 else (e + 1, 0, 1 - parity)

    @block.sync
    def _(sp):
        sp.dma_start(sf[:, 0, :].rearrange("p (j d) -> p j d", j=KS), a["sw1"].rearrange("(j p) d -> p j d", p=P)).then_inc(shared_loaded, 16)
        sp.dma_start(sf[:, 1, :].rearrange("p (j d) -> p j d", j=KS), a["sw2"].rearrange("(j p) d -> p j d", p=P)).then_inc(shared_loaded, 16)
        sp.dma_start(sf[:, 2, :].rearrange("p (k i) -> p k i", k=KD), a["sw3"].rearrange("(k p) i -> p k i", p=P)).then_inc(shared_loaded, 16)
        sp.dma_start(gate_rows[:, :], a["gate_w"]).then_inc(gate_loaded, 16)
        for n, b in enumerate(("b1", "b2", "b3")):
            sp.dma_start(bias_rows[n * E * KH:(n + 1) * E * KH, :], a[b].rearrange("e (k p) -> (e k) p", p=P)).then_inc(bias_loaded, 16)

        def load_expert(at, parity):
            for n, w in enumerate(names):
                flat = a[w].rearrange("e h d -> (e h d)")[bass.ds(at, HID * D)]
                sp.dma_start(wf[parity][:, n, :, :], flat.rearrange("(k p d) -> p k d", k=KH, p=P)).then_inc(wf_loaded[parity], 16)

        load_expert(0, 0)
        load_expert(HID * D, 1)

        with sp.Fori(0, E // 2 - 1) as i:
            for parity in range(2):
                at = sp.snap(i * (2 * HID * D) + (parity + 2) * HID * D)
                sp.wait_ge(we_lo, i * 6 + (3 * parity + 3))
                load_expert(at, parity)
        for t in range(TT):
            sp.wait_ge(fin_added, t + 1)
            sp.dma_start(out.rearrange("(t b) q d -> (b q) t d", b=2)[:, t, :], xn[:, t, :]).then_inc(stored, 16)
        sp.wait_ge(stored, 16 * TT)

    @block.gpsimd
    def _(pool):
        pool.memset(select[:, :, :], 0.0).then_inc(consts, 1)
        pool.wait_ge(consts, 1)
        pool.affine_select(out=select[:, :, :], in_=select[:, :, :], compare_op=ALU.not_equal, fill=1.0, base=0,
                           pattern=[[-1, E], [0, P]], channel_multiplier=1).then_inc(consts, 1)
        pool.wait_ge(consts, 2)
        pool.memset(before[:, :, :], 1.0).then_inc(consts, 1)
        pool.wait_ge(consts, 3)
        pool.affine_select(out=before[:, :, :], in_=before[:, :, :], compare_op=ALU.is_gt, fill=0.0, base=0,
                           pattern=[[1, E], [-1, E]], channel_multiplier=0).then_inc(consts, 1)
        pool.wait_ge(consts, 4)
        pool.wait_ge(gstep, 6)
        pool.tensor_tensor(equal[:, :, :, :].rearrange("p t e j -> p t (e j)"), equal[:, :, :, :].rearrange("p t e j -> p t (e j)"),
                          before[:, :, :].rearrange("p e j -> p (e j)").unsqueeze(1).broadcast_to([P, TT, E * E]), ALU.mult).then_inc(rank_step, 1)
        pool.wait_ge(rank_step, 1)
        pool.tensor_tensor(above[:, :, :, :].rearrange("p t e j -> p (t e j)"), above[:, :, :, :].rearrange("p t e j -> p (t e j)"),
                          equal[:, :, :, :].rearrange("p t e j -> p (t e j)"), ALU.add).then_inc(rank_step, 1)
        pool.wait_ge(sz_out, 2 * KD)

        def body(u, e, half, parity, very_last, last):
            at = acc[:, :, half * HALF:(half + 1) * HALF]
            pool.wait_ge(yt_ready, u + 2)
            pool.tensor_tensor(at, at, tb[half][:, :, :], ALU.add).then_inc(acc_ready, 1)

        units(pool, body)

    def shared_turn(job):
        n, half = divmod(job, 2)
        if n < 2:
            src = [sf[:, n, j * D + half * P:j * D + (half + 1) * P] for j in range(KS)]
        else:
            src = [sf[:, 2, k * SHID + j * P:k * SHID + (j + 1) * P] for j in (2 * half, 2 * half + 1) for k in range(KD)]
        return src, [w[:, n, half * 512:(half + 1) * 512] for w in ws]

    @block.tensor
    def _(pe):
        turned.tensor(pe, xn, norm.xn_ready, ident)
        pe.wait_ge(bias_loaded, 48)
        pe.wait_ge(gate_loaded, 16)
        pe.transpose(bank[:, 4, 0:3 * E * KH], bias_rows[:, :], ident[0:3 * E * KH, 0:3 * E * KH])
        for k in range(KD):
            mm = pe.transpose(bank[:, 4, 64 + k * E:64 + (k + 1) * E], gate_rows[:, k * P:(k + 1) * P], ident[0:E, 0:E])
        mm.then_inc(rows_turned, 1)
        pe.wait_ge(shared_loaded, 48)
        for job in range(6):
            if job >= 3:
                pe.wait_ge(ws_lo, job - 2)
            for q, src in enumerate(shared_turn(job)[0]):
                mm = pe.transpose(bank[:, 5 + job % 3, q * P:(q + 1) * P], src, ident[:, :])
            mm.then_inc(ws_turned, 1)
        pe.wait_ge(turned.lo, TT // 2)
        pe.wait_ge(gate_lo, 1)
        pe.wait_ge(bias_out, 2)
        for t in range(TT):
            for k in range(KD):
                mm = mm3(pe, bank[:, 4, t * E:(t + 1) * E], [x_[:, k, t * P:(t + 1) * P] for x_ in turned.T],
                         [g[:, k, :] for g in gate], k == 0, k == KD - 1)
        mm.then_inc(logits_ready, 1)
        pe.wait_ge(ws_lo, 6)
        for n in range(2):
            rhs = [[x_[:, k, n * HALF:(n + 1) * HALF] for x_ in turned.T] for k in range(KD)]
            for j in range(KS):
                at = n * KS + j
                if at >= 2:
                    pe.wait_ge(sg_out, at - 1)
                for k in range(KD):
                    mm = mm3(pe, bank[:, at % 2, :], [w[:, 0, k * SHID + j * P:k * SHID + (j + 1) * P] for w in ws], rhs[k],
                             k == 0, k == KD - 1)
                mm.then_inc(sg_ready, 1)
                if at >= 2:
                    pe.wait_ge(su_out, at - 1)
                for k in range(KD):
                    mm = mm3(pe, bank[:, 2 + at % 2, :], [w[:, 1, k * SHID + j * P:k * SHID + (j + 1) * P] for w in ws], rhs[k],
                             k == 0, k == KD - 1)
                mm.then_inc(su_ready, 1)
            if n:
                pe.wait_ge(sz_out, KD)
            for j in range(KS):
                pe.wait_ge(sh_lo, n * KS + j + 1)
                for k in range(KD):
                    mm = mm3(pe, bank[:, 5 + k, :], [w[:, 2, j * D + k * P:j * D + (k + 1) * P] for w in ws],
                             [h[:, j, :] for h in sh], j == 0, j == KS - 1)
                    if j == KS - 1:
                        mm.then_inc(sz_ready, 1)
        pe.wait_ge(gates_ready, 1)
        pe.wait_ge(sz_out, 2 * KD)
        for n, (src, at) in enumerate(((gs, 6), (mask, 4))):
            for t in range(TT):
                mm = pe.transpose(bank[0:E, at + t // 4, (t % 4) * P:(t % 4 + 1) * P], src[:, t, :], ident[:, :])
            mm.then_inc(gT_ready, 1)
        pe.wait_ge(gT_lo, 1)
        pe.wait_ge(mT_out, 1)
        pe.wait_ge(su_out, 2 * KS)
        for job in range(NT2):
            e, n = divmod(job, 2)
            if job >= 3:
                pe.wait_ge(wb_out, job - 2)
                pe.wait_ge(mb_out, job - 2)
            at = slice(n * HALF, (n + 1) * HALF)
            wb, mb = W_BANK[job % 3], M_BANK[job % 3]
            pe.matmul(bank[:, wb, :], select[:, e, :], wT[0][:, at], start=True, stop=False)
            pe.matmul(bank[:, wb, :], select[:, e, :], wT[1][:, at], start=False, stop=True).then_inc(wb_ready, 1)
            pe.matmul(bank[:, mb, :], select[:, e, :], mT[:, at], start=True, stop=True).then_inc(mb_ready, 1)

        def first_two(u, e, half, parity):
            for n, (at, free, ready) in enumerate(((0, ta_ready, a_ready), (2, tb_ready, b_ready))):
                if not isinstance(u, int) or u > 0:
                    pe.wait_ge(free, u)
                for c in range(KH):
                    for k in range(KD):
                        mm = mm3(pe, bank[:, at + c, :], [w[:, n, k, c * P:(c + 1) * P] for w in we[parity]],
                                 [x_[:, k, half * HALF:(half + 1) * HALF] for x_ in turned.T], k == 0, k == KD - 1)
                mm.then_inc(ready, 1)

        def last_one(u, half, parity):
            pe.wait_ge(h_lo, u + 1)
            pe.wait_ge(yt_ready, u + 1)
            for c in range(KD):
                for k in range(KH):
                    mm = mm3(pe, bank[:, 6 + c, :], [w[:, 2, k, c * P:(c + 1) * P] for w in we[parity]],
                             [h[:, k, :] for h in hT[half]], k == 0, k == KH - 1)
            mm.then_inc(y_ready, 1)

        def turn_weights(e, parity, which):
            for n in which:
                if not (isinstance(e, int) and e == 0 and n < 2):
                    pe.wait_ge(we_lo, e * 3 + (n - 1))
                for r in range(KD):
                    for c in range(2):
                        mm = pe.transpose(bank[:, 4 + (3 * parity + n) % 2, (2 * r + c) * P:(2 * r + c + 1) * P],
                                          wf[parity][:, n, c, r * P:(r + 1) * P], ident[:, :])
                mm.then_inc(we_turned, 1)

        pe.wait_ge(wf_loaded[0], 48)
        turn_weights(0, 0, (0, 1, 2))
        pe.wait_ge(wb_out, NT2)
        pe.wait_ge(mb_out, NT2)
        pe.wait_ge(we_lo, 3)
        first_two(0, 0, 0, 0)

        def body(u, e, half, parity, very_last, last):
            if not (last and parity == 1):
                if half == 0:
                    pe.wait_ge(wf_loaded[1 - parity], e * 24 + (72 if parity else 48))
                turn_weights(e + 1, 1 - parity, (0, 1) if half == 0 else (2,))
            if not very_last:
                ne, nhalf, nparity = next_of(e, half, parity)
                if nhalf == 0:
                    pe.wait_ge(we_lo, e * 3 + 5)
                first_two(u + 1, ne, nhalf, nparity)
            if half == 0:
                pe.wait_ge(we_lo, e * 3 + 3)
            last_one(u, half, parity)

        units(pe, body)
        pe.wait_ge(acc_ready, NU + 1)
        for t in range(TT):
            for k in range(KD):
                mm = pe.transpose(bank[:, t, k * P:(k + 1) * P], acc[:, k, t * P:(t + 1) * P], ident[:, :])
            mm.then_inc(fin_ready, 1)

    @block.scalar
    def _(act):
        turned.scalar(act)
        act.wait_ge(rows_turned, 1)
        act.activation(bias[:, :, :, :].rearrange("p n e k -> p (n e k)"), bank[:, 4, 0:3 * E * KH], ACT.Copy).then_inc(bias_out, 1)
        act.wait_ge(bias_out, 1)
        act.mul(bias[:, 1, :, :], bias[:, 1, :, :], SA * SW).then_inc(bias_out, 1)
        split_hi(act, gate[0][:, :, :], bank[:, 4, 64:64 + KD * E].rearrange("p (k e) -> p k e", k=KD), SW).then_inc(gate_hi, 1)
        for job in range(6):
            act.wait_ge(ws_turned, job + 1)
            split_hi(act, shared_turn(job)[1][0], bank[:, 5 + job % 3, :], SW).then_inc(ws_hi, 1)
        act.wait_ge(shifted, 1)
        act.activation(gs[:, :, :], gs[:, :, :], ACT.Exp, scale=1 / (SA * SW)).then_inc(gexp_ready, 1)
        for n in range(2):
            for j in range(KS):
                at = n * KS + j
                act.wait_ge(sg_ready, at + 1)
                if n and j == 0:
                    act.wait_ge(sh_lo, KS)
                act.activation(sg[:, j, :], bank[:, at % 2, :], ACT.Silu, scale=1 / (SA * SW)).then_inc(sg_out, 1)
                act.wait_ge(su_out, at + 1)
                if n and j == 0:
                    act.wait_ge(sz_ready, KD)
                split_hi(act, sh[0][:, j, :], sg[:, j, :], SA).then_inc(sh_hi, 1)
            for k in range(KD):
                act.wait_ge(sz_ready, n * KD + k + 1)
                act.activation(acc[:, k, n * HALF:(n + 1) * HALF], bank[:, 5 + k, :], ACT.Copy, scale=1 / (SA * SW)).then_inc(sz_out, 1)
        act.wait_ge(gT_ready, 1)
        split_hi(act, wT[0][:, :], bank[0:E, 6:8, :].rearrange("p a b -> p (a b)"), SP).then_inc(gT_hi, 1)
        act.wait_ge(gT_ready, 2)
        act.activation(mT[:, :], bank[0:E, 4:6, :].rearrange("p a b -> p (a b)"), ACT.Copy).then_inc(mT_out, 1)
        for job in range(NT2):
            e, n = divmod(job, 2)
            act.wait_ge(wb_ready, job + 1)
            act.activation(WB[:, e, n * HALF:(n + 1) * HALF], bank[:, W_BANK[job % 3], :], ACT.Copy, scale=1 / (SP * SA * SW)).then_inc(wb_out, 1)

        def weights_hi(e, parity, which):
            src = bias[:, 0, e, :] if isinstance(e, int) else bias[:, 0, bass.ds(e, 1), :].squeeze(1)
            if 0 in which:
                act.activation(b1_now[parity][:, :], src, ACT.Copy).then_inc(b1_ready, 1)
            for n in which:
                act.wait_ge(we_turned, e * 3 + (n + 1))
                split_hi(act, we[parity][0][:, n, :, :], bank[:, 4 + (3 * parity + n) % 2, :].rearrange("p (k c) -> p k c", k=KD), SW).then_inc(we_hi, 1)

        def hidden(u, e, half, parity):
            if half == 0:
                act.wait_ge(b1_ready, e + 1)
            act.wait_ge(ta_ready, u + 1)
            for k in range(KH):
                ins = act.activation(ta[half][:, k, :], ta[half][:, k, :], ACT.Silu, bias=b1_now[parity][:, k:k + 1])
            ins.then_inc(h_ready, 1)
            act.wait_ge(h_ready, u + 1)
            split_hi(act, hT[half][0][:, :, :], ta[half][:, :, :], SA).then_inc(h_hi, 1)

        weights_hi(0, 0, (0, 1, 2))
        hidden(0, 0, 0, 0)

        def body(u, e, half, parity, very_last, last):
            if not (last and parity == 1):
                weights_hi(e + 1, 1 - parity, (0, 1) if half == 0 else (2,))
            if not very_last:
                hidden(u + 1, *next_of(e, half, parity))

        units(act, body)

    @block.vector
    def _(dve):
        norm.normalize(dve, xn, x)
        turned.vector(dve)
        dve.wait_ge(gate_hi, 1)
        split_lo(dve, gate[1][:, :, :], bank[:, 4, 64:64 + KD * E].rearrange("p (k e) -> p k e", k=KD), gate[0][:, :, :], SW).then_inc(gate_lo, 1)
        for job in range(6):
            dve.wait_ge(ws_hi, job + 1)
            dst = shared_turn(job)[1]
            split_lo(dve, dst[1], bank[:, 5 + job % 3, :], dst[0], SW).then_inc(ws_lo, 1)
        logits = bank[:, 4, 0:TT * E].rearrange("p (t e) -> p t e", t=TT)
        by_token = lambda v: v.unsqueeze(2).broadcast_to([P, TT, E])
        dve.wait_ge(logits_ready, 1)
        dve.tensor_reduce(gmax[:, :], logits, X, ALU.max).then_inc(gstep, 1)
        dve.wait_ge(gstep, 1)
        dve.tensor_tensor(gs[:, :, :], logits, by_token(gmax[:, :]), ALU.subtract).then_inc(shifted, 1)
        dve.wait_ge(gexp_ready, 1)
        dve.tensor_reduce(gsum[:, :], gs[:, :, :], X, ALU.add).then_inc(gstep, 1)
        dve.wait_ge(gstep, 2)
        dve.reciprocal(gsum[:, :], gsum[:, :]).then_inc(gstep, 1)
        dve.wait_ge(gstep, 3)
        dve.tensor_tensor(gs[:, :, :], gs[:, :, :], by_token(gsum[:, :]), ALU.mult).then_inc(gstep, 1)
        dve.wait_ge(gstep, 4)
        own = gs[:, :, :].unsqueeze(3).broadcast_to([P, TT, E, E])
        other = gs[:, :, :].unsqueeze(2).broadcast_to([P, TT, E, E])
        dve.tensor_tensor(above[:, :, :, :], other, own, ALU.is_gt).then_inc(gstep, 1)
        dve.tensor_tensor(equal[:, :, :, :], other, own, ALU.is_equal).then_inc(gstep, 1)
        for n in range(2):
            for j in range(KS):
                at = n * KS + j
                dve.wait_ge(su_ready, at + 1)
                dve.wait_ge(sg_out, at + 1)
                dve.scalar_tensor_tensor(out=sg[:, j, :], in0=bank[:, 2 + at % 2, :], scalar=1 / (SA * SW), in1=sg[:, j, :],
                                         op0=ALU.mult, op1=ALU.mult).then_inc(su_out, 1)
                dve.wait_ge(sh_hi, at + 1)
                split_lo(dve, sh[1][:, j, :], sg[:, j, :], sh[0][:, j, :], SA).then_inc(sh_lo, 1)
            if n == 0:
                dve.wait_ge(rank_step, 2)
                dve.tensor_reduce(rank[:, :, :], above[:, :, :, :], X, ALU.add).then_inc(gstep, 1)
                dve.wait_ge(gstep, 7)
                dve.tensor_scalar(mask[:, :, :], rank[:, :, :], 1.5, None, ALU.is_lt).then_inc(gstep, 1)
                dve.wait_ge(gstep, 8)
                dve.tensor_tensor(gs[:, :, :], gs[:, :, :], mask[:, :, :], ALU.mult).then_inc(gates_ready, 1)
        dve.wait_ge(gT_hi, 1)
        split_lo(dve, wT[1][:, :], bank[0:E, 6:8, :].rearrange("p a b -> p (a b)"), wT[0][:, :], SP).then_inc(gT_lo, 1)
        for job in range(NT2):
            e, n = divmod(job, 2)
            dve.wait_ge(mb_ready, job + 1)
            dve.tensor_scalar(MB[:, e, n * HALF:(n + 1) * HALF], bank[:, M_BANK[job % 3], :], 1 / (SA * SW), None, ALU.mult).then_inc(mb_out, 1)

        def weights_lo(e, parity, which):
            for n in which:
                dve.wait_ge(we_hi, e * 3 + (n + 1))
                split_lo(dve, we[parity][1][:, n, :, :], bank[:, 4 + (3 * parity + n) % 2, :].rearrange("p (k c) -> p k c", k=KD),
                         we[parity][0][:, n, :, :], SW).then_inc(we_lo, 1)

        def at_tokens(tile, e, half):
            t = tile[:, e, half * HALF:(half + 1) * HALF].unsqueeze(1) if isinstance(e, int) else \
                tile[:, bass.ds(e, 1), half * HALF:(half + 1) * HALF]
            return t.broadcast_to([P, KH, HALF])

        def column(n, e, k):
            return bias[:, n, e, k:k + 1] if isinstance(e, int) else bias[:, n, bass.ds(e, 1), k]

        def weigh(u, e, half, first):
            dve.wait_ge(a_ready, u + 1)
            dve.tensor_tensor(ta[half][:, :, :], bank[:, 0:2, :], at_tokens(WB, e, half), ALU.mult).then_inc(ta_ready, 1)
            dve.wait_ge(b_ready, u + 1)
            if not first:
                dve.wait_ge(acc_ready, u)
            dve.tensor_tensor(tb[half][:, :, :], bank[:, 2:4, :], at_tokens(WB, e, half), ALU.mult).then_inc(tb_ready, 1)
            dve.wait_ge(tb_ready, u + 1)
            for k in range(KH):
                m_at = MB[:, e, half * HALF:(half + 1) * HALF] if isinstance(e, int) else \
                    MB[:, bass.ds(e, 1), half * HALF:(half + 1) * HALF].squeeze(1)
                ins = dve.scalar_tensor_tensor(out=tb[half][:, k, :], in0=tb[half][:, k, :], scalar=column(2, e, k), in1=m_at,
                                               op0=ALU.add, op1=ALU.mult)
            ins.then_inc(x3_ready, 1)
            dve.wait_ge(h_hi, u + 1)
            split_lo(dve, hT[half][1][:, :, :], ta[half][:, :, :], hT[half][0][:, :, :], SA).then_inc(h_lo, 1)

        dve.sem_inc(yt_ready, 1)
        dve.sem_inc(acc_ready, 1)
        weights_lo(0, 0, (0, 1, 2))
        weigh(0, 0, 0, True)

        def body(u, e, half, parity, very_last, last):
            if not (last and parity == 1):
                weights_lo(e + 1, 1 - parity, (0, 1) if half == 0 else (2,))
            if not very_last:
                ne, nhalf, _ = next_of(e, half, parity)
                weigh(u + 1, ne, nhalf, False)
            dve.wait_ge(y_ready, u + 1)
            dve.wait_ge(x3_ready, u + 1)
            for k in range(KD):
                ins = dve.scalar_tensor_tensor(out=tb[half][:, k, :], in0=bank[:, 6 + k, :], scalar=column(1, e, k),
                                               in1=tb[half][:, k, :], op0=ALU.add, op1=ALU.mult)
            ins.then_inc(yt_ready, 1)

        units(dve, body)
        for t in range(TT):
            dve.wait_ge(fin_ready, t + 1)
            dve.tensor_tensor(xn[:, t, :], bank[:, t, 0:D], x[:, t, :], ALU.add).then_inc(fin_added, 1)


INPUTS = {"x": "x", "ctx": "ctx_1024", "Wq": "L0_xattn_Wq", "Wk": "L0_xattn_Wk", "Wv": "L0_xattn_Wv",
          "Wk_ip": "L0_xattn_Wk_ip", "Wv_ip": "L0_xattn_Wv_ip", "Wk_ap": "L0_xattn_Wk_ap", "Wv_ap": "L0_xattn_Wv_ap",
          "Wo": "L0_xattn_Wo", "bo": "L0_xattn_bo", "rel_k": "L0_xattn_rel_k", "rel_v": "L0_xattn_rel_v",
          "alpha": "L0_xattn_alpha", "beta": "L0_xattn_beta", "w_attn": "L0_attn_w_attn", "b_attn": "L0_attn_b_attn",
          "w_proj": "L0_attn_w_proj", "b_proj": "L0_attn_b_proj", "gate_w": "L0_ffn_gate_w", "w1": "L0_ffn_w1",
          "b1": "L0_ffn_b1", "w2": "L0_ffn_w2", "b2": "L0_ffn_b2", "w3": "L0_ffn_w3", "b3": "L0_ffn_b3",
          "sw1": "L0_ffn_sw1", "sw2": "L0_ffn_sw2", "sw3": "L0_ffn_sw3"}


def perceiver_layer(nc, a, out):
    scr = {
        "kt": nc.dram_tensor("kt_scratch", [B, P, 2 * PAIRS * TI], F16).ap(),
        "v": nc.dram_tensor("v_scratch", [B * TI, 2 * INNER], F16).ap(),
        "R": nc.dram_tensor("rel_scratch", [B, TXT, 2, PAIRS * NQ], F32).ap(),
        "relv": nc.dram_tensor("relv_scratch", [EXT, HD], F32).ap(),
        "pt": nc.dram_tensor("prob_scratch", [B, TXT, 2, PAIRS * 2 * NQ], F16).ap(),
    }
    with ExitStack() as whole:
        m = Mem(nc, whole)
        ident = m.sb("ident", [P, P])
        x = m.sb("x_res", [P, TT, D])
        norm_c = Norm(m, "norm_c")
        used = []

        def phase(f, *args):
            with ExitStack() as ctx:
                own = Mem(nc, ctx)
                f(nc, own, *args)
                used.extend(own.sems)

        with ExitStack() as attending:
            keep = Mem(nc, attending)
            qT = [keep.sb(f"qT_{s}", [P, PAIRS, T], F16) for s in "hl"]
            rel_k = ExtendedRows(keep, "relk", a["rel_k"], 2)
            rel_v = ExtendedRows(keep, "relv", a["rel_v"], 1)
            phase(project, a, scr, x, qT, rel_k, rel_v, ident)
            OT = keep.sb("OT", [P, PAIRS, T])
            with ExitStack() as streaming:
                s = Mem(nc, streaming)
                audio, context = AudioWeights(s), AudioContext(s, a["ctx"])
                phase(relative_scores, a, scr, qT, OT, rel_k, rel_v, audio, context.load_first, ident)
                phase(cross_attention, scr, qT, OT, audio, context, ident)
            out_weights = OutputWeights(keep)
            phase(relative_values, a, scr, OT, x, out_weights)
            norm_b, self_weights = Norm(keep, "norm_b"), SelfWeights(keep)
            phase(cross_output, a, OT, x, out_weights, self_weights, norm_b)
            phase(self_attention, a, x, self_weights, norm_b, norm_c, ident, used)
        phase(experts, a, x, norm_c, out, ident)


def kernel(**inputs):
    import concourse.bacc as bacc
    from concourse.bass_utils import run_bass_kernel_spmd

    nc = bacc.Bacc("TRN2", target_bir_lowering=False, num_devices=1)
    arrays, a = {}, {}
    for name, key in INPUTS.items():
        v = np.ascontiguousarray(inputs[key])
        v = v.reshape(1) if v.ndim == 0 else v
        arrays["in_" + name] = v
        a[name] = nc.dram_tensor("in_" + name, v.shape, mybir.dt.from_np(v.dtype), kind="ExternalInput").ap()
    out = nc.dram_tensor("out_x", [B, NQ, D], F32, kind="ExternalOutput").ap()
    perceiver_layer(nc, a, out)
    r = run_bass_kernel_spmd(nc, [arrays], core_ids=[0])
    return r.results[0]["out_x"]
```
